# Optimizing a Trainium2 kernel written in Bass

```python
import numpy as np
import jax
import jax.numpy as jnp

def _softmax(x, axis=-1):
    return jax.nn.softmax(x, axis=axis)

def _gelu(x):
    return jax.nn.gelu(x, approximate=True)

def _silu(x):
    return jax.nn.silu(x)

def _sigmoid(x):
    return jax.nn.sigmoid(x)

def _layernorm(x, axis=-1, eps=1e-05):
    m = jnp.mean(x, axis=axis, keepdims=True)
    v = jnp.var(x, axis=axis, keepdims=True)
    return (x - m) / jnp.sqrt(v + eps)

def _scatter_add(tgt, idx, src, axis=0):
    return tgt.at[idx].add(src)

def _segment_sum(src, seg, n):
    return jax.ops.segment_sum(src, seg, n)
kernel_name = 'mk_seq_postln_d2_jaxref_r8_f2ff04'

def setup_inputs(seed: int=0):
    np.random.seed(seed)
    _w = jnp.asarray

    def _L0_attn_setup():
        import jax, jax.numpy as jnp
        import numpy as np
        H = 8
        LN_EPS = 1e-05
        key = jax.random.key(seed)
        ks = jax.random.split(key, 4)
        B, S, D = (4, 256, 128)
        x = jax.random.normal(ks[0], (B, S, D), dtype=jnp.float32)
        sc = 1.0 / np.sqrt(D)
        Wq = jax.random.normal(ks[1], (D, D), dtype=jnp.float32) * sc
        Wk = jax.random.normal(ks[2], (D, D), dtype=jnp.float32) * sc
        Wv = jax.random.normal(ks[3], (D, D * H), dtype=jnp.float32) * sc
        return {'x': x, 'Wq': Wq, 'bq': jnp.zeros((D,), jnp.float32), 'Wk': Wk, 'bk': jnp.zeros((D,), jnp.float32), 'Wv': Wv, 'bv': jnp.zeros((D * H,), jnp.float32), 'gamma': jnp.ones((D,), jnp.float32), 'beta': jnp.zeros((D,), jnp.float32)}
    _L0_attn_in = _L0_attn_setup()

    def _L0_ffn_setup():
        import jax, jax.numpy as jnp
        import numpy as np
        D_IN, D_HID = (128, 512)

        def _ternary(key, shape):
            return jax.random.randint(key, shape, -1, 2).astype(jnp.float32)

        def _tlin(x, w, s):
            return jnp.einsum('bsi,oi->bso', x, w) * s
        key = jax.random.key(seed)
        ks = jax.random.split(key, 12)
        inv = lambda fan: 1.0 / np.sqrt(fan).astype(np.float32)
        return {'x': jax.random.normal(ks[0], (4, 256, D_IN), dtype=jnp.float32), 'w1_w': _ternary(ks[1], (D_HID, D_IN)), 'w1_s': jax.random.uniform(ks[2], (D_HID,), dtype=jnp.float32) * inv(D_IN), 'w2_w': _ternary(ks[3], (D_HID, D_IN)), 'w2_s': jax.random.uniform(ks[4], (D_HID,), dtype=jnp.float32) * inv(D_IN), 'h1_w': _ternary(ks[5], (D_HID, D_HID)), 'h1_s': jax.random.uniform(ks[6], (D_HID,), dtype=jnp.float32) * inv(D_HID), 'h2_w': _ternary(ks[7], (D_HID, D_HID)), 'h2_s': jax.random.uniform(ks[8], (D_HID,), dtype=jnp.float32) * inv(D_HID), 'w3_w': _ternary(ks[9], (D_IN, D_HID)), 'w3_s': jax.random.uniform(ks[10], (D_IN,), dtype=jnp.float32) * inv(D_HID)}
    _L0_ffn_in = _L0_ffn_setup()

    def _L1_attn_setup():
        import jax, jax.numpy as jnp
        import numpy as np
        B, L, D = (2, 512, 128)
        H, DK, DV = (4, 32, 32)
        CONV_K, FIR_S, FIR_L = (4, 3, 31)
        CHUNK = 32
        EPS = 1e-05

        def l2norm(x):
            return x * jax.lax.rsqrt(jnp.sum(x * x, -1, keepdims=True) + 1e-06)

        def causal_dwconv(x, w):
            C, K = w.shape
            y = jax.lax.conv_general_dilated(jnp.swapaxes(x, 1, 2), w[:, None, :], (1,), [(K - 1, 0)], feature_group_count=C, dimension_numbers=('NCH', 'OIH', 'NCH'))
            return jnp.swapaxes(y, 1, 2)

        def delta_rule_chunkwise(q, k, v, beta, chunk=CHUNK):
            b, h, Lx, dk = q.shape
            dv = v.shape[-1]
            pad = -Lx % chunk
            if pad:
                q, k, v = (jnp.pad(t, ((0, 0), (0, 0), (0, pad), (0, 0))) for t in (q, k, v))
                beta = jnp.pad(beta, ((0, 0), (0, 0), (0, pad)))
            Lp = Lx + pad
            n = Lp // chunk
            q = l2norm(q)
            k = l2norm(k)
            v = v * beta[..., None]
            k_beta = k * beta[..., None]
            ch = lambda t: t.reshape(b, h, n, chunk, -1)
            qc, kc, vc, kbc = map(ch, (q, k, v, k_beta))
            A = jnp.einsum('bhncd,bhned->bhnce', kbc, kc)
            eye = jnp.eye(chunk, dtype=q.dtype)
            T = jnp.linalg.inv(eye + jnp.tril(A, -1))
            u = T @ vc
            w = T @ kbc
            tri = jnp.tril(jnp.ones((chunk, chunk), bool))

            def body(S, inp):
                q_i, k_i, u_i, w_i = inp
                attn = jnp.where(tri, jnp.einsum('bhcd,bhed->bhce', q_i, k_i), 0.0)
                u_i = u_i - w_i @ S
                o_i = q_i @ S + attn @ u_i
                S = S + jnp.einsum('bhcd,bhce->bhde', k_i, u_i)
                return (S, o_i)
            mv = lambda t: jnp.moveaxis(t, 2, 0)
            S0 = jnp.zeros((b, h, dk, dv), q.dtype)
            S, o = jax.lax.scan(body, S0, (mv(qc), mv(kc), mv(u), mv(w)))
            o = jnp.moveaxis(o, 0, 2).reshape(b, h, Lp, dv)[:, :, :Lx]
            return (o, S)
        key = jax.random.key(seed)
        ks = jax.random.split(key, 16)
        s = 0.02
        fir_short = jnp.zeros((H, DV, FIR_S)).at[..., -1].set(1.0) + 0.001 * jax.random.normal(ks[8], (H, DV, FIR_S))
        fir_long = jnp.zeros((H, DV, FIR_L)).at[..., -1].set(1.0) + 0.001 * jax.random.normal(ks[9], (H, DV, FIR_L))
        bl = jnp.zeros((H, 3)).at[:, 0].set(2.0).reshape(-1)
        return dict(hidden_states=jax.random.normal(ks[0], (B, L, D), jnp.float32), Wq=s * jax.random.normal(ks[1], (D, H * DK)), Wk=s * jax.random.normal(ks[2], (D, H * DK)), Wv=s * jax.random.normal(ks[3], (D, H * DV)), conv_q=0.3 * jax.random.normal(ks[4], (H * DK, CONV_K)), conv_k=0.3 * jax.random.normal(ks[5], (H * DK, CONV_K)), conv_v=0.3 * jax.random.normal(ks[6], (H * DV, CONV_K)), Wb=s * jax.random.normal(ks[7], (D, H)), fir_short=fir_short, fir_long=fir_long, Wg=s * jax.random.normal(ks[10], (D, H)), bg=0.5 * jnp.ones((H,)), Wl=s * jax.random.normal(ks[11], (D, H * 3)), bl=bl, log_temp=jnp.ones((H,)), rms_w=jnp.ones((DV,)), Wo=s * jax.random.normal(ks[12], (H * DV, D)))
    _L1_attn_in = _L1_attn_setup()

    def _L1_ffn_setup():
        import jax, jax.numpy as jnp
        import numpy as np
        import math
        D_IN = 128
        FEATURES = (512, 512, 128)
        BATCH, SEQ = (8, 256)

        def _conn_dense(kernel_bool, x):
            w = jnp.where(kernel_bool, jnp.float32(1.0), jnp.float32(-1.0))
            return x @ w
        key = jax.random.key(seed)
        kx, kk0, kk1, kk2 = jax.random.split(key, 4)
        x = jax.random.normal(kx, (BATCH, SEQ, D_IN), dtype=jnp.float32)
        k0 = jax.random.randint(kk0, (2 * D_IN, FEATURES[0]), 0, 2).astype(jnp.bool_)
        k1 = jax.random.randint(kk1, (FEATURES[0], FEATURES[1]), 0, 2).astype(jnp.bool_)
        k2 = jax.random.randint(kk2, (FEATURES[1], FEATURES[2]), 0, 2).astype(jnp.bool_)
        s0 = jnp.asarray(1.0 / math.sqrt(2 * D_IN), dtype=jnp.float32)
        s1 = jnp.asarray(1.0 / math.sqrt(FEATURES[0]), dtype=jnp.float32)
        s2 = jnp.asarray(1.0 / math.sqrt(FEATURES[1]), dtype=jnp.float32)
        return {'x': x, 'k0': k0, 'k1': k1, 'k2': k2, 's0': s0, 's1': s1, 's2': s2}
    _L1_ffn_in = _L1_ffn_setup()
    _d = {'L0_attn_x': _L0_attn_in['x'], 'L0_attn_Wq': _L0_attn_in['Wq'], 'L0_attn_bq': _L0_attn_in['bq'], 'L0_attn_Wk': _L0_attn_in['Wk'], 'L0_attn_bk': _L0_attn_in['bk'], 'L0_attn_Wv': _L0_attn_in['Wv'], 'L0_attn_bv': _L0_attn_in['bv'], 'L0_attn_gamma': _L0_attn_in['gamma'], 'L0_attn_beta': _L0_attn_in['beta'], 'L0_ffn_w1_w': _L0_ffn_in['w1_w'], 'L0_ffn_w1_s': _L0_ffn_in['w1_s'], 'L0_ffn_w2_w': _L0_ffn_in['w2_w'], 'L0_ffn_w2_s': _L0_ffn_in['w2_s'], 'L0_ffn_h1_w': _L0_ffn_in['h1_w'], 'L0_ffn_h1_s': _L0_ffn_in['h1_s'], 'L0_ffn_h2_w': _L0_ffn_in['h2_w'], 'L0_ffn_h2_s': _L0_ffn_in['h2_s'], 'L0_ffn_w3_w': _L0_ffn_in['w3_w'], 'L0_ffn_w3_s': _L0_ffn_in['w3_s'], 'L1_attn_Wq': _L1_attn_in['Wq'], 'L1_attn_Wk': _L1_attn_in['Wk'], 'L1_attn_Wv': _L1_attn_in['Wv'], 'L1_attn_conv_q': _L1_attn_in['conv_q'], 'L1_attn_conv_k': _L1_attn_in['conv_k'], 'L1_attn_conv_v': _L1_attn_in['conv_v'], 'L1_attn_Wb': _L1_attn_in['Wb'], 'L1_attn_fir_short': _L1_attn_in['fir_short'], 'L1_attn_fir_long': _L1_attn_in['fir_long'], 'L1_attn_Wg': _L1_attn_in['Wg'], 'L1_attn_bg': _L1_attn_in['bg'], 'L1_attn_Wl': _L1_attn_in['Wl'], 'L1_attn_bl': _L1_attn_in['bl'], 'L1_attn_log_temp': _L1_attn_in['log_temp'], 'L1_attn_rms_w': _L1_attn_in['rms_w'], 'L1_attn_Wo': _L1_attn_in['Wo'], 'L1_ffn_k0': _L1_ffn_in['k0'], 'L1_ffn_k1': _L1_ffn_in['k1'], 'L1_ffn_k2': _L1_ffn_in['k2'], 'L1_ffn_s0': _L1_ffn_in['s0'], 'L1_ffn_s1': _L1_ffn_in['s1'], 'L1_ffn_s2': _L1_ffn_in['s2']}
    _x0 = _d['L0_attn_x']
    _d['L0_attn_x'] = jax.random.normal(jax.random.fold_in(jax.random.key(seed), 1), (2, 1024, 128), dtype=_x0.dtype)
    del _x0
    return _d

def reference(L0_attn_x, L0_attn_Wq, L0_attn_bq, L0_attn_Wk, L0_attn_bk, L0_attn_Wv, L0_attn_bv, L0_attn_gamma, L0_attn_beta, L0_ffn_w1_w, L0_ffn_w1_s, L0_ffn_w2_w, L0_ffn_w2_s, L0_ffn_h1_w, L0_ffn_h1_s, L0_ffn_h2_w, L0_ffn_h2_s, L0_ffn_w3_w, L0_ffn_w3_s, L1_attn_Wq, L1_attn_Wk, L1_attn_Wv, L1_attn_conv_q, L1_attn_conv_k, L1_attn_conv_v, L1_attn_Wb, L1_attn_fir_short, L1_attn_fir_long, L1_attn_Wg, L1_attn_bg, L1_attn_Wl, L1_attn_bl, L1_attn_log_temp, L1_attn_rms_w, L1_attn_Wo, L1_ffn_k0, L1_ffn_k1, L1_ffn_k2, L1_ffn_s0, L1_ffn_s1, L1_ffn_s2):

    def _L0_attn_ref(x, Wq, bq, Wk, bk, Wv, bv, gamma, beta):
        import jax, jax.numpy as jnp
        import numpy as np
        H = 8
        LN_EPS = 1e-05
        B, S, D = x.shape
        dk = D // H
        mu = jnp.mean(x, axis=-1, keepdims=True)
        var = jnp.mean(jnp.square(x - mu), axis=-1, keepdims=True)
        xn = (x - mu) * jax.lax.rsqrt(var + LN_EPS) * gamma + beta
        q = (xn @ Wq + bq).reshape(B, S, H, dk).transpose(0, 2, 1, 3)
        k = (xn @ Wk + bk).reshape(B, S, H, dk).transpose(0, 2, 1, 3)
        v = (xn @ Wv + bv).reshape(B, S, H, D).transpose(0, 2, 1, 3)
        scores = jnp.einsum('bhsd,bhtd->bhst', q, k) / jnp.sqrt(jnp.asarray(dk, x.dtype))
        p = jax.nn.softmax(scores, axis=-1)
        att = jnp.einsum('bhst,bhtd->bhsd', p, v)
        out = att.reshape(S, B, D, H).sum(axis=-1).reshape(B, S, D)
        return out

    def _L0_ffn_ref(x, w1_w, w1_s, w2_w, w2_s, h1_w, h1_s, h2_w, h2_s, w3_w, w3_s):
        import jax, jax.numpy as jnp
        import numpy as np
        D_IN, D_HID = (128, 512)

        def _ternary(key, shape):
            return jax.random.randint(key, shape, -1, 2).astype(jnp.float32)

        def _tlin(x, w, s):
            return jnp.einsum('bsi,oi->bso', x, w) * s
        h = jax.nn.silu(_tlin(x, w1_w, w1_s)) * _tlin(x, w2_w, w2_s)
        h = jax.nn.gelu(_tlin(h, h1_w, h1_s), approximate=False)
        h = jax.nn.gelu(_tlin(h, h2_w, h2_s), approximate=False)
        return _tlin(h, w3_w, w3_s)

    def _L1_attn_ref(hidden_states, Wq, Wk, Wv, conv_q, conv_k, conv_v, Wb, fir_short, fir_long, Wg, bg, Wl, bl, log_temp, rms_w, Wo):
        import jax, jax.numpy as jnp
        import numpy as np
        B, L, D = (2, 512, 128)
        H, DK, DV = (4, 32, 32)
        CONV_K, FIR_S, FIR_L = (4, 3, 31)
        CHUNK = 32
        EPS = 1e-05

        def l2norm(x):
            return x * jax.lax.rsqrt(jnp.sum(x * x, -1, keepdims=True) + 1e-06)

        def causal_dwconv(x, w):
            C, K = w.shape
            y = jax.lax.conv_general_dilated(jnp.swapaxes(x, 1, 2), w[:, None, :], (1,), [(K - 1, 0)], feature_group_count=C, dimension_numbers=('NCH', 'OIH', 'NCH'))
            return jnp.swapaxes(y, 1, 2)

        def delta_rule_chunkwise(q, k, v, beta, chunk=CHUNK):
            b, h, Lx, dk = q.shape
            dv = v.shape[-1]
            pad = -Lx % chunk
            if pad:
                q, k, v = (jnp.pad(t, ((0, 0), (0, 0), (0, pad), (0, 0))) for t in (q, k, v))
                beta = jnp.pad(beta, ((0, 0), (0, 0), (0, pad)))
            Lp = Lx + pad
            n = Lp // chunk
            q = l2norm(q)
            k = l2norm(k)
            v = v * beta[..., None]
            k_beta = k * beta[..., None]
            ch = lambda t: t.reshape(b, h, n, chunk, -1)
            qc, kc, vc, kbc = map(ch, (q, k, v, k_beta))
            A = jnp.einsum('bhncd,bhned->bhnce', kbc, kc)
            eye = jnp.eye(chunk, dtype=q.dtype)
            T = jnp.linalg.inv(eye + jnp.tril(A, -1))
            u = T @ vc
            w = T @ kbc
            tri = jnp.tril(jnp.ones((chunk, chunk), bool))

            def body(S, inp):
                q_i, k_i, u_i, w_i = inp
                attn = jnp.where(tri, jnp.einsum('bhcd,bhed->bhce', q_i, k_i), 0.0)
                u_i = u_i - w_i @ S
                o_i = q_i @ S + attn @ u_i
                S = S + jnp.einsum('bhcd,bhce->bhde', k_i, u_i)
                return (S, o_i)
            mv = lambda t: jnp.moveaxis(t, 2, 0)
            S0 = jnp.zeros((b, h, dk, dv), q.dtype)
            S, o = jax.lax.scan(body, S0, (mv(qc), mv(kc), mv(u), mv(w)))
            o = jnp.moveaxis(o, 0, 2).reshape(b, h, Lp, dv)[:, :, :Lx]
            return (o, S)
        x = hidden_states
        Bx, Lx, _ = x.shape
        q = jax.nn.silu(causal_dwconv(x @ Wq, conv_q)).reshape(Bx, Lx, H, DK)
        k = jax.nn.silu(causal_dwconv(x @ Wk, conv_k)).reshape(Bx, Lx, H, DK)
        v = jax.nn.silu(causal_dwconv(x @ Wv, conv_v)).reshape(Bx, Lx, H, DV)
        beta = jax.nn.sigmoid(x @ Wb)
        o_d, S = delta_rule_chunkwise(q.transpose(0, 2, 1, 3), k.transpose(0, 2, 1, 3), v.transpose(0, 2, 1, 3), beta.transpose(0, 2, 1))
        delta_out = o_d.transpose(0, 2, 1, 3)
        vf = v.reshape(Bx, Lx, H * DV)
        local_short = causal_dwconv(vf, fir_short.reshape(H * DV, FIR_S)).reshape(Bx, Lx, H, DV)
        local_long = causal_dwconv(vf, fir_long.reshape(H * DV, FIR_L)).reshape(Bx, Lx, H, DV)
        w_global = jax.nn.sigmoid(x @ Wg + bg)
        temp = jnp.exp(log_temp)
        logits = (x @ Wl + bl).reshape(Bx, Lx, H, 3) / temp[:, None]
        p = jax.nn.softmax(logits, axis=-1)
        local_mix = p[..., 0:1] * v + p[..., 1:2] * local_short + p[..., 2:3] * local_long
        o = w_global[..., None] * delta_out + (1.0 - w_global)[..., None] * local_mix
        o = o * jax.lax.rsqrt(jnp.mean(o * o, -1, keepdims=True) + EPS) * rms_w
        return o.reshape(Bx, Lx, H * DV) @ Wo

    def _L1_ffn_ref(x, k0, k1, k2, s0, s1, s2):
        import jax, jax.numpy as jnp
        import numpy as np
        import math
        D_IN = 128
        FEATURES = (512, 512, 128)
        BATCH, SEQ = (8, 256)

        def _conn_dense(kernel_bool, x):
            w = jnp.where(kernel_bool, jnp.float32(1.0), jnp.float32(-1.0))
            return x @ w
        h = jnp.concatenate([x, -x], axis=-1)
        h = s0 * _conn_dense(k0, h)
        h = jax.nn.relu(h) * 2
        h = s1 * _conn_dense(k1, h)
        h = jax.nn.relu(h) * 2
        h = s2 * _conn_dense(k2, h)
        return h
    x = L0_attn_x
    x = _layernorm(x + _L0_attn_ref(x, L0_attn_Wq, L0_attn_bq, L0_attn_Wk, L0_attn_bk, L0_attn_Wv, L0_attn_bv, L0_attn_gamma, L0_attn_beta), axis=-1)
    x = _layernorm(x + _L0_ffn_ref(x, L0_ffn_w1_w, L0_ffn_w1_s, L0_ffn_w2_w, L0_ffn_w2_s, L0_ffn_h1_w, L0_ffn_h1_s, L0_ffn_h2_w, L0_ffn_h2_s, L0_ffn_w3_w, L0_ffn_w3_s), axis=-1)
    x = _layernorm(x + _L1_attn_ref(x, L1_attn_Wq, L1_attn_Wk, L1_attn_Wv, L1_attn_conv_q, L1_attn_conv_k, L1_attn_conv_v, L1_attn_Wb, L1_attn_fir_short, L1_attn_fir_long, L1_attn_Wg, L1_attn_bg, L1_attn_Wl, L1_attn_bl, L1_attn_log_temp, L1_attn_rms_w, L1_attn_Wo), axis=-1)
    x = _layernorm(x + _L1_ffn_ref(x, L1_ffn_k0, L1_ffn_k1, L1_ffn_k2, L1_ffn_s0, L1_ffn_s1, L1_ffn_s2), axis=-1)
    return x

_drawn_inputs = setup_inputs


def setup_inputs(seed=0):
    import zlib

    import numpy as np

    out = dict(_drawn_inputs(seed))
    spreads = {'L0_attn_bq': (0.0, 0.1),
     'L0_attn_bk': (0.0, 2.0),
     'L0_attn_bv': (0.0, 0.1),
     'L0_attn_gamma': (1.0, 0.2),
     'L0_attn_beta': (0.0, 0.1),
     'L1_attn_bg': (0.5, 0.6),
     'L1_attn_log_temp': (1.0, 0.6),
     'L1_attn_rms_w': (1.0, 0.2)}
    factors = {'L0_ffn_w1_w': 8.0,
     'L0_ffn_w1_s': 8.0,
     'L0_ffn_w2_w': 8.0,
     'L0_ffn_w2_s': 8.0,
     'L0_ffn_h1_w': 8.0,
     'L0_ffn_h1_s': 8.0,
     'L0_ffn_h2_w': 8.0,
     'L0_ffn_h2_s': 8.0,
     'L0_ffn_w3_w': 8.0,
     'L0_ffn_w3_s': 8.0,
     'L1_attn_Wb': 3.193,
     'L1_attn_fir_short': 64.0,
     'L1_attn_Wl': 64.0,
     'L1_attn_bl': 64.0,
     'L1_attn_fir_long': 8.0}
    for name, (base, spread) in spreads.items():
        noise = np.random.default_rng([zlib.crc32(name.encode()), seed]).standard_normal(out[name].shape)
        drawn = base * np.exp(spread * noise) if base else spread * noise
        out[name] = jnp.asarray(drawn.astype(out[name].dtype))
    for name, factor in factors.items():
        out[name] = (out[name] * factor).astype(out[name].dtype)
    return out
```

```python
import concourse.bass as bass
from concourse import mybir
from contextlib import ExitStack

F32, F32R, BF16, U8 = mybir.dt.float32, mybir.dt.float32r, mybir.dt.bfloat16, mybir.dt.uint8
ALU = mybir.AluOpType
ACT = mybir.ActivationFunctionType
AX = mybir.AxisListType

P = 128
D = 128
B, S = 2, 1024
NT = B * S // P
GT = 512
GROUPS = B * S // GT
H0 = 8
NH = B * H0
DK0 = D // H0
SCORE_SCALE = float(DK0) ** -0.5
FH = 512
FB = FH // P
LN_EPS = 1e-5
C = 32
CONV, FIRS, FIRL = 4, 3, 31


class Chain:

    def __init__(self, engine, semaphore, base=0):
        self.engine, self.semaphore, self.base, self.n = engine, semaphore, base, 0

    def __call__(self, instruction):
        self.n += 1
        instruction.then_inc(self.semaphore, 1)
        self.engine.wait_ge(self.semaphore, self.base + self.n)


def split3(engine, link, parts, src, rest, done):
    link(engine.tensor_copy(parts[:, 0], src[:]))
    link(engine.tensor_tensor(rest[:, 0], src[:], parts[:, 0], ALU.subtract))
    link(engine.tensor_copy(parts[:, 1], rest[:, 0]))
    link(engine.tensor_tensor(rest[:, 1], rest[:, 0], parts[:, 1], ALU.subtract))
    engine.tensor_copy(parts[:, 2], rest[:, 1]).then_inc(done, 1)


def build(nc, dr, out_dram):
    x_dram = dr["L0_attn_x"]
    q_scratch = nc.dram_tensor("q_scratch", (3, B, P, S), BF16, kind="Internal").ap()
    k_scratch = nc.dram_tensor("k_scratch", (3, B, P, S), BF16, kind="Internal").ap()

    with ExitStack() as ctx:
        program(nc, dr, out_dram, x_dram, q_scratch, k_scratch, ctx)


def program(nc, dr, out_dram, x_dram, q_scratch, k_scratch, ctx):
    def sb(name, shape, dt=F32):
        return ctx.enter_context(nc.sbuf_tensor(name, shape, dt))

    early = ExitStack()
    early_sems = []

    def sem(name):
        early_sems.append(early.enter_context(nc.semaphore(name)))
        return early_sems[-1]

    ps = ctx.enter_context(nc.psum_tensor("ps", [P, 8, 512], F32))
    X = sb("X", [P, NT, D])
    ident, ident_bf = sb("ident", [P, P]), sb("ident_bf", [P, P], BF16)
    neg_half = sb("neg_half", [P, 16])
    st6, mv, rs = sb("st6", [P, GROUPS, 4, 6]), sb("mv", [P, GROUPS, 4, 2]), sb("rs", [P, GROUPS, 4])
    xn = sb("xn", [P, 2, 4, P])
    eps_l2, eps_rms = sb("eps_l2", [P, 1]), sb("eps_rms", [P, 1])
    sub = ExitStack()
    sb_all = sb

    def sb(name, shape, dt=F32):
        return sub.enter_context(nc.sbuf_tensor(name, shape, dt))

    wq, wk, wv = sb("wq", [P, P]), sb("wk", [P, P]), sb("wv", [P, H0 * D])
    bq, bk, gam, bet = sb("bq", [P, 1]), sb("bk", [P, 1]), sb("gam", [P, 1]), sb("bet", [P, 1])
    bv_rows, wv_sum, bv_sum = sb("bv_rows", [P, H0 * D]), sb("wv_sum", [P, P]), sb("bv_sum", [P, P])
    xnT = sb("xnT", [P, 2, GT])
    qf, kf = sb("qf", [P, GT]), sb("kf", [P, GT])
    q_rest, k_rest = sb("q_rest", [P, 2, GT]), sb("k_rest", [P, 2, GT])
    qsplit, ksplit = sb("qsplit", [P, 2, 3, GT], BF16), sb("ksplit", [P, 2, 3, GT], BF16)
    vp = sb("vp", [P, NH, 8, 32])
    fold_sel = sb("fold_sel", [P, 32])
    qst, kst = sb("qst", [P, 2, S], BF16), sb("kst", [P, 2, S], BF16)
    qm, km = sb("qm", [P, 2, S], BF16), sb("km", [P, 2, S], BF16)
    mx, nmax = sb("mx", [P, 2, 8]), sb("nmax", [P, 2, 8])
    shift3, shift_sb = sb("shift3", [P, 2, 24], BF16), sb("shift_sb", [P, 2, P], BF16)
    prob = sb("prob", [P, 16, 512])
    vst = sb("vst", [P, 2, 8, 32])
    ot = sb("ot", [P, 2, 512])
    ot_by_m = ot[:].rearrange("p c t -> p (c t)").rearrange("p (r m) -> p m r", m=8)
    zeros8 = sb("zeros8", [P, 8])
    rsum, att = sb("rsum", [P, 8]), sb("att", [P, P])
    q_scr_h = q_scratch.rearrange("a b (h k) t -> a (b h) k t", k=DK0)
    k_scr_h = k_scratch.rearrange("a b (h k) t -> a (b h) k t", k=DK0)
    with nc.Block() as block:
        x_in = [sem(f"x_in{g}") for g in range(GROUPS)]
        weights_in = sem("weights_in")
        ident_ready = sem("ident_ready")
        stats_ready = sem("stats_ready")
        rstd_ready = sem("rstd_ready")
        xn_ready = sem("xn_ready")
        xnT_psum = sem("xnT_psum")
        xnT_ready = sem("xnT_ready")
        wv_summed = sem("wv_summed")
        q_psum, k_psum, v_psum = sem("q_psum"), sem("k_psum"), sem("v_psum")
        q_ready, k_ready, v_ready = sem("q_ready"), sem("k_ready"), sem("v_ready")
        q_split, k_split = sem("q_split"), sem("k_split")
        splits_stored = [sem(f"splits_stored{g}") for g in range(GROUPS)]
        dve_step, pool_step = sem("dve_step1"), sem("pool_step1")

        @block.sync
        def _(sp):
            xg = x_dram.rearrange("(n p) d -> p n d", p=P)
            for g in range(GROUPS):
                sp.dma_start(X[:, 4 * g:4 * g + 4, :], xg[:, 4 * g:4 * g + 4, :]).then_inc(x_in[g], 16)
            for g in range(GROUPS):
                b, cols = g // 2, slice(GT * (g % 2), GT * (g % 2) + GT)
                sp.wait_ge(q_split, g + 1)
                sp.dma_start(q_scratch[:, b, :, cols].rearrange("a p t -> p a t"), qsplit[:, g % 2]).then_inc(splits_stored[g], 16)
                sp.wait_ge(k_split, g + 1)
                sp.dma_start(k_scratch[:, b, :, cols].rearrange("a p t -> p a t"), ksplit[:, g % 2]).then_inc(splits_stored[g], 16)
            for g in range(GROUPS):
                sp.wait_ge(splits_stored[g], 2 * 16)

        @block.scalar
        def _(act):
            for dst, src in ((wq, "Wq"), (wk, "Wk"), (wv, "Wv")):
                act.dma_start(dst[:], dr["L0_attn_" + src]).then_inc(weights_in, 16)
            for dst, src in ((bq, "bq"), (bk, "bk"), (gam, "gamma"), (bet, "beta")):
                act.dma_start(dst[:], dr["L0_attn_" + src].rearrange("(p o) -> p o", o=1)).then_inc(weights_in, 16)
            act.dma_start(bv_rows[:], dr["L0_attn_bv"].rearrange("(o n) -> o n", o=1).broadcast_to([P, H0 * D])).then_inc(weights_in, 16)
            act.wait_ge(weights_in, 8 * 16)
            for g in range(GROUPS):
                act.wait_ge(xnT_psum, g + 1)
                if g >= 2:
                    act.wait_ge(v_psum, g - 1)
                nc.scalar.activation(xnT[:, g % 2, :], ps[:, 0, :], ACT.Identity, scale=gam[:, 0:1], bias=bet[:, 0:1]).then_inc(xnT_ready, 1)
                act.wait_ge(q_psum, g + 1)
                if g >= 1:
                    act.wait_ge(q_split, g)
                nc.scalar.activation(qf[:], ps[:, 1, :], ACT.Identity, bias=bq[:, 0:1]).then_inc(q_ready, 1)
                act.wait_ge(k_psum, g + 1)
                if g >= 1:
                    act.wait_ge(k_split, g)
                nc.scalar.activation(kf[:], ps[:, 2, :], ACT.Identity, bias=bk[:, 0:1]).then_inc(k_ready, 1)

        @block.gpsimd
        def _(pool):
            link = Chain(pool, pool_step)
            link(nc.gpsimd.memset(ident[:], 0.0))
            nc.gpsimd.affine_select(out=ident[:], in_=ident[:], compare_op=ALU.not_equal, fill=1.0, base=0,
                                    pattern=[[-1, P]], channel_multiplier=1).then_inc(ident_ready, 1)
            pool.wait_ge(ident_ready, 1)
            nc.gpsimd.tensor_copy(ident_bf[:], ident[:]).then_inc(ident_ready, 1)
            link(nc.gpsimd.memset(fold_sel[:], 0.0))
            for j in range(4):
                link(nc.gpsimd.affine_select(out=fold_sel[:], in_=fold_sel[:], compare_op=ALU.not_equal, fill=1.0,
                                             base=-32 * j, pattern=[[-1, 32]], channel_multiplier=1))
            link(nc.gpsimd.memset(neg_half[:], -0.5))
            link(nc.gpsimd.memset(zeros8[:], 0.0))
            link(nc.gpsimd.memset(eps_l2[:], 1e-6))
            link(nc.gpsimd.memset(eps_rms[:], LN_EPS))
            link(nc.gpsimd.memset(kst[96:99, 0], 1.0))
            link(nc.gpsimd.memset(kst[96:99, 1], 1.0))
            link(nc.gpsimd.memset(vp[:, :, :, 17:32], 0.0))
            link(nc.gpsimd.memset(vp[:, :, :, 16:17], 1.0))

            def rstd(g):
                pool.wait_ge(stats_ready, g + 1)
                link(nc.gpsimd.tensor_scalar(rs[:, g, :], mv[:, g, :, 1], LN_EPS, None, ALU.add))
                nc.gpsimd.tensor_tensor(rs[:, g, :], rs[:, g, :], neg_half[:, 0:4], ALU.pow).then_inc(rstd_ready, 1)

            rstd(0)
            for g in range(GROUPS):
                if g + 1 < GROUPS:
                    rstd(g + 1)
                pool.wait_ge(q_ready, g + 1)
                if g >= 2:
                    pool.wait_ge(splits_stored[g - 2], 2 * 16)
                split3(nc.gpsimd, link, qsplit[:, g % 2], qf, q_rest, q_split)

        @block.vector
        def _(dve):
            link = Chain(dve, dve_step)

            def stats(g):
                dve.wait_ge(x_in[g], 16)
                for n in range(4):
                    last = nc.vector.bn_stats(st6[:, g, n, :], X[:, 4 * g + n, :])
                link(last)
                for n in range(4):
                    last = nc.vector.bn_aggr(mv[:, g, n, :], st6[:, g, n, :])
                last.then_inc(stats_ready, 1)

            def normalise(g):
                dve.wait_ge(rstd_ready, g + 1)
                if g >= 2:
                    dve.wait_ge(xnT_psum, g - 1)
                for n in range(4):
                    last = nc.vector.tensor_scalar(xn[:, g % 2, n, :], X[:, 4 * g + n, :], mv[:, g, n, 0:1],
                                                   rs[:, g, n:n + 1], ALU.subtract, ALU.mult)
                last.then_inc(xn_ready, 1)

            stats(0)
            normalise(0)
            dve.wait_ge(weights_in, 8 * 16)
            nc.vector.tensor_reduce(wv_sum[:], wv[:].rearrange("p (n e) -> p n e", e=H0), AX.X, ALU.add).then_inc(wv_summed, 1)
            nc.vector.tensor_reduce(bv_sum[:], bv_rows[:].rearrange("p (n e) -> p n e", e=H0), AX.X, ALU.add).then_inc(wv_summed, 1)
            dve.wait_ge(wv_summed, 2)
            for g in range(GROUPS):
                if g + 1 < GROUPS:
                    stats(g + 1)
                    normalise(g + 1)
                b, half = g // 2, g % 2
                dve.wait_ge(v_psum, g + 1)
                heads = vp[:, 8 * b:8 * b + 8, 4 * half:4 * half + 4, 0:16].rearrange("p h t e -> p t h e")
                for t in range(4):
                    last = nc.vector.tensor_tensor(heads[:, t], ps[:, 3, 128 * t:128 * t + 128].rearrange("p (h e) -> p h e", e=16),
                                                   bv_sum[:].rearrange("p (h e) -> p h e", e=16), ALU.add)
                last.then_inc(v_ready, 1)
                dve.wait_ge(k_ready, g + 1)
                if g >= 2:
                    dve.wait_ge(splits_stored[g - 2], 2 * 16)
                split3(nc.vector, link, ksplit[:, g % 2], kf, k_rest, k_split)

        @block.tensor
        def _(pe):
            pe.wait_ge(ident_ready, 2)
            for g in range(GROUPS):
                pe.wait_ge(xn_ready, g + 1)
                if g >= 1:
                    pe.wait_ge(xnT_ready, g)
                for n in range(4):
                    last = nc.tensor.transpose(ps[:, 0, P * n:P * n + P], xn[:, g % 2, n, :], ident[:])
                last.then_inc(xnT_psum, 1)
                pe.wait_ge(xnT_ready, g + 1)
                if g >= 1:
                    pe.wait_ge(q_ready, g)
                nc.tensor.matmul(ps[:, 1, :], wq[:], xnT[:, g % 2, :], start=True, stop=True).then_inc(q_psum, 1)
                if g >= 1:
                    pe.wait_ge(k_ready, g)
                nc.tensor.matmul(ps[:, 2, :], wk[:], xnT[:, g % 2, :], start=True, stop=True).then_inc(k_psum, 1)
                pe.wait_ge(wv_summed, 2)
                if g >= 1:
                    pe.wait_ge(v_ready, g)
                for n in range(4):
                    last = nc.tensor.matmul(ps[:, 3, P * n:P * n + P], xnT[:, g % 2, P * n:P * n + P], wv_sum[:], start=True, stop=True)
                last.then_inc(v_psum, 1)

    with nc.Block() as block:
        mx_in = [sem(f"mx_in{p}") for p in range(2)]
        stack_in = [sem(f"stack_in{p}") for p in range(2)]
        shift_in = sem("shift_in")
        max_psum, max_done = sem("max_psum"), sem("max_done")
        shift_split, shift_psum, shift_rows = sem("shift_split"), sem("shift_psum"), sem("shift_rows")
        score_psum, exp_done = sem("score_psum"), sem("exp_done")
        v_staged, pv_psum = sem("v_staged"), sem("pv_psum")
        ot_half0, ot_half1 = sem("ot_half0"), sem("ot_half1")
        out_psum, out_normed, out_added = sem("out_psum"), sem("out_normed"), sem("out_added")
        dve_step, pool_step = sem("dve_step2"), sem("pool_step2")
        maxp = ps[:, 0:4, :].rearrange("p (k c) t -> p k (c t)", k=2)
        expp = ps[:, 4:6, :]
        pvp = ps[:, 6, :]
        misc = ps[:, 7, :]

        def windows(eng, window):
            for w in range(4):
                window(w, w % 2)
            with eng.Fori(4, NH - 2, 2) as w0:
                for p in range(2):
                    window(w0 + p, p)
            for w in range(NH - 2, NH + 2):
                window(w, w % 2)

        def inside(w, lo, hi):
            return lo <= w < hi if isinstance(w, int) else True

        @block.sync
        def _(sp):
            def load_max(h, p):
                qh = q_scr_h[:, bass.ds(h, 1)]
                kh = k_scr_h[:, bass.ds(h, 1)]
                for r in (0, 64):
                    sp.dma_start(qm[r:r + 32, p, :], qh[0:1].rearrange("a h k t -> (a h k) t").rearrange("(o k) t -> o k t", o=1).broadcast_to([2, 16, S])).then_inc(mx_in[p], 16)
                    sp.dma_start(qm[r + 32:r + 48, p, :], qh[1:2].rearrange("a h k t -> (a h k) t")).then_inc(mx_in[p], 16)
                    sp.dma_start(km[r:r + 32, p, :], kh[0:2].rearrange("a h k t -> a (h k) t")).then_inc(mx_in[p], 16)
                    sp.dma_start(km[r + 32:r + 48, p, :], kh[0:1].rearrange("a h k t -> (a h k) t")).then_inc(mx_in[p], 16)

            def load_stack(h, p):
                qh = q_scr_h[:, bass.ds(h, 1)]
                kh = k_scr_h[:, bass.ds(h, 1)]
                sp.dma_start(qst[0:48, p, :], qh[0:1].rearrange("a h k t -> (a h) k t").broadcast_to([3, 16, S])).then_inc(stack_in[p], 16)
                sp.dma_start(qst[48:80, p, :], qh[1:2].rearrange("a h k t -> (a h) k t").broadcast_to([2, 16, S])).then_inc(stack_in[p], 16)
                sp.dma_start(qst[80:96, p, :], qh[2:3].rearrange("a h k t -> (a h k) t")).then_inc(stack_in[p], 16)
                sp.dma_start(kst[0:48, p, :], kh[0:3].rearrange("a h k t -> a (h k) t")).then_inc(stack_in[p], 16)
                sp.dma_start(kst[48:80, p, :], kh[0:2].rearrange("a h k t -> a (h k) t")).then_inc(stack_in[p], 16)
                sp.dma_start(kst[80:96, p, :], kh[0:1].rearrange("a h k t -> (a h k) t")).then_inc(stack_in[p], 16)

            load_max(0, 0)

            def window(w, p):
                if inside(w, 0, NH - 1):
                    if inside(w, 1, NH):
                        sp.wait_ge(max_psum, 8 * w)
                    load_max(w + 1, 1 - p)
                if inside(w, 1, NH + 1):
                    sp.wait_ge(shift_rows, w)
                    for j in range(3):
                        sp.dma_start(qst[96 + j:97 + j, 1 - p, :], shift_sb[8 * j:8 * j + 8, 1 - p, :]).then_inc(shift_in, 16)
                if inside(w, 0, NH):
                    if inside(w, 2, NH):
                        sp.wait_ge(score_psum, 16 * (w - 1))
                    load_stack(w, p)

            windows(sp, window)

        @block.scalar
        def _(act):
            def exps(h, hp, units):
                for u in units:
                    act.wait_ge(score_psum, 16 * h + u + 1)
                    if inside(h, 1, NH + 9):
                        act.wait_ge(pv_psum, 4 * h - 3 + u // 4)
                    nc.scalar.activation(prob[:, u, :], expp[:, u % 2, :], ACT.Exp, scale=SCORE_SCALE).then_inc(exp_done, 1)

            def window(w, p):
                if inside(w, 2, NH + 2):
                    exps(w - 2, p, (8, 9))
                    act.wait_ge(pv_psum, 4 * (w - 2) + 2)
                    if inside(w, 3, NH + 2):
                        act.wait_ge(out_psum, w - 2)
                    nc.scalar.copy(ot[:, 0, :], pvp).then_inc(ot_half0, 1)
                if inside(w, 1, NH + 1):
                    act.wait_ge(shift_psum, w)
                    if inside(w, 3, NH + 1):
                        act.wait_ge(shift_in, 48 * (w - 2))
                    nc.scalar.copy(shift_sb[0:24, 1 - p, :], misc[0:24, 0:P]).then_inc(shift_rows, 1)
                if inside(w, 2, NH + 2):
                    exps(w - 2, p, range(10, 16))
                if inside(w, 1, NH + 1):
                    exps(w - 1, 1 - p, range(8))

            windows(act, window)

        @block.vector
        def _(dve):
            def row_max(w, p, k):
                dve.wait_ge(max_psum, 8 * w + k + 1)
                if k == 0 and inside(w, 2, NH):
                    dve.wait_ge(shift_split, w - 1)
                nc.vector.tensor_reduce(mx[:, p, k:k + 1], maxp[:, k % 2, :], AX.X, ALU.max).then_inc(max_done, 1)

            def window(w, p):
                for k in range(8):
                    if inside(w, 0, NH):
                        row_max(w, p, k)
                    if k == 5 and inside(w, 2, NH + 2):
                        dve.wait_ge(pv_psum, 4 * (w - 2) + 4)
                        if inside(w, 3, NH + 2):
                            dve.wait_ge(out_psum, w - 2)
                        nc.vector.tensor_copy(ot[:, 1, :], pvp).then_inc(ot_half1, 1)
                if inside(w, 2, NH + 2):
                    dve.wait_ge(out_psum, w - 1)
                    folded = misc[:, 0:256].rearrange("p (m e) -> p m e", e=32)
                    nc.vector.reciprocal(rsum[:], folded[:, :, 16]).then_inc(dve_step, 1)
                    dve.wait_ge(dve_step, w - 1)
                    if inside(w, 3, NH + 2):
                        dve.wait_ge(out_added, w - 2)
                    nc.vector.tensor_tensor(att[:].rearrange("p (m e) -> p m e", e=16), folded[:, :, 0:16],
                                            rsum[:].rearrange("p (m o) -> p m o", o=1).broadcast_to([P, 8, 16]), ALU.mult).then_inc(out_normed, 1)

            windows(dve, window)

        @block.gpsimd
        def _(pool):
            def window(w, p):
                if inside(w, 0, NH):
                    if inside(w, 2, NH):
                        pool.wait_ge(pv_psum, 4 * (w - 1))
                    nc.gpsimd.tensor_copy(vst[:, p], vp[:, bass.ds(w, 1)].rearrange("p h t e -> p (h t) e")).then_inc(v_staged, 1)
                if inside(w, 3, NH + 2):
                    pool.wait_ge(out_normed, w - 2)
                    add_residual(w - 3)
                if inside(w, 0, NH):
                    pool.wait_ge(max_done, 8 * (w + 1))
                    if inside(w, 1, NH):
                        pool.wait_ge(shift_split, w)
                    if inside(w, 2, NH):
                        pool.wait_ge(shift_psum, w - 1)
                    link = Chain(pool, pool_step, 5 * w)
                    link(nc.gpsimd.tensor_tensor(nmax[:, 0, :], zeros8[:], mx[:, p, :], ALU.subtract))
                    link(nc.gpsimd.tensor_tensor(shift3[:, p, 0:8], nmax[:, 0, :], zeros8[:], ALU.add))
                    link(nc.gpsimd.tensor_tensor(nmax[:, 1, :], nmax[:, 0, :], shift3[:, p, 0:8], ALU.subtract))
                    link(nc.gpsimd.tensor_tensor(shift3[:, p, 8:16], nmax[:, 1, :], zeros8[:], ALU.add))
                    link(nc.gpsimd.tensor_tensor(nmax[:, 0, :], nmax[:, 1, :], shift3[:, p, 8:16], ALU.subtract))
                    nc.gpsimd.tensor_tensor(shift3[:, p, 16:24], nmax[:, 0, :], zeros8[:], ALU.add).then_inc(shift_split, 1)

            def add_residual(h):
                tile = X[:, bass.ds(h, 1), :].rearrange("p a d -> p (a d)")
                nc.gpsimd.tensor_tensor(tile, tile, att[:], ALU.add).then_inc(out_added, 1)

            windows(pool, window)
            pool.wait_ge(out_normed, NH)
            add_residual(NH - 1)

        @block.tensor
        def _(pe):
            def row_scores(w, p, k):
                if k == 0:
                    pe.wait_ge(mx_in[p], 8 * 16 * (w // 2 + 1) if isinstance(w, int) else 64 * w + (128 - 64 * p))
                if inside(w, 1, NH) or k >= 2:
                    pe.wait_ge(max_done, 8 * w + k - 1)
                nc.tensor.matmul(maxp[:, k % 2, 0:512], qm[0:48, p, P * k:P * k + P], km[0:48, p, 0:512], start=True, stop=True)
                nc.tensor.matmul(maxp[:, k % 2, 512:1024], qm[64:112, p, P * k:P * k + P], km[64:112, p, 512:1024],
                                 start=True, stop=True).then_inc(max_psum, 1)

            def scores(h, p, units):
                for u in units:
                    if u == 0:
                        pe.wait_ge(stack_in[p], 96 * (h // 2 + 1) if isinstance(h, int) else 48 * h + (96 - 48 * p))
                        pe.wait_ge(shift_in, 48 * (h + 1))
                    if inside(h, 1, NH + 9) or u >= 2:
                        pe.wait_ge(exp_done, 16 * h + u - 1)
                    s, t = u // 8, u % 8
                    nc.tensor.matmul(expp[:, u % 2, :], kst[0:99, p, P * t:P * t + P], qst[0:99, p, 512 * s:512 * s + 512],
                                     start=True, stop=True).then_inc(score_psum, 1)

            def pv(h, p, g):
                pe.wait_ge(exp_done, 16 * h + 4 * g + 4)
                if g == 0:
                    pe.wait_ge(v_staged, h + 1)
                    if inside(h, 1, NH + 9):
                        pe.wait_ge(ot_half1, h)
                if g == 2:
                    pe.wait_ge(ot_half0, h + 1)
                for j in range(4):
                    u = 4 * g + j
                    last = nc.tensor.matmul(pvp[32 * j:32 * j + 32, :], vst[:, p, u % 8, :], prob[:, u, :],
                                            start=(g % 2 == 0), stop=(g % 2 == 1))
                last.then_inc(pv_psum, 1)

            def window(w, p):
                for k in range(8):
                    if k < 4 and inside(w, 2, NH + 2):
                        scores(w - 2, p, (8 + 2 * k, 9 + 2 * k))
                    if k >= 4 and inside(w, 1, NH + 1):
                        scores(w - 1, 1 - p, (2 * k - 8, 2 * k - 7))
                    if inside(w, 0, NH):
                        row_scores(w, p, k)
                    if k == 0 and inside(w, 2, NH + 2):
                        pv(w - 2, p, 1)
                    if k == 0 and inside(w, 1, NH + 1):
                        pe.wait_ge(shift_split, w)
                        if inside(w, 3, NH + 1):
                            pe.wait_ge(out_normed, w - 2)
                        nc.tensor.matmul(misc[0:24, 0:P], shift3[:, 1 - p, :], ident_bf[:], start=True, stop=True).then_inc(shift_psum, 1)
                    if k == 2 and inside(w, 2, NH + 2):
                        pv(w - 2, p, 2)
                    if k == 4 and inside(w, 2, NH + 2):
                        pv(w - 2, p, 3)
                    if k == 6 and inside(w, 2, NH + 2):
                        pe.wait_ge(ot_half0, w - 1)
                        pe.wait_ge(ot_half1, w - 1)
                        if inside(w, 2, NH + 1):
                            pe.wait_ge(shift_rows, w)
                        else:
                            pe.wait_ge(out_normed, w - 2)
                        for m in range(8):
                            last = nc.tensor.matmul(misc[:, 32 * m:32 * m + 32], ot_by_m[:, m, :], fold_sel[:], start=True, stop=True)
                        last.then_inc(out_psum, 1)
                    if k == 6 and inside(w, 1, NH + 1):
                        pv(w - 1, 1 - p, 0)

            windows(pe, window)
    sub.close()
    sub = ExitStack()

    def sb3(name, shape, dt=F32):
        return sub.enter_context(nc.sbuf_tensor(name, shape, dt))

    W1, W2, WH1, WH2, W3 = 0, FH, 2 * FH, 2 * FH + FB * FH, 2 * FH + 2 * FB * FH
    WCOLS = W3 + FB * D
    w_raw = sb3("w_raw", [P, WCOLS])
    w_hi, w_lo = sb3("w_hi", [P, WCOLS], F32R), sb3("w_lo", [P, WCOLS], F32R)
    ffn_scale = sb3("ffn_scale", [P, 4, FB])
    w3s_rows = sb3("w3s_rows", [P, D])
    xt_hi, xt_lo = sb3("xt_hi", [P, GT], F32R), sb3("xt_lo", [P, GT], F32R)
    hf = sb3("hf", [P, FB, GT])
    h_hi, h_lo = sb3("h_hi", [P, 2, FB, GT], F32R), sb3("h_lo", [P, 2, FB, GT], F32R)
    y_tok = sb3("y_tok", [P, 4, P])
    mv2, st62, rs2 = sb3("mv2", [P, GROUPS, 4, 2]), sb3("st62", [P, GROUPS, 4, 6]), sb3("rs2", [P, GROUPS, 4])

    with nc.Block() as block:
        w_in = [sem(f"ffn_w_in{i}") for i in range(5)]
        scales_in = sem("ffn_scales_in")
        w_split = sem("ffn_w_split")
        stats_ready, rstd_ready, x1_ready = sem("ln1_stats"), sem("ln1_rstd"), sem("x1_ready")
        stats2_ready, rstd2_ready, x2_ready = sem("ln2_stats"), sem("ln2_rstd"), sem("x2_ready")
        xT_psum, xT_hi, xT_lo = sem("x1T_psum"), sem("x1T_hi"), sem("x1T_lo")
        gate_psum, up_psum = sem("gate_psum"), sem("up_psum")
        silu_done, h_ready = sem("silu_done"), sem("h_ready")
        hid_psum, gelu_done = sem("hid_psum"), sem("gelu_done")
        hi_ready, lo_ready = sem("h_hi_ready"), sem("h_lo_ready")
        y_psum, y_scaled = sem("y_psum"), sem("y_scaled")
        dve_step, pool_step = sem("dve_step3"), sem("pool_step3")

        def raw(o, n):
            return w_raw[:, o:o + n]

        W_PARTS = ((W1, FH), (W2, FH), (WH1, FB * FH), (WH2, FB * FH), (W3, FB * D))

        @block.sync
        def _(sp):
            sp.dma_start(raw(W1, FH), dr["L0_ffn_w1_w"]).then_inc(w_in[0], 16)
            sp.dma_start(raw(W2, FH), dr["L0_ffn_w2_w"]).then_inc(w_in[1], 16)
            for i, (o, name) in enumerate(((WH1, "h1"), (WH2, "h2"), (W3, "w3"))):
                n = D if name == "w3" else FH
                sp.dma_start(raw(o, FB * n).rearrange("p (k n) -> p k n", k=FB),
                             dr[f"L0_ffn_{name}_w"].rearrange("(k p) n -> p k n", p=P)).then_inc(w_in[2 + i], 16)
            for i, name in enumerate(("w1", "w2", "h1", "h2")):
                sp.dma_start(ffn_scale[:, i, :], dr[f"L0_ffn_{name}_s"]).then_inc(scales_in, 16)
            sp.dma_start(w3s_rows[:], dr["L0_ffn_w3_s"].rearrange("(o n) -> o n", o=1).broadcast_to([P, D])).then_inc(scales_in, 16)
            sp.wait_ge(scales_in, 5 * 16)

        @block.scalar
        def _(act):
            act.wait_ge(scales_in, 5 * 16)

            def transposed(g):
                act.wait_ge(xT_psum, g + 1)
                nc.scalar.copy(xt_hi[:], ps[:, 1, :]).then_inc(xT_hi, 1)

            transposed(0)
            for g in range(GROUPS):
                for o in range(FB):
                    act.wait_ge(gate_psum, 4 * g + o + 1)
                    if g >= 1:
                        act.wait_ge(lo_ready, 12 * g)
                    nc.scalar.activation(hf[:, o, :], ps[:, o, :], ACT.Silu, scale=ffn_scale[:, 0, o:o + 1]).then_inc(silu_done, 1)
                for layer in (1, 2):
                    for o in range(FB):
                        act.wait_ge(hid_psum, 8 * g + 4 * (layer - 1) + o + 1)
                        act.wait_ge(lo_ready, 12 * g + 4 * (layer - 1) + o + 1)
                        nc.scalar.activation(hf[:, o, :], ps[:, 4 * (layer - 1) + o, :], ACT.Gelu,
                                             scale=ffn_scale[:, 1 + layer, o:o + 1]).then_inc(gelu_done, 1)
                if g + 1 < GROUPS:
                    transposed(g + 1)

        @block.gpsimd
        def _(pool):
            link = Chain(pool, pool_step)

            def rstd(g, stats, rstd_sem, mvt, rst):
                pool.wait_ge(stats, g + 1)
                link(nc.gpsimd.tensor_scalar(rst[:, g, :], mvt[:, g, :, 1], LN_EPS, None, ALU.add))
                nc.gpsimd.tensor_tensor(rst[:, g, :], rst[:, g, :], neg_half[:, 0:4], ALU.pow).then_inc(rstd_sem, 1)

            def split_weights(i):
                o, n = W_PARTS[i]
                pool.wait_ge(w_in[i], 16)
                link(nc.gpsimd.tensor_copy(w_hi[:, o:o + n], raw(o, n)))
                nc.gpsimd.tensor_tensor(w_lo[:, o:o + n], raw(o, n), w_hi[:, o:o + n].bitcast(F32), ALU.subtract).then_inc(w_split, 1)

            rstd(0, stats_ready, rstd_ready, mv, rs)
            for i in range(5):
                split_weights(i)
            for g in range(GROUPS):
                for layer in range(3):
                    for o in range(FB):
                        i = 4 * layer + o
                        pool.wait_ge(hi_ready, 12 * g + i + 1)
                        nc.gpsimd.tensor_tensor(h_lo[:, layer % 2, o, :], hf[:, o, :], h_hi[:, layer % 2, o, :].bitcast(F32),
                                                ALU.subtract).then_inc(lo_ready, 1)
                    if layer == 0 and g + 1 < GROUPS:
                        rstd(g + 1, stats_ready, rstd_ready, mv, rs)
                    if layer == 0 and g >= 1:
                        rstd(g - 1, stats2_ready, rstd2_ready, mv2, rs2)
            rstd(GROUPS - 1, stats2_ready, rstd2_ready, mv2, rs2)

        @block.vector
        def _(dve):
            link = Chain(dve, dve_step)

            def stats(g, ready, st, mvt):
                for n in range(4):
                    last = nc.vector.bn_stats(st[:, g, n, :], X[:, 4 * g + n, :])
                link(last)
                for n in range(4):
                    last = nc.vector.bn_aggr(mvt[:, g, n, :], st[:, g, n, :])
                last.then_inc(ready, 1)

            def normalise(g, rstd, ready, mvt, rst):
                dve.wait_ge(rstd, g + 1)
                for n in range(4):
                    tile = X[:, 4 * g + n, :]
                    last = nc.vector.tensor_scalar(tile, tile, mvt[:, g, n, 0:1], rst[:, g, n:n + 1], ALU.subtract, ALU.mult)
                last.then_inc(ready, 1)

            def transposed(g):
                dve.wait_ge(xT_hi, g + 1)
                nc.vector.tensor_tensor(xt_lo[:], ps[:, 1, :], xt_hi[:].bitcast(F32), ALU.subtract).then_inc(xT_lo, 1)

            def hi(g, layer, o):
                nc.vector.tensor_copy(h_hi[:, layer % 2, o, :], hf[:, o, :]).then_inc(hi_ready, 1)

            stats(0, stats_ready, st6, mv)
            normalise(0, rstd_ready, x1_ready, mv, rs)
            transposed(0)
            dve.wait_ge(scales_in, 5 * 16)
            for g in range(GROUPS):
                for o in range(FB):
                    dve.wait_ge(silu_done, 4 * g + o + 1)
                    dve.wait_ge(up_psum, 4 * g + o + 1)
                    nc.vector.scalar_tensor_tensor(hf[:, o, :], ps[:, 4 + o, :], ffn_scale[:, 1, o:o + 1], hf[:, o, :],
                                                   ALU.mult, ALU.mult).then_inc(h_ready, 1)
                    dve.wait_ge(h_ready, 4 * g + o + 1)
                    hi(g, 0, o)
                if g + 1 < GROUPS:
                    stats(g + 1, stats_ready, st6, mv)
                    normalise(g + 1, rstd_ready, x1_ready, mv, rs)
                if g >= 1:
                    normalise(g - 1, rstd2_ready, x2_ready, mv2, rs2)
                for layer in (1, 2):
                    for o in range(FB):
                        dve.wait_ge(gelu_done, 8 * g + 4 * (layer - 1) + o + 1)
                        hi(g, layer, o)
                if g + 1 < GROUPS:
                    transposed(g + 1)
                dve.wait_ge(y_psum, g + 1)
                w3s = w3s_rows[:].rearrange("p (o d) -> p o d", o=1).broadcast_to([P, 4, D])
                link(nc.vector.tensor_tensor(y_tok[:], ps[:, 0, :].rearrange("p (n d) -> p n d", n=4), w3s, ALU.mult))
                link(nc.vector.tensor_tensor(X[:, 4 * g:4 * g + 4, :], X[:, 4 * g:4 * g + 4, :], y_tok[:], ALU.add))
                stats(g, stats2_ready, st62, mv2)
            normalise(GROUPS - 1, rstd2_ready, x2_ready, mv2, rs2)
            dve.wait_ge(x2_ready, GROUPS)

        @block.tensor
        def _(pe):
            def product(out, w, x, start, stop):
                (wh, wl), (xh, xl) = w, x
                nc.tensor.matmul(out, wl, xh, start=start, stop=False)
                nc.tensor.matmul(out, wh, xl, start=False, stop=False)
                return nc.tensor.matmul(out, wh, xh, start=False, stop=stop)

            def weights(o, n):
                return w_hi[:, o:o + n], w_lo[:, o:o + n]

            def transposes(g):
                pe.wait_ge(x1_ready, g + 1)
                if g >= 1:
                    pe.wait_ge(gelu_done, 8 * g - 4)
                for n in range(4):
                    last = nc.tensor.transpose(ps[:, 1, P * n:P * n + P], X[:, 4 * g + n, :], ident[:])
                last.then_inc(xT_psum, 1)

            transposes(0)
            for g in range(GROUPS):
                pe.wait_ge(xT_hi, g + 1)
                pe.wait_ge(xT_lo, g + 1)
                pe.wait_ge(w_split, 2)
                xT = xt_hi[:], xt_lo[:]
                for o in range(FB):
                    if g >= 1:
                        if o == 0:
                            pe.wait_ge(stats2_ready, g)
                        pe.wait_ge(gelu_done, 8 * g - 4 + o + 1)
                    product(ps[:, o, :], weights(W1 + P * o, P), xT, True, True).then_inc(gate_psum, 1)
                    product(ps[:, 4 + o, :], weights(W2 + P * o, P), xT, True, True).then_inc(up_psum, 1)
                for layer, w0 in ((1, WH1), (2, WH2)):
                    src = (layer - 1) % 2
                    for k in range(FB):
                        pe.wait_ge(hi_ready, 12 * g + 4 * (layer - 1) + k + 1)
                        pe.wait_ge(lo_ready, 12 * g + 4 * (layer - 1) + k + 1)
                        if k == 0:
                            pe.wait_ge(w_split, 2 + layer)
                        for o in range(FB):
                            if k == 0:
                                if layer == 1:
                                    pe.wait_ge(silu_done, 4 * g + o + 1)
                                else:
                                    pe.wait_ge(h_ready, 4 * g + o + 1)
                            last = product(ps[:, 4 * (layer - 1) + o, :], weights(w0 + FH * k + P * o, P),
                                           (h_hi[:, src, k, :], h_lo[:, src, k, :]), k == 0, k == FB - 1)
                            if k == FB - 1:
                                last.then_inc(hid_psum, 1)
                if g + 1 < GROUPS:
                    transposes(g + 1)
                pe.wait_ge(lo_ready, 12 * g + 12)
                pe.wait_ge(w_split, 5)
                for n in range(4):
                    for k in range(FB):
                        tok = slice(P * n, P * n + P)
                        last = product(ps[:, 0, tok], (h_hi[:, 0, k, tok], h_lo[:, 0, k, tok]),
                                       weights(W3 + D * k, D), k == 0, k == FB - 1)
                last.then_inc(y_psum, 1)
    sub.close()

    with nc.Block() as block:
        @block.gpsimd
        def _(pool):
            for s in early_sems:
                pool.sem_clear(s)
    early.close()

    def sem(name):
        return ctx.enter_context(nc.semaphore(name))
    sub = ExitStack()

    def sb4(name, shape, dt=F32):
        return sub.enter_context(nc.sbuf_tensor(name, shape, dt))

    def sem4(name, n=1):
        made = [ctx.enter_context(nc.semaphore(f"{name}{i}")) for i in range(n)]
        return made if n > 1 else made[0]

    wqkv, wgates = sb4("wqkv", [P, 3, P]), sb4("wgates", [P, 20])
    wo1 = sb4("wo1", [P, P])
    taps = sb4("taps", [P, 3, CONV])
    fir_s, fir_l = sb4("fir_s", [P, FIRS]), sb4("fir_l", [P, FIRL])
    gate_bias, temp = sb4("gate_bias", [P, 16]), sb4("temp", [P, 4])
    rmsw = sb4("rmsw", [P, 1])
    tapped = sb4("tapped", [P, S])
    head_ones, eye32 = sb4("head_ones", [P, P]), sb4("eye32", [P, C])
    low_mask, up_mask = sb4("low_mask", [P, C]), sb4("up_mask", [P, C])
    gates, mixw = sb4("gates", [P, NT, 8]), sb4("mixw", [P, NT, 12])
    gmax, gsum = sb4("gmax", [P, NT, 4]), sb4("gsum", [P, NT, 4])
    pre_flat = sb4("pre_flat", [P, 3 * B * (S + CONV - 1)])
    pre = pre_flat[:].rearrange("p (i b t) -> p i b t", i=3, b=B)
    uw = pre_flat[:, 0:NT * 4 * 64].rearrange("p (n h e) -> p n h e", n=NT, h=4)
    mt = pre_flat[:, NT * 4 * 64:NT * 4 * 64 + B * S].rearrange("p (b c n e) -> p b c n e", b=B, c=4, n=8)
    xT = sb4("xT4", [P, B * S])
    bc = xT[:].rearrange("p (b c n e) -> p b c n e", b=B, c=4, n=8)
    sq = sb4("sq", [P, B * S])
    gT = sq
    rn = sb4("rn", [P, B * S])
    oT1 = rn
    qs, ks = sb4("qs", [P, B * S]), sb4("ks", [P, B * S])
    vpad = sb4("vpad", [P, B, S + FIRL - 1])
    kt = sb4("kt", [P, NT, P])
    vk = sb4("vk", [P, NT, 4, 2, C])
    low = sb4("low", [P, 4, NT, C])
    attT = sb4("attT", [P, 4, NT, C])
    inv_flat = sb4("inv_flat", [P, 3, B * C * C])
    lp, tp, prod = (inv_flat[:, i].rearrange("p (b i e) -> p b i e", b=B, i=C) for i in range(3))
    mix_rep = inv_flat
    glob_rep = low[:].rearrange("p h n e -> p (h n e)")
    tT = sb4("tT", [P, B, C, C])
    state = sb4("state", [P, 33, B, C])
    short, long_ = sb4("short", [P, B, S]), sb4("long_", [P, B, S])
    mv3, st63, rs3 = sb4("mv3", [P, GROUPS, 4, 2]), sb4("st63", [P, GROUPS, 4, 6]), sb4("rs3", [P, GROUPS, 4])
    low_dram = nc.dram_tensor("low_dram", (B, 4, 8, 4, C, C), F32, kind="Internal").ap()
    inv_dram = nc.dram_tensor("inv_dram", (B, 4, 8, 4, C, C), F32, kind="Internal").ap()

    def rows(ap, g):
        return ap[:, GT * g:GT * g + GT]

    with nc.Block() as block:
        w4_in = sem4("w4_in")
        x_in_psum, xT_ready = sem4("x2T_psum"), sem4("x2T_ready")
        qkv_psum, pre_ready = sem4("qkv_psum"), sem4("pre_ready")
        gates_psum, gates_biased, gates_sig = sem4("gates_psum"), sem4("gates_biased"), sem4("gates_sig")
        mix_in, mix_exp, mix_done = sem4("mix_in"), sem4("mix_exp"), sem4("mix_done")
        temp_exp = sem4("temp_exp")
        rep_ready = sem4("rep_ready")
        padded = sem4("padded")
        conv_done = sem4("conv_done", 2)
        silu_done = sem4("silu_done4")
        sq_ready, ss_psum, rn_ready = sem4("sq_ready"), sem4("ss_psum"), sem4("rn_ready")
        normed = sem4("qk_normed", 2)
        ktok_psum, ktok_ready, vtok_psum, vk_ready, kb_ready = (sem4("ktok_psum"), sem4("ktok_ready"), sem4("vtok_psum"),
                                                                sem4("vk_ready"), sem4("kb_ready"))
        tri_psum, att_psum, tri_masked, att_ready, low_ready = (sem4("tri_psum"), sem4("att_psum"), sem4("tri_masked"),
                                                                sem4("att_ready"), sem4("low_ready"))
        low_stored, low_in, inv_ready, inv_stored, inv_in = (sem4("low_stored", 2), sem4("low_in", 2), sem4("inv_ready", 2),
                                                             sem4("inv_stored", 2), sem4("inv_in", 2))
        uw_psum, uw_ready = sem4("uw_psum"), sem4("uw_ready")
        b_psum, b_ready, m_psum, m_ready = sem4("b_psum"), sem4("b_ready"), sem4("m_psum"), sem4("m_ready")
        o1_psum, o1_ready, g_psum, g_ready = sem4("o1_psum"), sem4("o1_ready"), sem4("g_psum"), sem4("g_ready")
        state_psum, state_ready = sem4("state_psum"), sem4("state_ready")
        o_psum, o_ready = sem4("o_psum"), sem4("o_ready")
        ex_psum, ex_used = sem4("ex_psum"), sem4("ex_used")
        fir_done = sem4("fir_done", 2)
        mixed, blend_in, blended, o_final = sem4("mixed"), sem4("blend_in"), sem4("blended"), sem4("o_final")
        osq_ready, oss_psum, orn_ready, on_ready = sem4("osq_ready"), sem4("oss_psum"), sem4("orn_ready"), sem4("on_ready")
        y_psum, x_added, stats_ready, rstd_ready, x3_ready = (sem4("y4_psum"), sem4("x4_added"), sem4("ln3_stats"),
                                                              sem4("ln3_rstd"), sem4("x3_ready"))
        dve_step, pool_step, act_step = sem4("dve_step4"), sem4("pool_step4"), sem4("act_step4")

        @block.sync
        def _(sp):
            for i, n in enumerate("qkv"):
                sp.dma_start(wqkv[:, i, :], dr[f"L1_attn_W{n}"]).then_inc(w4_in, 16)
                sp.dma_start(taps[:, i, :], dr[f"L1_attn_conv_{n}"]).then_inc(w4_in, 16)
            sp.dma_start(wgates[:, 0:4], dr["L1_attn_Wb"]).then_inc(w4_in, 16)
            sp.dma_start(wgates[:, 4:8], dr["L1_attn_Wg"]).then_inc(w4_in, 16)
            sp.dma_start(wgates[:, 8:20], dr["L1_attn_Wl"]).then_inc(w4_in, 16)
            sp.dma_start(wo1[:], dr["L1_attn_Wo"]).then_inc(w4_in, 16)
            sp.dma_start(fir_s[:], dr["L1_attn_fir_short"].rearrange("h c k -> (h c) k")).then_inc(w4_in, 16)
            sp.dma_start(fir_l[:], dr["L1_attn_fir_long"].rearrange("h c k -> (h c) k")).then_inc(w4_in, 16)
            for dst, name, n in ((gate_bias[:, 0:4], "bg", 4), (gate_bias[:, 4:16], "bl", 12), (temp[:], "log_temp", 4)):
                sp.dma_start(dst, dr["L1_attn_" + name].rearrange("(o n) -> o n", o=1).broadcast_to([P, n])).then_inc(w4_in, 16)
            for h in range(4):
                sp.dma_start(rmsw[32 * h:32 * h + 32, :], dr["L1_attn_rms_w"].rearrange("(p o) -> p o", o=1)).then_inc(w4_in, 16)
            for b in range(B):
                sp.wait_ge(low_ready, b + 1)
                for h in range(4):
                    sp.dma_start(low_dram[b, h].rearrange("n c t e -> (c t) n e"), low[:, h, 8 * b:8 * b + 8, :]).then_inc(low_stored[b], 16)
                sp.wait_ge(low_stored[b], 64)
                sp.dma_start(lp[:, b], low_dram[b].rearrange("h n c t e -> (h n c) t e")).then_inc(low_in[b], 16)
            for b in range(B):
                sp.wait_ge(inv_ready[b], 1)
                sp.dma_start(inv_dram[b].rearrange("h n c e i -> (h n c) e i"), tp[:, b]).then_inc(inv_stored[b], 16)
                sp.wait_ge(inv_stored[b], 16)
                sp.dma_start(tT[:, b], inv_dram[b].rearrange("h n c e i -> (c e) (h n) i")).then_inc(inv_in[b], 16)

        def add_tap(engine, link, dst, src, tap):
            if engine is nc.vector:
                return engine.scalar_tensor_tensor(dst, src, tap, dst, ALU.mult, ALU.add)
            link(engine.tensor_scalar(tapped[:], src, tap, None, ALU.mult))
            return engine.tensor_tensor(dst, dst, tapped[:], ALU.add)

        def convolve(engine, eng, link, b):
            for i in range(3):
                eng.wait_ge(pre_ready, 3 * (2 * b + 2))
                dst = (qs[:, S * b:S * b + S], ks[:, S * b:S * b + S], vpad[:, b, FIRL - 1:])[i]
                link(engine.tensor_scalar(dst, pre[:, i, b, 0:S], taps[:, i, 0:1], None, ALU.mult))
                for t in range(1, CONV):
                    ins = add_tap(engine, link, dst, pre[:, i, b, t:t + S], taps[:, i, t:t + 1])
                    if t < CONV - 1:
                        link(ins)
                    else:
                        ins.then_inc(conv_done[b], 1)

        def fir(engine, link, b, dst, w, lo, hi, done=None):
            k = w.shape[1]
            for t in range(lo, hi):
                src = vpad[:, b, FIRL - k + t:FIRL - k + t + S]
                if t == 0:
                    ins = engine.tensor_scalar(dst[:, b], src, w[:, 0:1], None, ALU.mult)
                else:
                    ins = add_tap(engine, link, dst[:, b], src, w[:, t:t + 1])
                if done is not None and t == hi - 1:
                    ins.then_inc(done, 1)
                else:
                    link(ins)

        def invert(engine, eng, link, b):
            eng.wait_ge(low_in[b], 16)
            for j in range(C - 1):
                n, m = j + 1, C - 1 - j
                part = prod[:, b, 0:n, 0:m]
                link(engine.tensor_tensor(part, lp[:, b, j + 1:C, j:j + 1].rearrange("p i o -> p o i").broadcast_to([P, n, m]),
                                          tp[:, b, 0:n, j:j + 1].broadcast_to([P, n, m]), ALU.mult))
                ins = engine.tensor_tensor(tp[:, b, 0:n, j + 1:C], tp[:, b, 0:n, j + 1:C], part, ALU.subtract)
                if j < C - 2:
                    link(ins)
                else:
                    ins.then_inc(inv_ready[b], 1)

        def start_inverse(engine, link, b):
            link(engine.memset(tp[:, b], 0.0))
            link(engine.memset(tp[:, b].rearrange("p e i -> p (e i)")[:, 0:C * C:C + 1], 1.0))

        def normalise_qk(engine, eng, link, b):
            for i, t in enumerate((qs, ks)):
                for g in (2 * b, 2 * b + 1):
                    eng.wait_ge(rn_ready, 4 * i + g + 1)
                    engine.tensor_tensor(rows(t, g), rows(t, g), rows(rn, g), ALU.mult).then_inc(normed[b], 1)

        @block.vector
        def _(dve):
            link = Chain(dve, dve_step)
            dve.wait_ge(w4_in, 16 * 19)
            for g in range(GROUPS):
                pass
            convolve(nc.vector, dve, link, 0)
            dve.wait_ge(gates_psum, 1)
            gp = ps[:, 5, :].rearrange("p (n e) -> p n e", n=NT)
            bias = gate_bias[:].rearrange("p (o e) -> p o e", o=1)
            nc.vector.tensor_copy(gates[:, :, 0:4], gp[:, :, 0:4])
            nc.vector.tensor_tensor(gates[:, :, 4:8], gp[:, :, 4:8], bias[:, :, 0:4].broadcast_to([P, NT, 4]), ALU.add)
            link(nc.vector.tensor_tensor(mixw[:], gp[:, :, 8:20], bias[:, :, 4:16].broadcast_to([P, NT, 12]), ALU.add))
            logits = mixw[:].rearrange("p n (h j) -> p (n h) j", j=3)
            dve.wait_ge(temp_exp, 1)
            for j in range(3):
                last = nc.vector.tensor_tensor(mixw[:, :, j:12:3], mixw[:, :, j:12:3],
                                               temp[:].rearrange("p (o h) -> p o h", o=1).broadcast_to([P, NT, 4]), ALU.mult)
            link(last)
            gm = gmax[:].rearrange("p n h -> p (n h)")
            gs = gsum[:].rearrange("p n h -> p (n h)")
            link(nc.vector.tensor_reduce(gm, logits, AX.X, ALU.max))
            nc.vector.tensor_tensor(logits, logits, gm.rearrange("p (a o) -> p a o", o=1).broadcast_to([P, 4 * NT, 3]),
                                    ALU.subtract).then_inc(mix_in, 1)
            start_inverse(nc.vector, link, 0)
            normalise_qk(nc.vector, dve, link, 0)
            dve.wait_ge(mix_exp, 1)
            link(nc.vector.tensor_reduce(gs, logits, AX.X, ALU.add))
            link(nc.vector.reciprocal(gs, gs))
            nc.vector.tensor_tensor(logits, logits, gs.rearrange("p (a o) -> p a o", o=1).broadcast_to([P, 4 * NT, 3]),
                                    ALU.mult).then_inc(mix_done, 1)
            dve.wait_ge(gates_sig, 1)
            for g in range(GROUPS):
                dve.wait_ge(vtok_psum, g + 1)
                for n in range(4):
                    t = 4 * g + n
                    last = nc.vector.tensor_tensor(vk[:, t, :, 0, :], ps[:, 2 + g % 2, P * n:P * n + P].rearrange("p (h e) -> p h e", h=4),
                                                   gates[:, t, 0:4].rearrange("p (h o) -> p h o", o=1).broadcast_to([P, 4, C]), ALU.mult)
                last.then_inc(vk_ready, 1)
            for src, mask, dst, ready, done in ((0, low_mask, low, tri_psum, tri_masked), (4, up_mask, attT, att_psum, att_ready)):
                dve.wait_ge(ready, 2)
                for b in range(B):
                    for h in range(4):
                        last = nc.vector.tensor_tensor(dst[:, h, 8 * b:8 * b + 8, :],
                                                       ps[:, src + h, 256 * b:256 * b + 256].rearrange("p (n e) -> p n e", e=C),
                                                       mask[:].rearrange("p (o e) -> p o e", o=1).broadcast_to([P, 8, C]), ALU.mult)
                    last.then_inc(done, 1)
            fir(nc.vector, link, 0, long_, fir_l, 0, 10)
            invert(nc.vector, dve, link, 0)
            fir(nc.vector, link, 0, long_, fir_l, 10, 16)
            for b in range(B):
                cols = slice(256 * b, 256 * b + 256)
                dve.wait_ge(m_psum, 2)
                for c in range(4):
                    last = nc.vector.tensor_tensor(mt[:, b, c], eye32[:].rearrange("p (o e) -> p o e", o=1).broadcast_to([P, 8, C]),
                                                   ps[:, 4 + c, cols].rearrange("p (n e) -> p n e", e=C), ALU.subtract)
                last.then_inc(m_ready, 1)
            for b in range(B):
                cols = slice(256 * b, 256 * b + 256)
                dve.wait_ge(g_psum, 2)
                for c in range(4):
                    view = "p (n c t) -> p c n t"
                    last = nc.vector.tensor_tensor(gT[:, S * b:S * b + S].rearrange(view, n=8, c=4)[:, c],
                                                   qs[:, S * b:S * b + S].rearrange(view, n=8, c=4)[:, c],
                                                   ps[:, 4 + c, cols].rearrange("p (n e) -> p n e", e=C), ALU.subtract)
                last.then_inc(g_ready, 1)
            fir(nc.vector, link, 0, long_, fir_l, 16, FIRL, done=fir_done[0])
            fir(nc.vector, link, 0, short, fir_s, 0, FIRS, done=fir_done[0])
            dve.wait_ge(fir_done[0], 2)
            dve.wait_ge(fir_done[1], 2)
            for g in range(GROUPS):
                b, cols = g // 2, slice(GT * (g % 2), GT * (g % 2) + GT)
                vcols = slice(FIRL - 1 + GT * (g % 2), FIRL - 1 + GT * (g % 2) + GT)
                for j, (dst, src) in enumerate(((rows(ks, g), vpad[:, b, vcols]), (short[:, b, cols], short[:, b, cols]),
                                                (long_[:, b, cols], long_[:, b, cols]))):
                    dve.wait_ge(ex_psum, 3 * g + j + 1)
                    nc.vector.tensor_tensor(dst, ps[:, 2 + (3 * g + j) % 2, :], src, ALU.mult).then_inc(ex_used, 1)
            for g in range(GROUPS):
                dve.wait_ge(o_psum, g + 1)
                nc.vector.tensor_tensor(rows(qs, g), ps[:, 4 + g, :], rows(oT1, g), ALU.add).then_inc(o_ready, 1)
            for g in range(GROUPS):
                dve.wait_ge(blend_in, g + 1)
                dve.wait_ge(ex_psum, 12 + g + 1)
                nc.vector.tensor_tensor(rows(qs, g), ps[:, 2 + g % 2, :], rows(qs, g), ALU.mult).then_inc(blended, 1)
            for g in range(GROUPS):
                dve.wait_ge(orn_ready, g + 1)
                nc.vector.scalar_tensor_tensor(rows(ks, g), rows(ks, g), rmsw[:, 0:1], rows(rn, g), ALU.mult, ALU.mult).then_inc(on_ready, 1)
            for g in range(GROUPS):
                dve.wait_ge(y_psum, g + 1)
                x4 = X[:, 4 * g:4 * g + 4, :].rearrange("p n d -> p (n d)")
                link(nc.vector.tensor_tensor(x4, x4, ps[:, 4 + g, :], ALU.add))
                for n in range(4):
                    last = nc.vector.bn_stats(st63[:, g, n, :], X[:, 4 * g + n, :])
                link(last)
                for n in range(4):
                    last = nc.vector.bn_aggr(mv3[:, g, n, :], st63[:, g, n, :])
                last.then_inc(stats_ready, 1)
            for g in range(GROUPS):
                dve.wait_ge(rstd_ready, g + 1)
                for n in range(4):
                    tile = X[:, 4 * g + n, :]
                    last = nc.vector.tensor_scalar(tile, tile, mv3[:, g, n, 0:1], rs3[:, g, n:n + 1], ALU.subtract, ALU.mult)
                last.then_inc(x3_ready, 1)

        @block.gpsimd
        def _(pool):
            link = Chain(pool, pool_step)
            link(nc.gpsimd.memset(pre[:, :, :, 0:CONV - 1], 0.0))
            link(nc.gpsimd.memset(vpad[:, :, 0:FIRL - 1], 0.0))
            link(nc.gpsimd.memset(state[:, 0], 0.0))
            link(nc.gpsimd.memset(head_ones[:], 0.0))
            link(nc.gpsimd.memset(low_mask[:], 1.0))
            link(nc.gpsimd.memset(up_mask[:], 1.0))
            for h in range(4):
                q = slice(32 * h, 32 * h + 32)
                link(nc.gpsimd.memset(head_ones[q, q], 1.0))
                link(nc.gpsimd.tensor_copy(eye32[q, :], ident[q, q]))
                link(nc.gpsimd.affine_select(out=low_mask[q, :], in_=low_mask[q, :], compare_op=ALU.is_gt, fill=0.0, base=0,
                                             pattern=[[-1, C]], channel_multiplier=1))
                link(nc.gpsimd.affine_select(out=up_mask[q, :], in_=up_mask[q, :], compare_op=ALU.is_ge, fill=0.0, base=0,
                                             pattern=[[1, C]], channel_multiplier=-1))
            nc.gpsimd.tensor_copy(gmax[:, 0, :], ident[:, 0:4]).then_inc(padded, 1)
            pool.wait_ge(w4_in, 16 * 19)
            convolve(nc.gpsimd, pool, link, 1)
            start_inverse(nc.gpsimd, link, 1)
            normalise_qk(nc.gpsimd, pool, link, 1)
            pool.wait_ge(gates_sig, 1)
            for g in range(GROUPS):
                pool.wait_ge(ktok_ready, g + 1)
                for n in range(4):
                    t = 4 * g + n
                    last = nc.gpsimd.tensor_tensor(vk[:, t, :, 1, :], kt[:, t, :].rearrange("p (h e) -> p h e", h=4),
                                                   gates[:, t, 0:4].rearrange("p (h o) -> p h o", o=1).broadcast_to([P, 4, C]), ALU.mult)
                last.then_inc(kb_ready, 1)
            for b in range(B):
                pool.wait_ge(tri_masked, b + 1)
                for h in range(4):
                    tri = low[:, h, 8 * b:8 * b + 8, :]
                    last = nc.gpsimd.tensor_tensor(tri, tri, gates[:, 8 * b:8 * b + 8, h:h + 1].broadcast_to([P, 8, C]), ALU.mult)
                last.then_inc(low_ready, 1)
            fir(nc.gpsimd, link, 1, long_, fir_l, 0, 14)
            invert(nc.gpsimd, pool, link, 1)
            fir(nc.gpsimd, link, 1, long_, fir_l, 14, FIRL, done=fir_done[1])
            fir(nc.gpsimd, link, 1, short, fir_s, 0, FIRS, done=fir_done[1])
            for g in range(GROUPS):
                b, cols = g // 2, slice(GT * (g % 2), GT * (g % 2) + GT)
                pool.wait_ge(ex_used, 3 * g + 3)
                link(nc.gpsimd.tensor_tensor(rows(ks, g), rows(ks, g), short[:, b, cols], ALU.add))
                nc.gpsimd.tensor_tensor(rows(ks, g), rows(ks, g), long_[:, b, cols], ALU.add).then_inc(mixed, 1)
            for g in range(GROUPS):
                pool.wait_ge(o_ready, g + 1)
                pool.wait_ge(mixed, g + 1)
                nc.gpsimd.tensor_tensor(rows(qs, g), rows(qs, g), rows(ks, g), ALU.subtract).then_inc(blend_in, 1)
            for g in range(GROUPS):
                pool.wait_ge(blended, g + 1)
                nc.gpsimd.tensor_tensor(rows(ks, g), rows(ks, g), rows(qs, g), ALU.add).then_inc(o_final, 1)
            for g in range(GROUPS):
                pool.wait_ge(stats_ready, g + 1)
                link(nc.gpsimd.tensor_scalar(rs3[:, g, :], mv3[:, g, :, 1], LN_EPS, None, ALU.add))
                nc.gpsimd.tensor_tensor(rs3[:, g, :], rs3[:, g, :], neg_half[:, 0:4], ALU.pow).then_inc(rstd_ready, 1)

        @block.scalar
        def _(act):
            act.wait_ge(w4_in, 16 * 19)
            act.wait_ge(padded, 1)
            nc.scalar.activation(temp[:], temp[:], ACT.Exp, scale=-1.0).then_inc(temp_exp, 1)
            for g in range(GROUPS):
                act.wait_ge(x_in_psum, g + 1)
                nc.scalar.copy(rows(xT, g), ps[:, g % 2, :]).then_inc(xT_ready, 1)
                for i in range(3):
                    act.wait_ge(qkv_psum, 3 * g + i + 1)
                    nc.scalar.copy(pre[:, i, g // 2, CONV - 1 + GT * (g % 2):CONV - 1 + GT * (g % 2) + GT], ps[:, 2 + i, :]).then_inc(pre_ready, 1)
            for b in range(B):
                for i, t in enumerate((qs, ks, None)):
                    act.wait_ge(conv_done[b], i + 1)
                    t = vpad[:, b, FIRL - 1:] if t is None else t[:, S * b:S * b + S]
                    nc.scalar.activation(t, t, ACT.Silu).then_inc(silu_done, 1)
            act.wait_ge(mix_in, 1)
            nc.scalar.activation(gates[:], gates[:], ACT.Sigmoid).then_inc(gates_sig, 1)
            nc.scalar.preload_act_table_set("natural_log_exp_and_others")
            nc.scalar.activation(mixw[:], mixw[:], ACT.Exp).then_inc(mix_exp, 1)
            for i, t in enumerate((qs, ks)):
                for g in range(GROUPS):
                    n = 4 * i + g
                    act.wait_ge(silu_done, 3 * (g // 2) + i + 1)
                    if i == 1:
                        act.wait_ge(ss_psum, g + 1)
                    nc.scalar.activation(rows(sq, g), rows(t, g), ACT.Square).then_inc(sq_ready, 1)
                for g in range(GROUPS):
                    n = 4 * i + g
                    act.wait_ge(ss_psum, n + 1)
                    if i == 1:
                        act.wait_ge(normed[g // 2], 1 + g % 2)
                    nc.scalar.activation(rows(rn, g), ps[:, 6 + g % 2, :], ACT.Ln, bias=eps_l2[:, 0:1]).then_inc(act_step, 1)
                    act.wait_ge(act_step, n + 1)
                    nc.scalar.activation(rows(rn, g), rows(rn, g), ACT.Exp, scale=-0.5).then_inc(rn_ready, 1)
            for g in range(GROUPS):
                act.wait_ge(ktok_psum, g + 1)
                nc.scalar.copy(kt[:, 4 * g:4 * g + 4, :].rearrange("p n d -> p (n d)"), ps[:, g % 2, :]).then_inc(ktok_ready, 1)
            for b in range(B):
                act.wait_ge(uw_psum, b + 1)
                for k in range(4):
                    last = nc.scalar.copy(uw[:, 8 * b + 2 * k:8 * b + 2 * k + 2].rearrange("p n h e -> p (n h e)"), ps[:, 4 * b + k, :])
                last.then_inc(uw_ready, 1)
            for b in range(B):
                act.wait_ge(b_psum, 2)
                for c in range(4):
                    last = nc.scalar.copy(bc[:, b, c].rearrange("p n e -> p (n e)"), ps[:, c, 256 * b:256 * b + 256])
                last.then_inc(b_ready, 1)
            for b in range(B):
                act.wait_ge(o1_psum, 2)
                for c in range(4):
                    last = nc.scalar.copy(oT1[:, S * b:S * b + S].rearrange("p (n c t) -> p c n t", n=8, c=4)[:, c],
                                          ps[:, c, 256 * b:256 * b + 256].rearrange("p (n e) -> p n e", e=C))
                last.then_inc(o1_ready, 1)
            act.wait_ge(mix_done, 1)
            for b in range(B):
                act.wait_ge(inv_stored[b], 16)
                act.wait_ge(low_in[b], 16)
            for j in range(4):
                src = mixw[:, :, j:12:3] if j < 3 else gates[:, :, 4:8]
                dst = mix_rep[:, j, :] if j < 3 else glob_rep
                for n in range(0, NT, 4):
                    last = nc.scalar.copy(dst[:, P * n:P * n + 4 * P].rearrange("p (n h e) -> p n h e", n=4, h=4),
                                          src[:, n:n + 4, :].rearrange("p n (h o) -> p n h o", o=1).broadcast_to([P, 4, 4, C]))
            last.then_inc(rep_ready, 1)
            for j in range(32):
                act.wait_ge(state_psum, j + 1)
                nc.scalar.copy(state[:, j + 1], ps[:, j % 2, 0:B * C].rearrange("p (b e) -> p b e", b=B)).then_inc(state_ready, 1)
            for g in range(GROUPS):
                act.wait_ge(o_final, g + 1)
                nc.scalar.activation(rows(sq, g), rows(ks, g), ACT.Square).then_inc(osq_ready, 1)
            for g in range(GROUPS):
                act.wait_ge(oss_psum, g + 1)
                nc.scalar.activation(rows(rn, g), ps[:, g, :], ACT.Ln, scale=1.0 / C, bias=eps_rms[:, 0:1]).then_inc(act_step, 1)
                act.wait_ge(act_step, 8 + g + 1)
                nc.scalar.activation(rows(rn, g), rows(rn, g), ACT.Exp, scale=-0.5).then_inc(orn_ready, 1)

        @block.tensor
        def _(pe):
            pe.wait_ge(w4_in, 16 * 19)
            pe.wait_ge(padded, 1)

            def transposes(g):
                if g >= 2:
                    pe.wait_ge(xT_ready, g - 1)
                for n in range(4):
                    last = nc.tensor.transpose(ps[:, g % 2, P * n:P * n + P], X[:, 4 * g + n, :], ident[:])
                last.then_inc(x_in_psum, 1)

            transposes(0)
            for g in range(GROUPS):
                if g + 1 < GROUPS:
                    transposes(g + 1)
                pe.wait_ge(xT_ready, g + 1)
                for i in range(3):
                    if g >= 1:
                        pe.wait_ge(pre_ready, 3 * g - 2 + i)
                    nc.tensor.matmul(ps[:, 2 + i, :], wqkv[:, i, :], rows(xT, g), start=True, stop=True).then_inc(qkv_psum, 1)
                for n in range(4):
                    t = 4 * g + n
                    last = nc.tensor.matmul(ps[:, 5, 32 * t:32 * t + 20], xT[:, P * t:P * t + P], wgates[:], start=True, stop=True)
            last.then_inc(gates_psum, 1)
            for i in range(2):
                for g in range(GROUPS):
                    n = 4 * i + g
                    pe.wait_ge(sq_ready, n + 1)
                    if n >= 2:
                        pe.wait_ge(act_step, n - 1)
                    nc.tensor.matmul(ps[:, 6 + g % 2, :], head_ones[:], rows(sq, g), start=True, stop=True).then_inc(ss_psum, 1)
            for g in range(GROUPS):
                pe.wait_ge(silu_done, 3 * (g // 2) + 3)
                if g >= 2:
                    pe.wait_ge(vk_ready, g - 1)
                for n in range(4):
                    t = 4 * g + n
                    off = FIRL - 1 + P * (t % 8)
                    last = nc.tensor.transpose(ps[:, 2 + g % 2, P * n:P * n + P], vpad[:, t // 8, off:off + P], ident[:])
                last.then_inc(vtok_psum, 1)
                pe.wait_ge(normed[g // 2], 3 + g % 2)
                if g >= 2:
                    pe.wait_ge(ktok_ready, g - 1)
                for n in range(4):
                    t = 4 * g + n
                    last = nc.tensor.transpose(ps[:, g % 2, P * n:P * n + P], ks[:, P * t:P * t + P], ident[:])
                last.then_inc(ktok_psum, 1)
            pe.wait_ge(vk_ready, GROUPS)
            pe.wait_ge(ktok_ready, GROUPS)
            pe.wait_ge(act_step, 8)

            def chunk(n, c):
                t0 = P * n + C * c
                return slice(t0, t0 + C)

            for b in range(B):
                for n in range(8 * b, 8 * b + 8):
                    for h in range(4):
                        f = slice(32 * h, 32 * h + 32)
                        for c in range(4):
                            last = nc.tensor.matmul(ps[32 * c:32 * c + 32, h, 32 * n:32 * n + 32], ks[f, chunk(n, c)], ks[f, chunk(n, c)],
                                                    start=True, stop=True)
                last.then_inc(tri_psum, 1)
            for b in range(B):
                for n in range(8 * b, 8 * b + 8):
                    for h in range(4):
                        f = slice(32 * h, 32 * h + 32)
                        for c in range(4):
                            last = nc.tensor.matmul(ps[32 * c:32 * c + 32, 4 + h, 32 * n:32 * n + 32], ks[f, chunk(n, c)], qs[f, chunk(n, c)],
                                                    start=True, stop=True)
                last.then_inc(att_psum, 1)
            pe.wait_ge(kb_ready, GROUPS)
            for b in range(B):
                pe.wait_ge(inv_in[b], 16)
                pe.wait_ge(tri_masked, 2)
                pe.wait_ge(att_ready, 2)
                for n in range(8):
                    for h in range(4):
                        for c in range(4):
                            r = slice(32 * c, 32 * c + 32)
                            last = nc.tensor.matmul(ps[r, 4 * b + n // 2, (4 * (n % 2) + h) * 64:(4 * (n % 2) + h) * 64 + 64],
                                                    tT[r, b, 8 * h + n, :], vk[r, 8 * b + n, h].rearrange("p a e -> p (a e)"),
                                                    start=True, stop=True)
                last.then_inc(uw_psum, 1)

            def per_chunk(b, bank, lhs, rhs):
                for n in range(8):
                    for c in range(4):
                        for h in range(4):
                            r = slice(32 * c, 32 * c + 32)
                            last = nc.tensor.matmul(ps[32 * h:32 * h + 32, bank + c, 256 * b + 32 * n:256 * b + 32 * n + 32],
                                                    lhs(r, 8 * b + n, h), rhs(r, 8 * b + n, h), start=True, stop=True)
                return last

            def u_of(r, n, h):
                return uw[r, n, h, 0:32]

            def w_of(r, n, h):
                return uw[r, n, h, 32:64]

            def k_of(r, n, h):
                return kt[r, n, 32 * h:32 * h + 32]

            def att_of(r, n, h):
                return attT[r, h, n, :]

            pe.wait_ge(uw_ready, 2)
            for b in range(B):
                per_chunk(b, 4, w_of, k_of).then_inc(m_psum, 1)
            for b in range(B):
                per_chunk(b, 0, k_of, u_of).then_inc(b_psum, 1)
            pe.wait_ge(m_ready, 2)
            for b in range(B):
                per_chunk(b, 4, w_of, att_of).then_inc(g_psum, 1)
            pe.wait_ge(b_ready, 2)
            for b in range(B):
                per_chunk(b, 0, u_of, att_of).then_inc(o1_psum, 1)
            pe.wait_ge(o1_ready, 2)
            for j in range(32):
                n, c = j // 4, j % 4
                if j >= 1:
                    pe.wait_ge(state_ready, j)
                nc.tensor.matmul(ps[:, j % 2, 0:B * C].rearrange("p (b e) -> p b e", b=B), ident[:], bc[:, :, c, n, :], start=True, stop=False,
                                 skip_group_check=True)
                for b in range(B):
                    for h in range(4):
                        f = slice(32 * h, 32 * h + 32)
                        last = nc.tensor.matmul(ps[f, j % 2, C * b:C * b + C], mt[f, b, c, n, :], state[f, j, b, :], start=False, stop=True,
                                                skip_group_check=True)
                last.then_inc(state_psum, 1)
            pe.wait_ge(g_ready, 2)

            def expand(k, reps):
                g = k // 3 if k < 12 else k - 12
                if k >= 2:
                    if k < 14:
                        pe.wait_ge(ex_used, k - 1)
                    if k >= 14:
                        pe.wait_ge(blended, k - 13)
                for n in range(4):
                    t = 4 * g + n
                    last = nc.tensor.transpose(ps[:, 2 + k % 2, P * n:P * n + P],
                                               reps[:, P * t:P * t + P],
                                               ident[:])
                last.then_inc(ex_psum, 1)

            for g in range(GROUPS):
                b = g // 2
                for n in range(4 * (g % 2), 4 * (g % 2) + 4):
                    for c in range(4):
                        for h in range(4):
                            f = slice(32 * h, 32 * h + 32)
                            last = nc.tensor.matmul(ps[f, 4 + g, 128 * (n % 4) + 32 * c:128 * (n % 4) + 32 * c + 32], state[f, 4 * n + c, b, :],
                                                    gT[f, chunk(8 * b + n, c)], start=True, stop=True)
                last.then_inc(o_psum, 1)
            pe.wait_ge(rep_ready, 1)
            for k in range(12):
                expand(k, mix_rep[:, k % 3, :])
            for k in range(12, 16):
                expand(k, glob_rep)
            for g in range(GROUPS):
                pe.wait_ge(osq_ready, g + 1)
                if g >= 2:
                    pe.wait_ge(blended, g + 1)
                nc.tensor.matmul(ps[:, g, :], head_ones[:], rows(sq, g), start=True, stop=True).then_inc(oss_psum, 1)
            for g in range(GROUPS):
                pe.wait_ge(on_ready, g + 1)
                for n in range(4):
                    t = 4 * g + n
                    last = nc.tensor.matmul(ps[:, 4 + g, P * n:P * n + P], ks[:, P * t:P * t + P], wo1[:], start=True, stop=True)
                last.then_inc(y_psum, 1)
    sub.close()
    sub = ExitStack()

    def sb5(name, shape, dt=F32):
        return sub.enter_context(nc.sbuf_tensor(name, shape, dt))

    k0, k1, k2 = sb5("k0", [P, 2, FH], U8), sb5("k1", [P, FB, FH], U8), sb5("k2", [P, FB, D], U8)
    sw0, sw1, sw2 = sb5("sw0", [P, FH], F32R), sb5("sw1", [P, FB, FH], F32R), sb5("sw2", [P, FB, D], F32R)
    s_in, s_out = sb5("s_in", [P, 3]), sb5("s_out", [P, 3])
    xt_hi, xt_lo = sb5("xt_hi5", [P, GT], F32R), sb5("xt_lo5", [P, GT], F32R)
    hf = sb5("hf5", [P, FB, GT])
    h_hi, h_lo = sb5("h_hi5", [P, 2, FB, GT], F32R), sb5("h_lo5", [P, 2, FB, GT], F32R)
    mv4, st64, rs4 = sb5("mv4", [P, GROUPS, 4, 2]), sb5("st64", [P, GROUPS, 4, 6]), sb5("rs4", [P, GROUPS, 4])

    with nc.Block() as block:
        k_in, scales_in = [sem(f"signs_in{i}") for i in range(3)], sem("signs_scales_in")
        first_signs, signs_ready, scales_ready = sem("first_signs"), sem("signs_ready"), sem("signs_scales_ready")
        xT_psum, xT_hi, xT_lo = sem("x3T_psum"), sem("x3T_hi"), sem("x3T_lo")
        hid_psum, relu_done = sem("hid5_psum"), sem("relu_done")
        hi_ready, lo_ready = sem("h5_hi_ready"), sem("h5_lo_ready")
        y_psum = sem("y5_psum")
        stats_ready, rstd_ready, out_ready, stored = sem("ln4_stats"), sem("ln4_rstd"), sem("out_ready"), sem("stored")
        dve_step, pool_step = sem("dve_step5"), sem("pool_step5")

        @block.sync
        def _(sp):
            sp.dma_start(k0[:], dr["L1_ffn_k0"].rearrange("(a p) n -> p a n", p=P)).then_inc(k_in[0], 16)
            sp.dma_start(k1[:], dr["L1_ffn_k1"].rearrange("(a p) n -> p a n", p=P)).then_inc(k_in[1], 16)
            sp.dma_start(k2[:], dr["L1_ffn_k2"].rearrange("(a p) n -> p a n", p=P)).then_inc(k_in[2], 16)
            for i in range(3):
                sp.dma_start(s_in[:, i:i + 1], dr[f"L1_ffn_s{i}"].rearrange("(o n) -> o n", o=1).broadcast_to([P, 1])).then_inc(scales_in, 16)
            out_tiles = out_dram.rearrange("(n p) d -> p n d", p=P)
            for g in range(GROUPS):
                sp.wait_ge(out_ready, g + 1)
                sp.dma_start(out_tiles[:, 4 * g:4 * g + 4, :], X[:, 4 * g:4 * g + 4, :]).then_inc(stored, 16)
            sp.wait_ge(stored, 16 * GROUPS)

        @block.scalar
        def _(act):
            def transposed(g):
                act.wait_ge(xT_psum, g + 1)
                nc.scalar.copy(xt_hi[:], ps[:, 1, :]).then_inc(xT_hi, 1)

            transposed(0)
            act.wait_ge(scales_ready, 1)
            for g in range(GROUPS):
                for layer in range(2):
                    for o in range(FB):
                        act.wait_ge(hid_psum, 8 * g + 4 * layer + o + 1)
                        if g >= 1 or layer == 1:
                            act.wait_ge(lo_ready, 8 * g + 4 * (layer - 1) + o + 1)
                        nc.scalar.activation(hf[:, o, :], ps[:, 4 * layer + o, :], ACT.Relu, scale=s_out[:, layer:layer + 1]).then_inc(relu_done, 1)
                if g + 1 < GROUPS:
                    transposed(g + 1)

        @block.gpsimd
        def _(pool):
            link = Chain(pool, pool_step)
            pool.wait_ge(k_in[1], 16)
            nc.gpsimd.tensor_scalar(sw1[:], k1[:], 2.0, -1.0, ALU.mult, ALU.add).then_inc(signs_ready, 1)
            pool.wait_ge(k_in[2], 16)
            nc.gpsimd.tensor_scalar(sw2[:], k2[:], 2.0, -1.0, ALU.mult, ALU.add).then_inc(signs_ready, 1)

            def rstd(g):
                pool.wait_ge(stats_ready, g + 1)
                link(nc.gpsimd.tensor_scalar(rs4[:, g, :], mv4[:, g, :, 1], LN_EPS, None, ALU.add))
                nc.gpsimd.tensor_tensor(rs4[:, g, :], rs4[:, g, :], neg_half[:, 0:4], ALU.pow).then_inc(rstd_ready, 1)

            for g in range(GROUPS):
                for layer in range(2):
                    for o in range(FB):
                        pool.wait_ge(hi_ready, 8 * g + 4 * layer + o + 1)
                        nc.gpsimd.tensor_tensor(h_lo[:, layer, o, :], hf[:, o, :], h_hi[:, layer, o, :].bitcast(F32), ALU.subtract).then_inc(lo_ready, 1)
                    if layer == 0 and g >= 1:
                        rstd(g - 1)
            rstd(GROUPS - 1)

        @block.vector
        def _(dve):
            link = Chain(dve, dve_step)

            def transposed(g):
                dve.wait_ge(xT_hi, g + 1)
                nc.vector.tensor_tensor(xt_lo[:], ps[:, 1, :], xt_hi[:].bitcast(F32), ALU.subtract).then_inc(xT_lo, 1)

            def normalise(g):
                dve.wait_ge(rstd_ready, g + 1)
                for n in range(4):
                    tile = X[:, 4 * g + n, :]
                    last = nc.vector.tensor_scalar(tile, tile, mv4[:, g, n, 0:1], rs4[:, g, n:n + 1], ALU.subtract, ALU.mult)
                last.then_inc(out_ready, 1)

            dve.wait_ge(k_in[0], 16)
            nc.vector.tensor_tensor(sw0[:], k0[:, 0, :], k0[:, 1, :], ALU.subtract).then_inc(first_signs, 1)
            dve.wait_ge(scales_in, 48)
            nc.vector.tensor_scalar(s_out[:, 0:1], s_in[:, 0:1], 4.0, None, ALU.mult)
            nc.vector.tensor_scalar(s_out[:, 1:2], s_in[:, 1:2], 2.0, None, ALU.mult).then_inc(scales_ready, 1)
            transposed(0)
            for g in range(GROUPS):
                for layer in range(2):
                    for o in range(FB):
                        dve.wait_ge(relu_done, 8 * g + 4 * layer + o + 1)
                        nc.vector.tensor_copy(h_hi[:, layer, o, :], hf[:, o, :]).then_inc(hi_ready, 1)
                    if layer == 0 and g >= 1:
                        normalise(g - 1)
                if g + 1 < GROUPS:
                    transposed(g + 1)
                dve.wait_ge(y_psum, g + 1)
                x4 = X[:, 4 * g:4 * g + 4, :].rearrange("p n d -> p (n d)")
                link(nc.vector.scalar_tensor_tensor(x4, ps[:, 0, :], s_in[:, 2:3], x4, ALU.mult, ALU.add))
                for n in range(4):
                    last = nc.vector.bn_stats(st64[:, g, n, :], X[:, 4 * g + n, :])
                link(last)
                for n in range(4):
                    last = nc.vector.bn_aggr(mv4[:, g, n, :], st64[:, g, n, :])
                last.then_inc(stats_ready, 1)
            normalise(GROUPS - 1)

        @block.tensor
        def _(pe):
            def transposes(g):
                if g >= 1:
                    pe.wait_ge(relu_done, 8 * g - 4)
                for n in range(4):
                    last = nc.tensor.transpose(ps[:, 1, P * n:P * n + P], X[:, 4 * g + n, :], ident[:])
                last.then_inc(xT_psum, 1)

            transposes(0)
            for g in range(GROUPS):
                pe.wait_ge(xT_hi, g + 1)
                pe.wait_ge(xT_lo, g + 1)
                pe.wait_ge(first_signs, 1)
                if g >= 1:
                    pe.wait_ge(stats_ready, g)
                for o in range(FB):
                    w = sw0[:, P * o:P * o + P]
                    nc.tensor.matmul(ps[:, o, :], w, xt_lo[:], start=True, stop=False)
                    nc.tensor.matmul(ps[:, o, :], w, xt_hi[:], start=False, stop=True).then_inc(hid_psum, 1)
                pe.wait_ge(signs_ready, 1)
                for k in range(FB):
                    pe.wait_ge(lo_ready, 8 * g + k + 1)
                    for o in range(FB):
                        if k == 0 and g >= 1:
                            pe.wait_ge(relu_done, 8 * g - 4 + o + 1)
                        w = sw1[:, k, P * o:P * o + P]
                        nc.tensor.matmul(ps[:, 4 + o, :], w, h_lo[:, 0, k, :], start=(k == 0), stop=False)
                        last = nc.tensor.matmul(ps[:, 4 + o, :], w, h_hi[:, 0, k, :], start=False, stop=(k == FB - 1))
                        if k == FB - 1:
                            last.then_inc(hid_psum, 1)
                if g + 1 < GROUPS:
                    transposes(g + 1)
                pe.wait_ge(lo_ready, 8 * g + 8)
                pe.wait_ge(signs_ready, 2)
                for n in range(4):
                    tok = slice(P * n, P * n + P)
                    for k in range(FB):
                        nc.tensor.matmul(ps[:, 0, tok], h_lo[:, 1, k, tok], sw2[:, k, :], start=(k == 0), stop=False)
                        last = nc.tensor.matmul(ps[:, 0, tok], h_hi[:, 1, k, tok], sw2[:, k, :], start=False, stop=(k == FB - 1))
                last.then_inc(y_psum, 1)
    sub.close()


def kernel(**inputs):
    import numpy as _np
    import concourse.bacc as _bacc
    from concourse import mybir as _mybir
    from concourse.bass_utils import run_bass_kernel_spmd as _run

    arrays = {}
    for name, a in inputs.items():
        a = _np.asarray(a)
        if name in ("L0_attn_x",):
            a = a.reshape(-1, a.shape[-1])
        elif name.startswith("L0_ffn") and name.endswith("_w"):
            a = a.T
        elif name.startswith("L0_ffn") and name.endswith("_s") and a.size > 128:
            a = a.reshape(-1, 128).T
        elif a.ndim == 0:
            a = a.reshape(1)
        arrays[name] = _np.ascontiguousarray(a)
    nc = _bacc.Bacc("TRN2", target_bir_lowering=False, num_devices=1)
    dr = {n: nc.dram_tensor(n, a.shape, _mybir.dt.from_np(a.dtype), kind="ExternalInput").ap() for n, a in arrays.items()}
    out = nc.dram_tensor("out", (B * S, D), _mybir.dt.float32, kind="ExternalOutput").ap()
    build(nc, dr, out)
    r = _run(nc, [arrays], core_ids=[0])
    return r.results[0]["out"].reshape(B, S, D)
```

```python
import concourse.bass as bass
from concourse import mybir
from contextlib import ExitStack

F32, F32R, BF16, U8 = mybir.dt.float32, mybir.dt.float32r, mybir.dt.bfloat16, mybir.dt.uint8
ALU = mybir.AluOpType
ACT = mybir.ActivationFunctionType
AX = mybir.AxisListType

P = 128
D = 128
B, S = 2, 1024
NT = B * S // P
GT = 512
GROUPS = B * S // GT
H0 = 8
NH = B * H0
DK0 = D // H0
SCORE_SCALE = float(DK0) ** -0.5
FH = 512
FB = FH // P
LN_EPS = 1e-5
C = 32
CONV, FIRS, FIRL = 4, 3, 31


class Chain:

    def __init__(self, engine, semaphore, base=0):
        self.engine, self.semaphore, self.base, self.n = engine, semaphore, base, 0

    def __call__(self, instruction):
        self.n += 1
        instruction.then_inc(self.semaphore, 1)
        self.engine.wait_ge(self.semaphore, self.base + self.n)


def split3(engine, link, parts, src, rest, done):
    link(engine.tensor_copy(parts[:, 0], src[:]))
    link(engine.tensor_tensor(rest[:, 0], src[:], parts[:, 0], ALU.subtract))
    link(engine.tensor_copy(parts[:, 1], rest[:, 0]))
    link(engine.tensor_tensor(rest[:, 1], rest[:, 0], parts[:, 1], ALU.subtract))
    engine.tensor_copy(parts[:, 2], rest[:, 1]).then_inc(done, 1)


def build(nc, dr, out_dram):
    x_dram = dr["L0_attn_x"]
    q_scratch = nc.dram_tensor("q_scratch", (3, B, P, S), BF16, kind="Internal").ap()
    k_scratch = nc.dram_tensor("k_scratch", (3, B, P, S), BF16, kind="Internal").ap()

    with ExitStack() as ctx:
        program(nc, dr, out_dram, x_dram, q_scratch, k_scratch, ctx)


def program(nc, dr, out_dram, x_dram, q_scratch, k_scratch, ctx):
    def sb(name, shape, dt=F32):
        return ctx.enter_context(nc.sbuf_tensor(name, shape, dt))

    early = ExitStack()
    early_sems = []

    def sem(name):
        early_sems.append(early.enter_context(nc.semaphore(name)))
        return early_sems[-1]

    ps = ctx.enter_context(nc.psum_tensor("ps", [P, 8, 512], F32))
    X = sb("X", [P, NT, D])
    ident, ident_bf = sb("ident", [P, P]), sb("ident_bf", [P, P], BF16)
    neg_half = sb("neg_half", [P, 16])
    st6, mv, rs = sb("st6", [P, GROUPS, 4, 6]), sb("mv", [P, GROUPS, 4, 2]), sb("rs", [P, GROUPS, 4])
    xn = sb("xn", [P, 2, 4, P])
    eps_l2, eps_rms = sb("eps_l2", [P, 1]), sb("eps_rms", [P, 1])
    sub = ExitStack()
    sb_all = sb

    def sb(name, shape, dt=F32):
        return sub.enter_context(nc.sbuf_tensor(name, shape, dt))

    wq, wk, wv = sb("wq", [P, P]), sb("wk", [P, P]), sb("wv", [P, H0 * D])
    bq, bk, gam, bet = sb("bq", [P, 1]), sb("bk", [P, 1]), sb("gam", [P, 1]), sb("bet", [P, 1])
    bv_rows, wv_sum, bv_sum = sb("bv_rows", [P, H0 * D]), sb("wv_sum", [P, P]), sb("bv_sum", [P, P])
    xnT = sb("xnT", [P, 2, GT])
    qf, kf = sb("qf", [P, GT]), sb("kf", [P, GT])
    q_rest, k_rest = sb("q_rest", [P, 2, GT]), sb("k_rest", [P, 2, GT])
    qsplit, ksplit = sb("qsplit", [P, 2, 3, GT], BF16), sb("ksplit", [P, 2, 3, GT], BF16)
    vp = sb("vp", [P, NH, 8, 32])
    fold_sel = sb("fold_sel", [P, 32])
    qst, kst = sb("qst", [P, 2, S], BF16), sb("kst", [P, 2, S], BF16)
    qm, km = sb("qm", [P, 2, S], BF16), sb("km", [P, 2, S], BF16)
    mx, nmax = sb("mx", [P, 2, 8]), sb("nmax", [P, 2, 8])
    shift3, shift_sb = sb("shift3", [P, 2, 24], BF16), sb("shift_sb", [P, 2, P], BF16)
    prob = sb("prob", [P, 16, 512])
    vst = sb("vst", [P, 2, 8, 32])
    ot = sb("ot", [P, 2, 512])
    ot_by_m = ot[:].rearrange("p c t -> p (c t)").rearrange("p (r m) -> p m r", m=8)
    zeros8 = sb("zeros8", [P, 8])
    rsum, att = sb("rsum", [P, 8]), sb("att", [P, P])
    q_scr_h = q_scratch.rearrange("a b (h k) t -> a (b h) k t", k=DK0)
    k_scr_h = k_scratch.rearrange("a b (h k) t -> a (b h) k t", k=DK0)
    with nc.Block() as block:
        x_in = [sem(f"x_in{g}") for g in range(GROUPS)]
        weights_in = sem("weights_in")
        ident_ready = sem("ident_ready")
        stats_ready = sem("stats_ready")
        rstd_ready = sem("rstd_ready")
        xn_ready = sem("xn_ready")
        xnT_psum = sem("xnT_psum")
        xnT_ready = sem("xnT_ready")
        wv_summed = sem("wv_summed")
        q_psum, k_psum, v_psum = sem("q_psum"), sem("k_psum"), sem("v_psum")
        q_ready, k_ready, v_ready = sem("q_ready"), sem("k_ready"), sem("v_ready")
        q_split, k_split = sem("q_split"), sem("k_split")
        splits_stored = [sem(f"splits_stored{g}") for g in range(GROUPS)]
        dve_step, pool_step = sem("dve_step1"), sem("pool_step1")

        @block.sync
        def _(sp):
            xg = x_dram.rearrange("(n p) d -> p n d", p=P)
            for g in range(GROUPS):
                sp.dma_start(X[:, 4 * g:4 * g + 4, :], xg[:, 4 * g:4 * g + 4, :]).then_inc(x_in[g], 16)
            for g in range(GROUPS):
                b, cols = g // 2, slice(GT * (g % 2), GT * (g % 2) + GT)
                sp.wait_ge(q_split, g + 1)
                sp.dma_start(q_scratch[:, b, :, cols].rearrange("a p t -> p a t"), qsplit[:, g % 2]).then_inc(splits_stored[g], 16)
                sp.wait_ge(k_split, g + 1)
                sp.dma_start(k_scratch[:, b, :, cols].rearrange("a p t -> p a t"), ksplit[:, g % 2]).then_inc(splits_stored[g], 16)
            for g in range(GROUPS):
                sp.wait_ge(splits_stored[g], 2 * 16)

        @block.scalar
        def _(act):
            for dst, src in ((wq, "Wq"), (wk, "Wk"), (wv, "Wv")):
                act.dma_start(dst[:], dr["L0_attn_" + src]).then_inc(weights_in, 16)
            for dst, src in ((bq, "bq"), (bk, "bk"), (gam, "gamma"), (bet, "beta")):
                act.dma_start(dst[:], dr["L0_attn_" + src].rearrange("(p o) -> p o", o=1)).then_inc(weights_in, 16)
            act.dma_start(bv_rows[:], dr["L0_attn_bv"].rearrange("(o n) -> o n", o=1).broadcast_to([P, H0 * D])).then_inc(weights_in, 16)
            act.wait_ge(weights_in, 8 * 16)
            for g in range(GROUPS):
                act.wait_ge(xnT_psum, g + 1)
                if g >= 2:
                    act.wait_ge(v_psum, g - 1)
                nc.scalar.activation(xnT[:, g % 2, :], ps[:, 0, :], ACT.Identity, scale=gam[:, 0:1], bias=bet[:, 0:1]).then_inc(xnT_ready, 1)
                act.wait_ge(q_psum, g + 1)
                if g >= 1:
                    act.wait_ge(q_split, g)
                nc.scalar.activation(qf[:], ps[:, 1, :], ACT.Identity, bias=bq[:, 0:1]).then_inc(q_ready, 1)
                act.wait_ge(k_psum, g + 1)
                if g >= 1:
                    act.wait_ge(k_split, g)
                nc.scalar.activation(kf[:], ps[:, 2, :], ACT.Identity, bias=bk[:, 0:1]).then_inc(k_ready, 1)

        @block.gpsimd
        def _(pool):
            link = Chain(pool, pool_step)
            link(nc.gpsimd.memset(ident[:], 0.0))
            nc.gpsimd.affine_select(out=ident[:], in_=ident[:], compare_op=ALU.not_equal, fill=1.0, base=0,
                                    pattern=[[-1, P]], channel_multiplier=1).then_inc(ident_ready, 1)
            pool.wait_ge(ident_ready, 1)
            nc.gpsimd.tensor_copy(ident_bf[:], ident[:]).then_inc(ident_ready, 1)
            link(nc.gpsimd.memset(fold_sel[:], 0.0))
            for j in range(4):
                link(nc.gpsimd.affine_select(out=fold_sel[:], in_=fold_sel[:], compare_op=ALU.not_equal, fill=1.0,
                                             base=-32 * j, pattern=[[-1, 32]], channel_multiplier=1))
            link(nc.gpsimd.memset(neg_half[:], -0.5))
            link(nc.gpsimd.memset(zeros8[:], 0.0))
            link(nc.gpsimd.memset(eps_l2[:], 1e-6))
            link(nc.gpsimd.memset(eps_rms[:], LN_EPS))
            link(nc.gpsimd.memset(kst[96:99, 0], 1.0))
            link(nc.gpsimd.memset(kst[96:99, 1], 1.0))
            link(nc.gpsimd.memset(vp[:, :, :, 17:32], 0.0))
            link(nc.gpsimd.memset(vp[:, :, :, 16:17], 1.0))

            def rstd(g):
                pool.wait_ge(stats_ready, g + 1)
                link(nc.gpsimd.tensor_scalar(rs[:, g, :], mv[:, g, :, 1], LN_EPS, None, ALU.add))
                nc.gpsimd.tensor_tensor(rs[:, g, :], rs[:, g, :], neg_half[:, 0:4], ALU.pow).then_inc(rstd_ready, 1)

            rstd(0)
            for g in range(GROUPS):
                if g + 1 < GROUPS:
                    rstd(g + 1)
                pool.wait_ge(q_ready, g + 1)
                if g >= 2:
                    pool.wait_ge(splits_stored[g - 2], 2 * 16)
                split3(nc.gpsimd, link, qsplit[:, g % 2], qf, q_rest, q_split)

        @block.vector
        def _(dve):
            link = Chain(dve, dve_step)

            def stats(g):
                dve.wait_ge(x_in[g], 16)
                for n in range(4):
                    last = nc.vector.bn_stats(st6[:, g, n, :], X[:, 4 * g + n, :])
                link(last)
                for n in range(4):
                    last = nc.vector.bn_aggr(mv[:, g, n, :], st6[:, g, n, :])
                last.then_inc(stats_ready, 1)

            def normalise(g):
                dve.wait_ge(rstd_ready, g + 1)
                if g >= 2:
                    dve.wait_ge(xnT_psum, g - 1)
                for n in range(4):
                    last = nc.vector.tensor_scalar(xn[:, g % 2, n, :], X[:, 4 * g + n, :], mv[:, g, n, 0:1],
                                                   rs[:, g, n:n + 1], ALU.subtract, ALU.mult)
                last.then_inc(xn_ready, 1)

            stats(0)
            normalise(0)
            dve.wait_ge(weights_in, 8 * 16)
            nc.vector.tensor_reduce(wv_sum[:], wv[:].rearrange("p (n e) -> p n e", e=H0), AX.X, ALU.add).then_inc(wv_summed, 1)
            nc.vector.tensor_reduce(bv_sum[:], bv_rows[:].rearrange("p (n e) -> p n e", e=H0), AX.X, ALU.add).then_inc(wv_summed, 1)
            dve.wait_ge(wv_summed, 2)
            for g in range(GROUPS):
                if g + 1 < GROUPS:
                    stats(g + 1)
                    normalise(g + 1)
                b, half = g // 2, g % 2
                dve.wait_ge(v_psum, g + 1)
                heads = vp[:, 8 * b:8 * b + 8, 4 * half:4 * half + 4, 0:16].rearrange("p h t e -> p t h e")
                for t in range(4):
                    last = nc.vector.tensor_tensor(heads[:, t], ps[:, 3, 128 * t:128 * t + 128].rearrange("p (h e) -> p h e", e=16),
                                                   bv_sum[:].rearrange("p (h e) -> p h e", e=16), ALU.add)
                last.then_inc(v_ready, 1)
                dve.wait_ge(k_ready, g + 1)
                if g >= 2:
                    dve.wait_ge(splits_stored[g - 2], 2 * 16)
                split3(nc.vector, link, ksplit[:, g % 2], kf, k_rest, k_split)

        @block.tensor
        def _(pe):
            pe.wait_ge(ident_ready, 2)
            for g in range(GROUPS):
                pe.wait_ge(xn_ready, g + 1)
                if g >= 1:
                    pe.wait_ge(xnT_ready, g)
                for n in range(4):
                    last = nc.tensor.transpose(ps[:, 0, P * n:P * n + P], xn[:, g % 2, n, :], ident[:])
                last.then_inc(xnT_psum, 1)
                pe.wait_ge(xnT_ready, g + 1)
                if g >= 1:
                    pe.wait_ge(q_ready, g)
                nc.tensor.matmul(ps[:, 1, :], wq[:], xnT[:, g % 2, :], start=True, stop=True).then_inc(q_psum, 1)
                if g >= 1:
                    pe.wait_ge(k_ready, g)
                nc.tensor.matmul(ps[:, 2, :], wk[:], xnT[:, g % 2, :], start=True, stop=True).then_inc(k_psum, 1)
                pe.wait_ge(wv_summed, 2)
                if g >= 1:
                    pe.wait_ge(v_ready, g)
                for n in range(4):
                    last = nc.tensor.matmul(ps[:, 3, P * n:P * n + P], xnT[:, g % 2, P * n:P * n + P], wv_sum[:], start=True, stop=True)
                last.then_inc(v_psum, 1)

    with nc.Block() as block:
        mx_in = [sem(f"mx_in{p}") for p in range(2)]
        stack_in = [sem(f"stack_in{p}") for p in range(2)]
        shift_in = sem("shift_in")
        max_psum, max_done = sem("max_psum"), sem("max_done")
        shift_split, shift_psum, shift_rows = sem("shift_split"), sem("shift_psum"), sem("shift_rows")
        score_psum, exp_done = sem("score_psum"), sem("exp_done")
        v_staged, pv_psum = sem("v_staged"), sem("pv_psum")
        ot_half0, ot_half1 = sem("ot_half0"), sem("ot_half1")
        out_psum, out_normed, out_added = sem("out_psum"), sem("out_normed"), sem("out_added")
        dve_step, pool_step = sem("dve_step2"), sem("pool_step2")
        maxp = ps[:, 0:4, :].rearrange("p (k c) t -> p k (c t)", k=2)
        expp = ps[:, 4:6, :]
        pvp = ps[:, 6, :]
        misc = ps[:, 7, :]

        def windows(eng, window):
            for w in range(4):
                window(w, w % 2)
            with eng.Fori(4, NH - 2, 2) as w0:
                for p in range(2):
                    window(w0 + p, p)
            for w in range(NH - 2, NH + 2):
                window(w, w % 2)

        def inside(w, lo, hi):
            return lo <= w < hi if isinstance(w, int) else True

        @block.sync
        def _(sp):
            def load_max(h, p):
                qh = q_scr_h[:, bass.ds(h, 1)]
                kh = k_scr_h[:, bass.ds(h, 1)]
                for r in (0, 64):
                    sp.dma_start(qm[r:r + 32, p, :], qh[0:1].rearrange("a h k t -> (a h k) t").rearrange("(o k) t -> o k t", o=1).broadcast_to([2, 16, S])).then_inc(mx_in[p], 16)
                    sp.dma_start(qm[r + 32:r + 48, p, :], qh[1:2].rearrange("a h k t -> (a h k) t")).then_inc(mx_in[p], 16)
                    sp.dma_start(km[r:r + 32, p, :], kh[0:2].rearrange("a h k t -> a (h k) t")).then_inc(mx_in[p], 16)
                    sp.dma_start(km[r + 32:r + 48, p, :], kh[0:1].rearrange("a h k t -> (a h k) t")).then_inc(mx_in[p], 16)

            def load_stack(h, p):
                qh = q_scr_h[:, bass.ds(h, 1)]
                kh = k_scr_h[:, bass.ds(h, 1)]
                sp.dma_start(qst[0:48, p, :], qh[0:1].rearrange("a h k t -> (a h) k t").broadcast_to([3, 16, S])).then_inc(stack_in[p], 16)
                sp.dma_start(qst[48:80, p, :], qh[1:2].rearrange("a h k t -> (a h) k t").broadcast_to([2, 16, S])).then_inc(stack_in[p], 16)
                sp.dma_start(qst[80:96, p, :], qh[2:3].rearrange("a h k t -> (a h k) t")).then_inc(stack_in[p], 16)
                sp.dma_start(kst[0:48, p, :], kh[0:3].rearrange("a h k t -> a (h k) t")).then_inc(stack_in[p], 16)
                sp.dma_start(kst[48:80, p, :], kh[0:2].rearrange("a h k t -> a (h k) t")).then_inc(stack_in[p], 16)
                sp.dma_start(kst[80:96, p, :], kh[0:1].rearrange("a h k t -> (a h k) t")).then_inc(stack_in[p], 16)

            load_max(0, 0)

            def window(w, p):
                if inside(w, 0, NH - 1):
                    if inside(w, 1, NH):
                        sp.wait_ge(max_psum, 8 * w)
                    load_max(w + 1, 1 - p)
                if inside(w, 1, NH + 1):
                    sp.wait_ge(shift_rows, w)
                    for j in range(3):
                        sp.dma_start(qst[96 + j:97 + j, 1 - p, :], shift_sb[8 * j:8 * j + 8, 1 - p, :]).then_inc(shift_in, 16)
                if inside(w, 0, NH):
                    if inside(w, 2, NH):
                        sp.wait_ge(score_psum, 16 * (w - 1))
                    load_stack(w, p)

            windows(sp, window)

        @block.scalar
        def _(act):
            def exps(h, hp, units):
                for u in units:
                    act.wait_ge(score_psum, 16 * h + u + 1)
                    if inside(h, 1, NH + 9):
                        act.wait_ge(pv_psum, 4 * h - 3 + u // 4)
                    nc.scalar.activation(prob[:, u, :], expp[:, u % 2, :], ACT.Exp, scale=SCORE_SCALE).then_inc(exp_done, 1)

            def window(w, p):
                if inside(w, 2, NH + 2):
                    exps(w - 2, p, (8, 9))
                    act.wait_ge(pv_psum, 4 * (w - 2) + 2)
                    if inside(w, 3, NH + 2):
                        act.wait_ge(out_psum, w - 2)
                    nc.scalar.copy(ot[:, 0, :], pvp).then_inc(ot_half0, 1)
                if inside(w, 1, NH + 1):
                    act.wait_ge(shift_psum, w)
                    if inside(w, 3, NH + 1):
                        act.wait_ge(shift_in, 48 * (w - 2))
                    nc.scalar.copy(shift_sb[0:24, 1 - p, :], misc[0:24, 0:P]).then_inc(shift_rows, 1)
                if inside(w, 2, NH + 2):
                    exps(w - 2, p, range(10, 16))
                if inside(w, 1, NH + 1):
                    exps(w - 1, 1 - p, range(8))

            windows(act, window)

        @block.vector
        def _(dve):
            def row_max(w, p, k):
                dve.wait_ge(max_psum, 8 * w + k + 1)
                if k == 0 and inside(w, 2, NH):
                    dve.wait_ge(shift_split, w - 1)
                nc.vector.tensor_reduce(mx[:, p, k:k + 1], maxp[:, k % 2, :], AX.X, ALU.max).then_inc(max_done, 1)

            def window(w, p):
                for k in range(8):
                    if inside(w, 0, NH):
                        row_max(w, p, k)
                    if k == 5 and inside(w, 2, NH + 2):
                        dve.wait_ge(pv_psum, 4 * (w - 2) + 4)
                        if inside(w, 3, NH + 2):
                            dve.wait_ge(out_psum, w - 2)
                        nc.vector.tensor_copy(ot[:, 1, :], pvp).then_inc(ot_half1, 1)
                if inside(w, 2, NH + 2):
                    dve.wait_ge(out_psum, w - 1)
                    folded = misc[:, 0:256].rearrange("p (m e) -> p m e", e=32)
                    nc.vector.reciprocal(rsum[:], folded[:, :, 16]).then_inc(dve_step, 1)
                    dve.wait_ge(dve_step, w - 1)
                    if inside(w, 3, NH + 2):
                        dve.wait_ge(out_added, w - 2)
                    nc.vector.tensor_tensor(att[:].rearrange("p (m e) -> p m e", e=16), folded[:, :, 0:16],
                                            rsum[:].rearrange("p (m o) -> p m o", o=1).broadcast_to([P, 8, 16]), ALU.mult).then_inc(out_normed, 1)

            windows(dve, window)

        @block.gpsimd
        def _(pool):
            def window(w, p):
                if inside(w, 0, NH):
                    if inside(w, 2, NH):
                        pool.wait_ge(pv_psum, 4 * (w - 1))
                    nc.gpsimd.tensor_copy(vst[:, p], vp[:, bass.ds(w, 1)].rearrange("p h t e -> p (h t) e")).then_inc(v_staged, 1)
                if inside(w, 3, NH + 2):
                    pool.wait_ge(out_normed, w - 2)
                    add_residual(w - 3)
                if inside(w, 0, NH):
                    pool.wait_ge(max_done, 8 * (w + 1))
                    if inside(w, 1, NH):
                        pool.wait_ge(shift_split, w)
                    if inside(w, 2, NH):
                        pool.wait_ge(shift_psum, w - 1)
                    link = Chain(pool, pool_step, 5 * w)
                    link(nc.gpsimd.tensor_tensor(nmax[:, 0, :], zeros8[:], mx[:, p, :], ALU.subtract))
                    link(nc.gpsimd.tensor_tensor(shift3[:, p, 0:8], nmax[:, 0, :], zeros8[:], ALU.add))
                    link(nc.gpsimd.tensor_tensor(nmax[:, 1, :], nmax[:, 0, :], shift3[:, p, 0:8], ALU.subtract))
                    link(nc.gpsimd.tensor_tensor(shift3[:, p, 8:16], nmax[:, 1, :], zeros8[:], ALU.add))
                    link(nc.gpsimd.tensor_tensor(nmax[:, 0, :], nmax[:, 1, :], shift3[:, p, 8:16], ALU.subtract))
                    nc.gpsimd.tensor_tensor(shift3[:, p, 16:24], nmax[:, 0, :], zeros8[:], ALU.add).then_inc(shift_split, 1)

            def add_residual(h):
                tile = X[:, bass.ds(h, 1), :].rearrange("p a d -> p (a d)")
                nc.gpsimd.tensor_tensor(tile, tile, att[:], ALU.add).then_inc(out_added, 1)

            windows(pool, window)
            pool.wait_ge(out_normed, NH)
            add_residual(NH - 1)

        @block.tensor
        def _(pe):
            def row_scores(w, p, k):
                if k == 0:
                    pe.wait_ge(mx_in[p], 8 * 16 * (w // 2 + 1) if isinstance(w, int) else 64 * w + (128 - 64 * p))
                if inside(w, 1, NH) or k >= 2:
                    pe.wait_ge(max_done, 8 * w + k - 1)
                nc.tensor.matmul(maxp[:, k % 2, 0:512], qm[0:48, p, P * k:P * k + P], km[0:48, p, 0:512], start=True, stop=True)
                nc.tensor.matmul(maxp[:, k % 2, 512:1024], qm[64:112, p, P * k:P * k + P], km[64:112, p, 512:1024],
                                 start=True, stop=True).then_inc(max_psum, 1)

            def scores(h, p, units):
                for u in units:
                    if u == 0:
                        pe.wait_ge(stack_in[p], 96 * (h // 2 + 1) if isinstance(h, int) else 48 * h + (96 - 48 * p))
                        pe.wait_ge(shift_in, 48 * (h + 1))
                    if inside(h, 1, NH + 9) or u >= 2:
                        pe.wait_ge(exp_done, 16 * h + u - 1)
                    s, t = u // 8, u % 8
                    nc.tensor.matmul(expp[:, u % 2, :], kst[0:99, p, P * t:P * t + P], qst[0:99, p, 512 * s:512 * s + 512],
                                     start=True, stop=True).then_inc(score_psum, 1)

            def pv(h, p, g):
                pe.wait_ge(exp_done, 16 * h + 4 * g + 4)
                if g == 0:
                    pe.wait_ge(v_staged, h + 1)
                    if inside(h, 1, NH + 9):
                        pe.wait_ge(ot_half1, h)
                if g == 2:
                    pe.wait_ge(ot_half0, h + 1)
                for j in range(4):
                    u = 4 * g + j
                    last = nc.tensor.matmul(pvp[32 * j:32 * j + 32, :], vst[:, p, u % 8, :], prob[:, u, :],
                                            start=(g % 2 == 0), stop=(g % 2 == 1))
                last.then_inc(pv_psum, 1)

            def window(w, p):
                for k in range(8):
                    if k < 4 and inside(w, 2, NH + 2):
                        scores(w - 2, p, (8 + 2 * k, 9 + 2 * k))
                    if k >= 4 and inside(w, 1, NH + 1):
                        scores(w - 1, 1 - p, (2 * k - 8, 2 * k - 7))
                    if inside(w, 0, NH):
                        row_scores(w, p, k)
                    if k == 0 and inside(w, 2, NH + 2):
                        pv(w - 2, p, 1)
                    if k == 0 and inside(w, 1, NH + 1):
                        pe.wait_ge(shift_split, w)
                        if inside(w, 3, NH + 1):
                            pe.wait_ge(out_normed, w - 2)
                        nc.tensor.matmul(misc[0:24, 0:P], shift3[:, 1 - p, :], ident_bf[:], start=True, stop=True).then_inc(shift_psum, 1)
                    if k == 2 and inside(w, 2, NH + 2):
                        pv(w - 2, p, 2)
                    if k == 4 and inside(w, 2, NH + 2):
                        pv(w - 2, p, 3)
                    if k == 6 and inside(w, 2, NH + 2):
                        pe.wait_ge(ot_half0, w - 1)
                        pe.wait_ge(ot_half1, w - 1)
                        if inside(w, 2, NH + 1):
                            pe.wait_ge(shift_rows, w)
                        else:
                            pe.wait_ge(out_normed, w - 2)
                        for m in range(8):
                            last = nc.tensor.matmul(misc[:, 32 * m:32 * m + 32], ot_by_m[:, m, :], fold_sel[:], start=True, stop=True)
                        last.then_inc(out_psum, 1)
                    if k == 6 and inside(w, 1, NH + 1):
                        pv(w - 1, 1 - p, 0)

            windows(pe, window)
    sub.close()
    sub = ExitStack()

    def sb3(name, shape, dt=F32):
        return sub.enter_context(nc.sbuf_tensor(name, shape, dt))

    W1, W2, WH1, WH2, W3 = 0, FH, 2 * FH, 2 * FH + FB * FH, 2 * FH + 2 * FB * FH
    WCOLS = W3 + FB * D
    w_raw = sb3("w_raw", [P, WCOLS])
    w_hi, w_lo = sb3("w_hi", [P, WCOLS], F32R), sb3("w_lo", [P, WCOLS], F32R)
    ffn_scale = sb3("ffn_scale", [P, 4, FB])
    w3s_rows = sb3("w3s_rows", [P, D])
    xt_hi, xt_lo = sb3("xt_hi", [P, GT], F32R), sb3("xt_lo", [P, GT], F32R)
    hf = sb3("hf", [P, FB, GT])
    h_hi, h_lo = sb3("h_hi", [P, 2, FB, GT], F32R), sb3("h_lo", [P, 2, FB, GT], F32R)
    y_tok = sb3("y_tok", [P, 4, P])
    mv2, st62, rs2 = sb3("mv2", [P, GROUPS, 4, 2]), sb3("st62", [P, GROUPS, 4, 6]), sb3("rs2", [P, GROUPS, 4])

    with nc.Block() as block:
        w_in = [sem(f"ffn_w_in{i}") for i in range(5)]
        scales_in = sem("ffn_scales_in")
        w_split = sem("ffn_w_split")
        stats_ready, rstd_ready, x1_ready = sem("ln1_stats"), sem("ln1_rstd"), sem("x1_ready")
        stats2_ready, rstd2_ready, x2_ready = sem("ln2_stats"), sem("ln2_rstd"), sem("x2_ready")
        xT_psum, xT_hi, xT_lo = sem("x1T_psum"), sem("x1T_hi"), sem("x1T_lo")
        gate_psum, up_psum = sem("gate_psum"), sem("up_psum")
        silu_done, h_ready = sem("silu_done"), sem("h_ready")
        hid_psum, gelu_done = sem("hid_psum"), sem("gelu_done")
        hi_ready, lo_ready = sem("h_hi_ready"), sem("h_lo_ready")
        y_psum, y_scaled = sem("y_psum"), sem("y_scaled")
        dve_step, pool_step = sem("dve_step3"), sem("pool_step3")

        def raw(o, n):
            return w_raw[:, o:o + n]

        W_PARTS = ((W1, FH), (W2, FH), (WH1, FB * FH), (WH2, FB * FH), (W3, FB * D))

        @block.sync
        def _(sp):
            sp.dma_start(raw(W1, FH), dr["L0_ffn_w1_w"]).then_inc(w_in[0], 16)
            sp.dma_start(raw(W2, FH), dr["L0_ffn_w2_w"]).then_inc(w_in[1], 16)
            for i, (o, name) in enumerate(((WH1, "h1"), (WH2, "h2"), (W3, "w3"))):
                n = D if name == "w3" else FH
                sp.dma_start(raw(o, FB * n).rearrange("p (k n) -> p k n", k=FB),
                             dr[f"L0_ffn_{name}_w"].rearrange("(k p) n -> p k n", p=P)).then_inc(w_in[2 + i], 16)
            for i, name in enumerate(("w1", "w2", "h1", "h2")):
                sp.dma_start(ffn_scale[:, i, :], dr[f"L0_ffn_{name}_s"]).then_inc(scales_in, 16)
            sp.dma_start(w3s_rows[:], dr["L0_ffn_w3_s"].rearrange("(o n) -> o n", o=1).broadcast_to([P, D])).then_inc(scales_in, 16)
            sp.wait_ge(scales_in, 5 * 16)

        @block.scalar
        def _(act):
            act.wait_ge(scales_in, 5 * 16)

            def transposed(g):
                act.wait_ge(xT_psum, g + 1)
                nc.scalar.copy(xt_hi[:], ps[:, 1, :]).then_inc(xT_hi, 1)

            transposed(0)
            for g in range(GROUPS):
                for o in range(FB):
                    act.wait_ge(gate_psum, 4 * g + o + 1)
                    if g >= 1:
                        act.wait_ge(lo_ready, 12 * g)
                    nc.scalar.activation(hf[:, o, :], ps[:, o, :], ACT.Silu, scale=ffn_scale[:, 0, o:o + 1]).then_inc(silu_done, 1)
                for layer in (1, 2):
                    for o in range(FB):
                        act.wait_ge(hid_psum, 8 * g + 4 * (layer - 1) + o + 1)
                        act.wait_ge(lo_ready, 12 * g + 4 * (layer - 1) + o + 1)
                        nc.scalar.activation(hf[:, o, :], ps[:, 4 * (layer - 1) + o, :], ACT.Gelu,
                                             scale=ffn_scale[:, 1 + layer, o:o + 1]).then_inc(gelu_done, 1)
                if g + 1 < GROUPS:
                    transposed(g + 1)

        @block.gpsimd
        def _(pool):
            link = Chain(pool, pool_step)

            def rstd(g, stats, rstd_sem, mvt, rst):
                pool.wait_ge(stats, g + 1)
                link(nc.gpsimd.tensor_scalar(rst[:, g, :], mvt[:, g, :, 1], LN_EPS, None, ALU.add))
                nc.gpsimd.tensor_tensor(rst[:, g, :], rst[:, g, :], neg_half[:, 0:4], ALU.pow).then_inc(rstd_sem, 1)

            def split_weights(i):
                o, n = W_PARTS[i]
                pool.wait_ge(w_in[i], 16)
                link(nc.gpsimd.tensor_copy(w_hi[:, o:o + n], raw(o, n)))
                nc.gpsimd.tensor_tensor(w_lo[:, o:o + n], raw(o, n), w_hi[:, o:o + n].bitcast(F32), ALU.subtract).then_inc(w_split, 1)

            rstd(0, stats_ready, rstd_ready, mv, rs)
            for i in range(5):
                split_weights(i)
            for g in range(GROUPS):
                for layer in range(3):
                    for o in range(FB):
                        i = 4 * layer + o
                        pool.wait_ge(hi_ready, 12 * g + i + 1)
                        nc.gpsimd.tensor_tensor(h_lo[:, layer % 2, o, :], hf[:, o, :], h_hi[:, layer % 2, o, :].bitcast(F32),
                                                ALU.subtract).then_inc(lo_ready, 1)
                    if layer == 0 and g + 1 < GROUPS:
                        rstd(g + 1, stats_ready, rstd_ready, mv, rs)
                    if layer == 0 and g >= 1:
                        rstd(g - 1, stats2_ready, rstd2_ready, mv2, rs2)
            rstd(GROUPS - 1, stats2_ready, rstd2_ready, mv2, rs2)

        @block.vector
        def _(dve):
            link = Chain(dve, dve_step)

            def stats(g, ready, st, mvt):
                for n in range(4):
                    last = nc.vector.bn_stats(st[:, g, n, :], X[:, 4 * g + n, :])
                link(last)
                for n in range(4):
                    last = nc.vector.bn_aggr(mvt[:, g, n, :], st[:, g, n, :])
                last.then_inc(ready, 1)

            def normalise(g, rstd, ready, mvt, rst):
                dve.wait_ge(rstd, g + 1)
                for n in range(4):
                    tile = X[:, 4 * g + n, :]
                    last = nc.vector.tensor_scalar(tile, tile, mvt[:, g, n, 0:1], rst[:, g, n:n + 1], ALU.subtract, ALU.mult)
                last.then_inc(ready, 1)

            def transposed(g):
                dve.wait_ge(xT_hi, g + 1)
                nc.vector.tensor_tensor(xt_lo[:], ps[:, 1, :], xt_hi[:].bitcast(F32), ALU.subtract).then_inc(xT_lo, 1)

            def hi(g, layer, o):
                nc.vector.tensor_copy(h_hi[:, layer % 2, o, :], hf[:, o, :]).then_inc(hi_ready, 1)

            stats(0, stats_ready, st6, mv)
            normalise(0, rstd_ready, x1_ready, mv, rs)
            transposed(0)
            dve.wait_ge(scales_in, 5 * 16)
            for g in range(GROUPS):
                for o in range(FB):
                    dve.wait_ge(silu_done, 4 * g + o + 1)
                    dve.wait_ge(up_psum, 4 * g + o + 1)
                    nc.vector.scalar_tensor_tensor(hf[:, o, :], ps[:, 4 + o, :], ffn_scale[:, 1, o:o + 1], hf[:, o, :],
                                                   ALU.mult, ALU.mult).then_inc(h_ready, 1)
                    dve.wait_ge(h_ready, 4 * g + o + 1)
                    hi(g, 0, o)
                if g + 1 < GROUPS:
                    stats(g + 1, stats_ready, st6, mv)
                    normalise(g + 1, rstd_ready, x1_ready, mv, rs)
                if g >= 1:
                    normalise(g - 1, rstd2_ready, x2_ready, mv2, rs2)
                for layer in (1, 2):
                    for o in range(FB):
                        dve.wait_ge(gelu_done, 8 * g + 4 * (layer - 1) + o + 1)
                        hi(g, layer, o)
                if g + 1 < GROUPS:
                    transposed(g + 1)
                dve.wait_ge(y_psum, g + 1)
                w3s = w3s_rows[:].rearrange("p (o d) -> p o d", o=1).broadcast_to([P, 4, D])
                link(nc.vector.tensor_tensor(y_tok[:], ps[:, 0, :].rearrange("p (n d) -> p n d", n=4), w3s, ALU.mult))
                link(nc.vector.tensor_tensor(X[:, 4 * g:4 * g + 4, :], X[:, 4 * g:4 * g + 4, :], y_tok[:], ALU.add))
                stats(g, stats2_ready, st62, mv2)
            normalise(GROUPS - 1, rstd2_ready, x2_ready, mv2, rs2)
            dve.wait_ge(x2_ready, GROUPS)

        @block.tensor
        def _(pe):
            def product(out, w, x, start, stop):
                (wh, wl), (xh, xl) = w, x
                nc.tensor.matmul(out, wl, xh, start=start, stop=False)
                nc.tensor.matmul(out, wh, xl, start=False, stop=False)
                return nc.tensor.matmul(out, wh, xh, start=False, stop=stop)

            def weights(o, n):
                return w_hi[:, o:o + n], w_lo[:, o:o + n]

            def transposes(g):
                pe.wait_ge(x1_ready, g + 1)
                if g >= 1:
                    pe.wait_ge(gelu_done, 8 * g - 4)
                for n in range(4):
                    last = nc.tensor.transpose(ps[:, 1, P * n:P * n + P], X[:, 4 * g + n, :], ident[:])
                last.then_inc(xT_psum, 1)

            transposes(0)
            for g in range(GROUPS):
                pe.wait_ge(xT_hi, g + 1)
                pe.wait_ge(xT_lo, g + 1)
                pe.wait_ge(w_split, 2)
                xT = xt_hi[:], xt_lo[:]
                for o in range(FB):
                    if g >= 1:
                        if o == 0:
                            pe.wait_ge(stats2_ready, g)
                        pe.wait_ge(gelu_done, 8 * g - 4 + o + 1)
                    product(ps[:, o, :], weights(W1 + P * o, P), xT, True, True).then_inc(gate_psum, 1)
                    product(ps[:, 4 + o, :], weights(W2 + P * o, P), xT, True, True).then_inc(up_psum, 1)
                for layer, w0 in ((1, WH1), (2, WH2)):
                    src = (layer - 1) % 2
                    for k in range(FB):
                        pe.wait_ge(hi_ready, 12 * g + 4 * (layer - 1) + k + 1)
                        pe.wait_ge(lo_ready, 12 * g + 4 * (layer - 1) + k + 1)
                        if k == 0:
                            pe.wait_ge(w_split, 2 + layer)
                        for o in range(FB):
                            if k == 0:
                                if layer == 1:
                                    pe.wait_ge(silu_done, 4 * g + o + 1)
                                else:
                                    pe.wait_ge(h_ready, 4 * g + o + 1)
                            last = product(ps[:, 4 * (layer - 1) + o, :], weights(w0 + FH * k + P * o, P),
                                           (h_hi[:, src, k, :], h_lo[:, src, k, :]), k == 0, k == FB - 1)
                            if k == FB - 1:
                                last.then_inc(hid_psum, 1)
                if g + 1 < GROUPS:
                    transposes(g + 1)
                pe.wait_ge(lo_ready, 12 * g + 12)
                pe.wait_ge(w_split, 5)
                for n in range(4):
                    for k in range(FB):
                        tok = slice(P * n, P * n + P)
                        last = product(ps[:, 0, tok], (h_hi[:, 0, k, tok], h_lo[:, 0, k, tok]),
                                       weights(W3 + D * k, D), k == 0, k == FB - 1)
                last.then_inc(y_psum, 1)
    sub.close()

    with nc.Block() as block:
        @block.gpsimd
        def _(pool):
            for s in early_sems:
                pool.sem_clear(s)
    early.close()

    def sem(name):
        return ctx.enter_context(nc.semaphore(name))
    sub = ExitStack()

    def sb4(name, shape, dt=F32):
        return sub.enter_context(nc.sbuf_tensor(name, shape, dt))

    def sem4(name, n=1):
        made = [ctx.enter_context(nc.semaphore(f"{name}{i}")) for i in range(n)]
        return made if n > 1 else made[0]

    XCOLS = S + CONV - 1
    FIR_PE = 8
    wqkv, wgates = sb4("wqkv", [P, 3, P]), sb4("wgates", [P, 20])
    prep = sb4("prep", [P, 4 * P * CONV])
    tap_rows = prep[:, 0:3 * P * CONV].rearrange("p (i c) -> p i c", i=3)
    wc_full = prep[:, 3 * P * CONV:].rearrange("p (k c) -> p k c", k=CONV)
    bc = prep[:].rearrange("p (b c n e) -> p b c n e", b=B, c=4, n=8)
    wc_hi, wc_lo = sb4("wc_hi", [P, 3, CONV, P], F32R), sb4("wc_lo", [P, 3, CONV, P], F32R)
    wo1 = sb4("wo1", [P, P])
    fir_s, fir_l = sb4("fir_s", [P, FIRS]), sb4("fir_l", [P, FIRL])
    fir_diag = sb4("fir_diag", [P, FIR_PE, P])
    gate_bias, temp = sb4("gate_bias", [P, 16]), sb4("temp", [P, 4])
    rmsw = sb4("rmsw", [P, 1])
    head_ones, eye32 = sb4("head_ones", [P, P]), sb4("eye32", [P, C])
    low_mask, up_mask = sb4("low_mask", [P, C]), sb4("up_mask", [P, C])
    gates, mixw = sb4("gates", [P, NT, 8]), sb4("mixw", [P, NT, 12])
    gmax, gsum = sb4("gmax", [P, NT, 4]), sb4("gsum", [P, NT, 4])
    keep_local = sb4("keep_local", [P, NT, 4])
    xf = sb4("xf", [P, GT])
    x_hi, x_lo = sb4("x_hi4", [P, B, XCOLS], F32R), sb4("x_lo4", [P, B, XCOLS], F32R)
    mt = sb4("mt", [P, B, 4, 8, C])
    ks, qs = sb4("ks", [P, B * S]), sb4("qs", [P, B * S])
    vpad = sb4("vpad", [P, B, S + FIRL - 1])
    sq, rn = sb4("sq", [P, 2, GT]), sb4("rn", [P, 2, GT])
    vtok = sb4("vtok", [P, NT, P])
    ka = sb4("ka", [P, NT, 4, 2, C])
    vk = sb4("vk", [P, NT, 4, 2, C])
    low = sb4("low", [P, 4, NT, C])
    inv_flat = sb4("inv_flat", [P, B, 3, C * C])
    lp, tp, prod = (inv_flat[:, :, i].rearrange("p b (i e) -> p b i e", i=C) for i in range(3))
    tT = sb4("tT", [P, B, C, C])
    state = sb4("state", [P, 33, B, C])
    short, long_ = sb4("short", [P, B, S]), sb4("long_", [P, B, S])
    tapped = sq[:].rearrange("p i t -> p (i t)")
    gT = qs
    blend = low[:].rearrange("p h (a n) e -> p (h a) (n e)", a=1)
    oss, ors = sb4("oss", [P, GROUPS, 16]), sb4("ors", [P, GROUPS, 16])
    osq, oT = (vk[:, 8 * i:8 * i + 4].rearrange("p n h a e -> p (n h a e)").rearrange("p (i t) -> p i t", i=2) for i in range(2))
    mv3, st63, rs3 = sb4("mv3", [P, GROUPS, 4, 2]), sb4("st63", [P, GROUPS, 4, 6]), sb4("rs3", [P, GROUPS, 4])
    low_dram = nc.dram_tensor("low_dram", (B, 4, 8, 4, C, C), F32, kind="Internal").ap()
    inv_dram = nc.dram_tensor("inv_dram", (B, 4, 8, 4, C, C), F32, kind="Internal").ap()

    def uw(b, r, n, h):
        o = (4 * n + h) * 64
        return inv_flat[r, b].rearrange("p i e -> p (i e)")[:, o:o + 64]

    def rows(ap, g):
        return ap[:, GT * g:GT * g + GT]

    def v_rows(g):
        return vpad[:, g // 2, FIRL - 1 + GT * (g % 2):FIRL - 1 + GT * (g % 2) + GT]

    def heads(ap):
        return ap.rearrange("p (n h e) -> p n h e", h=4, e=C)

    def per_head(ap):
        return ap.rearrange("p n (h o) -> p n h o", o=1).broadcast_to([P, ap.shape[1], 4, C])

    FINAL = (0, 2, 1, 3)

    with nc.Block() as block:
        k_in, q_in, v_in, gates_in, rest_in = sem4("wk4_in"), sem4("wq4_in"), sem4("wv4_in"), sem4("gates_in"), sem4("rest_in")
        padded, masks_ready, temp_exp = sem4("padded"), sem4("masks_ready"), sem4("temp_exp")
        wc_full_ready, wc_ready, diag_ready, wo_scaled = sem4("wc_full_ready"), sem4("wc_ready"), sem4("diag_ready"), sem4("wo_scaled")
        xT_psum, xf_ready, xhi_ready, xlo_ready = sem4("x2T_psum"), sem4("xf_ready"), sem4("xhi_ready"), sem4("xlo_ready")
        conv_psum, silu_done = sem4("conv_psum"), sem4("silu_done4")
        gates_psum, gates_biased, gates_exp, beta_ready, mix_done = (sem4("gates_psum"), sem4("gates_biased"), sem4("gates_exp"),
                                                                     sem4("beta_ready"), sem4("mix_done"))
        sq_ready, ss_psum, ln_done, rn_ready, normed = (sem4("sq_ready"), sem4("ss_psum"), sem4("ln_done"), sem4("rn_ready"),
                                                        sem4("qk_normed"))
        vtok_psum, vtok_ready, ktok_psum, ktok_ready, vb_ready, kb_ready = (
            sem4("vtok_psum"), sem4("vtok_ready"), sem4("ktok_psum"), sem4("ktok_ready"), sem4("vb_ready"), sem4("kb_ready"))
        tri_psum, att_psum, tri_masked, att_ready, low_ready = (sem4("tri_psum"), sem4("att_psum"), sem4("tri_masked"),
                                                                sem4("att_ready"), sem4("low_ready", 2))
        low_stored, low_in, inv_ready, inv_stored, inv_in = (sem4("low_stored", 2), sem4("low_in", 2), sem4("inv_ready", 2),
                                                             sem4("inv_stored", 2), sem4("inv_in", 2))
        fir_psum, fir_begun, long_done, short_done = sem4("fir_psum"), sem4("fir_begun"), sem4("long_done"), sem4("short_done")
        uw_psum, uw_ready, mg_psum, m_ready, g_ready, b_psum, b_ready = (
            sem4("uw_psum"), sem4("uw_ready"), sem4("mg_psum"), sem4("m_ready"), sem4("g_ready"), sem4("b_psum"), sem4("b_ready"))
        state_psum, state_ready, o_begun, o_psum = sem4("state_psum"), sem4("state_ready"), sem4("o_begun"), sem4("o_psum")
        local_psum, local_used, local_ready = sem4("local_psum"), sem4("local_used"), sem4("local_ready")
        blended, osq_ready, oss_ready, ors_ready, o_scaled = (sem4("blended"), sem4("osq_ready"), sem4("oss_ready"), sem4("ors_ready"),
                                                              sem4("o_scaled"))
        oT_psum, oT_ready, y_psum, stats_ready, rstd_ready, x3_ready = (
            sem4("oT_psum"), sem4("oT_ready"), sem4("y4_psum"), sem4("ln3_stats"), sem4("ln3_rstd"), sem4("x3_ready"))
        dve_step, pool_step = sem4("dve_step4"), sem4("pool_step4")

        CONVS = (("k", k_in), ("q", q_in), ("v", v_in))

        @block.sync
        def _(sp):
            for i, (n, arrived) in enumerate(CONVS):
                sp.dma_start(wqkv[:, i, :], dr[f"L1_attn_W{n}"]).then_inc(arrived, 16)
                sp.dma_start(tap_rows[:, i, :], dr[f"L1_attn_conv_{n}"].rearrange("(o c) k -> o (c k)", o=1).broadcast_to([P, P * CONV])).then_inc(arrived, 16)
            sp.dma_start(wgates[:, 0:4], dr["L1_attn_Wb"]).then_inc(gates_in, 16)
            sp.dma_start(wgates[:, 4:8], dr["L1_attn_Wg"]).then_inc(gates_in, 16)
            sp.dma_start(wgates[:, 8:20], dr["L1_attn_Wl"]).then_inc(gates_in, 16)
            for dst, name, n in ((gate_bias[:, 0:4], "bg", 4), (gate_bias[:, 4:16], "bl", 12), (temp[:], "log_temp", 4)):
                sp.dma_start(dst, dr["L1_attn_" + name].rearrange("(o n) -> o n", o=1).broadcast_to([P, n])).then_inc(gates_in, 16)
            sp.dma_start(fir_s[:], dr["L1_attn_fir_short"].rearrange("h c k -> (h c) k")).then_inc(rest_in, 16)
            sp.dma_start(fir_l[:], dr["L1_attn_fir_long"].rearrange("h c k -> (h c) k")).then_inc(rest_in, 16)
            sp.dma_start(wo1[:], dr["L1_attn_Wo"]).then_inc(rest_in, 16)
            for h in range(4):
                sp.dma_start(rmsw[32 * h:32 * h + 32, :], dr["L1_attn_rms_w"].rearrange("(p o) -> p o", o=1)).then_inc(rest_in, 16)
            for b in range(B):
                sp.wait_ge(low_ready[b], 2)
                for h in range(4):
                    sp.dma_start(low_dram[b, h].rearrange("n c t e -> (c t) n e"), low[:, h, 8 * b:8 * b + 8, :]).then_inc(low_stored[b], 16)
                sp.wait_ge(low_stored[b], 64)
                sp.dma_start(lp[:, b], low_dram[b].rearrange("h n c t e -> (h n c) t e")).then_inc(low_in[b], 16)
            for b in range(B):
                sp.wait_ge(inv_ready[b], 1)
                sp.dma_start(inv_dram[b].rearrange("h n c e i -> (h n c) e i"), tp[:, b]).then_inc(inv_stored[b], 16)
                sp.wait_ge(inv_stored[b], 16)
                sp.dma_start(tT[:, b], inv_dram[b].rearrange("h n c e i -> (c e) (h n) i")).then_inc(inv_in[b], 16)

        def invert(engine, eng, link, b):
            eng.wait_ge(low_in[b], 16)
            for j in range(C - 1):
                n, m = j + 1, C - 1 - j
                part = prod[:, b, 0:n, 0:m]
                link(engine.tensor_tensor(part, lp[:, b, j + 1:C, j:j + 1].rearrange("p i o -> p o i").broadcast_to([P, n, m]),
                                          tp[:, b, 0:n, j:j + 1].broadcast_to([P, n, m]), ALU.mult))
                ins = engine.tensor_tensor(tp[:, b, 0:n, j + 1:C], tp[:, b, 0:n, j + 1:C], part, ALU.subtract)
                if j < C - 2:
                    link(ins)
                else:
                    ins.then_inc(inv_ready[b], 1)

        def start_inverse(engine, link, b):
            link(engine.memset(tp[:, b], 0.0))
            link(engine.memset(tp[:, b].rearrange("p e i -> p (e i)")[:, 0:C * C:C + 1], 1.0))

        def times_beta(engine, eng, g):
            for src, i, ready, done in ((vtok[:, 4 * g:4 * g + 4, :], 0, vtok_ready, vb_ready), (None, 1, ktok_ready, kb_ready)):
                eng.wait_ge(ready, g + 1)
                for n in range(4):
                    t = 4 * g + n
                    src = vtok[:, t, :].rearrange("p (h e) -> p h e", h=4) if i == 0 else ka[:, t, :, 0, :]
                    last = engine.tensor_tensor(vk[:, t, :, i, :], src,
                                                gates[:, t, 0:4].rearrange("p (h o) -> p h o", o=1).broadcast_to([P, 4, C]), ALU.mult)
                last.then_inc(done, 1)

        def triangles_times_beta(engine, eng, g):
            eng.wait_ge(tri_masked, g + 1)
            t = 4 * g
            for h in range(4):
                tri = low[:, h, t:t + 4, :]
                last = engine.tensor_tensor(tri, tri, gates[:, t:t + 4, h:h + 1].broadcast_to([P, 4, C]), ALU.mult)
            last.then_inc(low_ready[g // 2], 1)

        @block.vector
        def _(dve):
            link = Chain(dve, dve_step)

            def split_x(g):
                dve.wait_ge(xhi_ready, g + 1)
                cols = slice(CONV - 1 + GT * (g % 2), CONV - 1 + GT * (g % 2) + GT)
                nc.vector.tensor_tensor(x_lo[:, g // 2, cols], ps[:, 0, :], x_hi[:, g // 2, cols].bitcast(F32), ALU.subtract).then_inc(xlo_ready, 1)

            def square(g, i):
                dve.wait_ge(silu_done, 3 * g + i + 1)
                if g >= 1:
                    dve.wait_ge(ss_psum, 2 * g - 1 + i)
                t = rows((ks, qs)[i], g)
                nc.vector.tensor_tensor(sq[:, i, :], t, t, ALU.mult).then_inc(sq_ready, 1)

            def normalise(g, i):
                dve.wait_ge(rn_ready, 2 * g + i + 1)
                t = rows((ks, qs)[i], g)
                nc.vector.tensor_tensor(t, t, rn[:, i, :], ALU.mult).then_inc(normed, 1)

            def gate_logits(g):
                dve.wait_ge(gates_psum, g + 1)
                n4 = slice(4 * g, 4 * g + 4)
                gp = ps[:, 3, 0:80].rearrange("p (n e) -> p n e", n=4)
                bias = gate_bias[:].rearrange("p (o e) -> p o e", o=1)
                nc.vector.tensor_copy(gates[:, n4, 0:4], gp[:, :, 0:4])
                nc.vector.tensor_tensor(gates[:, n4, 4:8], gp[:, :, 4:8], bias[:, :, 0:4].broadcast_to([P, 4, 4]), ALU.add)
                link(nc.vector.tensor_tensor(mixw[:, n4, :], gp[:, :, 8:20], bias[:, :, 4:16].broadcast_to([P, 4, 12]), ALU.add))
                for j in range(3):
                    last = nc.vector.tensor_tensor(mixw[:, n4, j:12:3], mixw[:, n4, j:12:3],
                                                   temp[:].rearrange("p (o h) -> p o h", o=1).broadcast_to([P, 4, 4]), ALU.mult)
                link(last)
                logits = mixw[:, n4, :].rearrange("p n (h j) -> p (n h) j", j=3)
                gm = gmax[:, n4, :].rearrange("p n h -> p (n h)")
                link(nc.vector.tensor_reduce(gm, logits, AX.X, ALU.max))
                nc.vector.tensor_tensor(logits, logits, gm.rearrange("p (a o) -> p a o", o=1).broadcast_to([P, 16, 3]),
                                        ALU.subtract).then_inc(gates_biased, 1)

            def gate_sigmoids(g):
                dve.wait_ge(gates_exp, g + 1)
                n4 = slice(4 * g, 4 * g + 4)
                link(nc.vector.tensor_scalar(gates[:, n4, :], gates[:, n4, :], 1.0, None, ALU.add))
                nc.vector.reciprocal(gates[:, n4, :], gates[:, n4, :]).then_inc(beta_ready, 1)

            def masks(g):
                dve.wait_ge(tri_psum, g + 1)
                n4 = slice(4 * g, 4 * g + 4)

                def mask4(m):
                    return m[:].rearrange("p (a o e) -> p a o e", a=1, o=1).broadcast_to([P, 4, 4, C])

                nc.vector.tensor_tensor(low[:, :, n4, :], ps[:, 4:8, 0:128].rearrange("p h (n e) -> p h n e", e=C), mask4(low_mask),
                                        ALU.mult).then_inc(tri_masked, 1)
                nc.vector.tensor_tensor(ka[:, n4, :, 1, :].rearrange("p n h e -> p h n e"),
                                        ps[:, 4:8, 128:256].rearrange("p h (n e) -> p h n e", e=C), mask4(up_mask),
                                        ALU.mult).then_inc(att_ready, 1)

            def fir(b, lo, hi, done=False):
                dve.wait_ge(fir_begun, 2 * b + 2)
                for t in range(lo, hi):
                    ins = nc.vector.scalar_tensor_tensor(long_[:, b], vpad[:, b, t:t + S], fir_l[:, t:t + 1], long_[:, b], ALU.mult, ALU.add)
                    if done and t == hi - 1:
                        ins.then_inc(long_done, 1)
                    else:
                        link(ins)

            dve.wait_ge(gates_in, 16 * 6)
            dve.wait_ge(temp_exp, 1)
            dve.wait_ge(masks_ready, 1)
            start_inverse(nc.vector, link, 1)
            split_x(0)
            for g in range(GROUPS):
                gate_logits(g)
                if g + 1 < GROUPS:
                    split_x(g + 1)
                square(g, 0)
                square(g, 1)
                if g >= 1:
                    masks(g - 1)
                if g >= 3:
                    triangles_times_beta(nc.vector, dve, g - 1)
                    times_beta(nc.vector, dve, g - 1)
                gate_sigmoids(g)
                normalise(g, 0)
                normalise(g, 1)
            masks(3)
            triangles_times_beta(nc.vector, dve, 3)
            times_beta(nc.vector, dve, 3)
            dve.wait_ge(gates_exp, GROUPS)
            logits = mixw[:].rearrange("p n (h j) -> p (n h) j", j=3)
            gs = gsum[:].rearrange("p n h -> p (n h)")
            nc.vector.tensor_scalar(keep_local[:], gates[:, :, 4:8], -1.0, 1.0, ALU.mult, ALU.add)
            link(nc.vector.tensor_reduce(gs, logits, AX.X, ALU.add))
            link(nc.vector.reciprocal(gs, gs))
            link(nc.vector.tensor_tensor(gs, gs, keep_local[:].rearrange("p n h -> p (n h)"), ALU.mult))
            nc.vector.tensor_tensor(logits, logits, gs.rearrange("p (a o) -> p a o", o=1).broadcast_to([P, 4 * NT, 3]),
                                    ALU.mult).then_inc(mix_done, 1)
            invert(nc.vector, dve, link, 1)

            def transitions(b):
                view = "p (n a e) -> p n a e"
                dve.wait_ge(mg_psum, b + 1)
                for c in range(4):
                    src = ps[:, c, :].rearrange(view, n=8, a=2)
                    last = nc.vector.tensor_tensor(mt[:, b, c], eye32[:].rearrange("p (o e) -> p o e", o=1).broadcast_to([P, 8, C]),
                                                   src[:, :, 0, :], ALU.subtract)
                last.then_inc(m_ready, 1)
                for c in range(4):
                    src = ps[:, c, :].rearrange(view, n=8, a=2)
                    q = qs[:, S * b:S * b + S].rearrange("p (n c t) -> p c n t", n=8, c=4)[:, c]
                    last = nc.vector.tensor_tensor(q, q, src[:, :, 1, :], ALU.subtract)
                last.then_inc(g_ready, 1)

            fir(0, FIR_PE, FIR_PE + 4)
            transitions(0)
            fir(0, FIR_PE + 4, FIR_PE + 9)
            transitions(1)
            fir(0, FIR_PE + 9, FIRL, done=True)
            fir(1, FIR_PE, FIRL, done=True)

            def local(g, i):
                n4 = slice(4 * g, 4 * g + 4)
                k = 2 * FINAL.index(g) + i
                dve.wait_ge(local_psum, k + 1)
                if i == 1:
                    tmp = tapped[:, GT:2 * GT]
                else:
                    tmp = tapped[:, 0:GT]
                if k >= 2:
                    dve.wait_ge(local_ready, k // 2)
                nc.vector.tensor_tensor(heads(tmp), heads(ps[:, 2 + i, :]), per_head(mixw[:, n4, 1 + i:12:3]), ALU.mult).then_inc(local_used, 1)

            def blend_global(i):
                g = FINAL[i]
                dve.wait_ge(o_psum, 1)
                nc.vector.tensor_tensor(heads(blend[:, g, :]), ps[:, 4:8, P * g:P * g + P].rearrange("p h (n e) -> p n h e", e=C), per_head(gates[:, 4 * g:4 * g + 4, 4:8]), ALU.mult).then_inc(dve_step, 1)
                link.n += 1
                dve.wait_ge(dve_step, link.n)
                dve.wait_ge(local_ready, i + 1)
                nc.vector.tensor_tensor(blend[:, g, :], blend[:, g, :], vtok[:, 4 * g:4 * g + 4, :].rearrange("p n d -> p (n d)"), ALU.add).then_inc(blended, 1)

            def sum_squares(i):
                g = FINAL[i]
                dve.wait_ge(osq_ready, i + 1)
                nc.vector.tensor_reduce(oss[:, g, :], osq[:, i % 2, :].rearrange("p (a e) -> p a e", e=C), AX.X, ALU.add).then_inc(oss_ready, 1)

            def scale_o(i):
                g = FINAL[i]
                dve.wait_ge(ors_ready, i + 1)
                b3 = blend[:, g, :].rearrange("p (a e) -> p a e", e=C)
                nc.vector.tensor_tensor(b3, b3, ors[:, g, :].rearrange("p (a o) -> p a o", o=1).broadcast_to([P, 16, C]), ALU.mult).then_inc(o_scaled, 1)

            def residual(i):
                g = FINAL[i]
                dve.wait_ge(y_psum, i + 1)
                x4 = X[:, 4 * g:4 * g + 4, :].rearrange("p n d -> p (n d)")
                link(nc.vector.tensor_tensor(x4, x4, ps[:, i % 2, :], ALU.add))
                for n in range(4):
                    last = nc.vector.bn_stats(st63[:, g, n, :], X[:, 4 * g + n, :])
                link(last)
                for n in range(4):
                    last = nc.vector.bn_aggr(mv3[:, g, n, :], st63[:, g, n, :])
                last.then_inc(stats_ready, 1)

            def last_norm(i):
                g = FINAL[i]
                dve.wait_ge(rstd_ready, i + 1)
                for n in range(4):
                    tile = X[:, 4 * g + n, :]
                    last = nc.vector.tensor_scalar(tile, tile, mv3[:, g, n, 0:1], rs3[:, g, n:n + 1], ALU.subtract, ALU.mult)
                last.then_inc(x3_ready, 1)

            dve.wait_ge(short_done, B)
            for g in FINAL:
                local(g, 0)
                local(g, 1)
            blend_global(0)
            blend_global(1)
            for i in range(GROUPS):
                sum_squares(i)
                if i + 2 < GROUPS:
                    blend_global(i + 2)
                scale_o(i)
                if i >= 1:
                    residual(i - 1)
            residual(GROUPS - 1)
            for i in range(GROUPS):
                last_norm(i)

        @block.gpsimd
        def _(pool):
            link = Chain(pool, pool_step)
            link(nc.gpsimd.memset(xf[:, 0:2 * (CONV - 1)], 0.0))
            for b in range(B):
                link(nc.gpsimd.tensor_copy(x_hi[:, b, 0:CONV - 1], xf[:, 0:CONV - 1]))
                link(nc.gpsimd.tensor_copy(x_lo[:, b, 0:CONV - 1], xf[:, 0:CONV - 1]))
            nc.gpsimd.memset(vpad[:, :, 0:FIRL - 1], 0.0).then_inc(padded, 1)

            for i, (_, arrived) in enumerate(CONVS):
                pool.wait_ge(arrived, 32)
                if i:
                    pool.wait_ge(wc_ready, 2 * i)
                taps = tap_rows[:, i, :].rearrange("p (c k) -> p k c", k=CONV)
                for k in range(CONV):
                    last = nc.gpsimd.tensor_tensor(wc_full[:, k, :], wqkv[:, i, :], taps[:, k, :], ALU.mult)
                last.then_inc(wc_full_ready, 1)
                pool.wait_ge(wc_full_ready, i + 1)
                nc.gpsimd.tensor_copy(wc_hi[:, i], wc_full).then_inc(wc_ready, 1)
                pool.wait_ge(wc_ready, 2 * i + 1)
                nc.gpsimd.tensor_tensor(wc_lo[:, i], wc_full, wc_hi[:, i].bitcast(F32), ALU.subtract).then_inc(wc_ready, 1)
                if i == 0:
                    link(nc.gpsimd.memset(head_ones[:], 0.0))
                    link(nc.gpsimd.memset(low_mask[:], 1.0))
                    link(nc.gpsimd.memset(up_mask[:], 1.0))
                    for h in range(4):
                        q = slice(32 * h, 32 * h + 32)
                        link(nc.gpsimd.memset(head_ones[q, q], 1.0))
                        link(nc.gpsimd.tensor_copy(eye32[q, :], ident[q, q]))
                        link(nc.gpsimd.affine_select(out=low_mask[q, :], in_=low_mask[q, :], compare_op=ALU.is_gt, fill=0.0, base=0,
                                                     pattern=[[-1, C]], channel_multiplier=1))
                        link(nc.gpsimd.affine_select(out=up_mask[q, :], in_=up_mask[q, :], compare_op=ALU.is_ge, fill=0.0, base=0,
                                                     pattern=[[1, C]], channel_multiplier=-1))
                    nc.gpsimd.memset(state[:, 0], 0.0).then_inc(masks_ready, 1)
            start_inverse(nc.gpsimd, link, 0)
            for g in range(2):
                pool.wait_ge(beta_ready, g + 1)
                times_beta(nc.gpsimd, pool, g)
                triangles_times_beta(nc.gpsimd, pool, g)
            pool.wait_ge(rest_in, 16 * 7)
            nc.gpsimd.tensor_scalar(wo1[:], wo1[:], rmsw[:, 0:1], None, ALU.mult).then_inc(wo_scaled, 1)
            for t in range(FIR_PE):
                last = nc.gpsimd.tensor_scalar(fir_diag[:, t, :], ident[:], fir_l[:, t:t + 1], None, ALU.mult)
            last.then_inc(diag_ready, 1)
            invert(nc.gpsimd, pool, link, 0)
            for b in range(B):
                pool.wait_ge(silu_done, 6 * b + 6)
                for t in range(FIRS):
                    pool.wait_ge(ss_psum, 2 * GROUPS)
                    src = vpad[:, b, FIRL - FIRS + t:FIRL - FIRS + t + S]
                    tap = fir_s[:, t:t + 1].broadcast_to([P, S])
                    if t == 0:
                        link(nc.gpsimd.tensor_tensor(short[:, b], src, tap, ALU.mult))
                        continue
                    link(nc.gpsimd.tensor_tensor(tapped, src, tap, ALU.mult))
                    ins = nc.gpsimd.tensor_tensor(short[:, b], short[:, b], tapped, ALU.add)
                    if t < FIRS - 1:
                        link(ins)
                    else:
                        ins.then_inc(short_done, 1)
                        pool.wait_ge(short_done, b + 1)
            pool.wait_ge(mix_done, 1)
            for g in FINAL:
                last = nc.gpsimd.tensor_tensor(vtok[:, 4 * g:4 * g + 4, :].rearrange("p n (h e) -> p n h e", h=4),
                                               vtok[:, 4 * g:4 * g + 4, :].rearrange("p n (h e) -> p n h e", h=4),
                                               per_head(mixw[:, 4 * g:4 * g + 4, 0:12:3]), ALU.mult)
            link(last)
            for i, g in enumerate(FINAL):
                v4 = vtok[:, 4 * g:4 * g + 4, :].rearrange("p n d -> p (n d)")
                pool.wait_ge(local_used, 2 * i + 1)
                link(nc.gpsimd.tensor_tensor(v4, v4, tapped[:, 0:GT], ALU.add))
                pool.wait_ge(local_used, 2 * i + 2)
                nc.gpsimd.tensor_tensor(v4, v4, tapped[:, GT:2 * GT], ALU.add).then_inc(local_ready, 1)

            def rstd(i):
                g = FINAL[i]
                pool.wait_ge(stats_ready, i + 1)
                link(nc.gpsimd.tensor_scalar(rs3[:, g, :], mv3[:, g, :, 1], LN_EPS, None, ALU.add))
                nc.gpsimd.tensor_tensor(rs3[:, g, :], rs3[:, g, :], neg_half[:, 0:4], ALU.pow).then_inc(rstd_ready, 1)

            for i in range(GROUPS):
                g = FINAL[i]
                pool.wait_ge(oss_ready, i + 1)
                link(nc.gpsimd.tensor_scalar(ors[:, g, :], oss[:, g, :], 1.0 / C, LN_EPS, ALU.mult, ALU.add))
                nc.gpsimd.tensor_tensor(ors[:, g, :], ors[:, g, :], neg_half[:], ALU.pow).then_inc(ors_ready, 1)
                if i >= 2:
                    rstd(i - 2)
            rstd(GROUPS - 2)
            rstd(GROUPS - 1)

        @block.scalar
        def _(act):
            act.wait_ge(gates_in, 16 * 6)
            nc.scalar.activation(temp[:], temp[:], ACT.Exp, scale=-1.0).then_inc(temp_exp, 1)
            act.wait_ge(padded, 1)

            def load_x(g):
                act.wait_ge(xT_psum, g + 1)
                if g >= 1:
                    act.wait_ge(gates_psum, g)
                nc.scalar.copy(xf[:], ps[:, 0, :]).then_inc(xf_ready, 1)
                cols = slice(CONV - 1 + GT * (g % 2), CONV - 1 + GT * (g % 2) + GT)
                nc.scalar.copy(x_hi[:, g // 2, cols], ps[:, 0, :]).then_inc(xhi_ready, 1)

            def norms(g, i):
                act.wait_ge(ss_psum, 2 * g + i + 1)
                if g >= 1:
                    act.wait_ge(normed, 2 * g - 1 + i)
                nc.scalar.activation(rn[:, i, :], ps[:, (3, 2)[i], :], ACT.Ln, bias=eps_l2[:, 0:1]).then_inc(ln_done, 1)
                act.wait_ge(ln_done, 2 * g + i + 1)
                nc.scalar.activation(rn[:, i, :], rn[:, i, :], ACT.Exp, scale=-0.5).then_inc(rn_ready, 1)

            def vtok_copy(g):
                act.wait_ge(vtok_psum, g + 1)
                nc.scalar.copy(vtok[:, 4 * g:4 * g + 4, :].rearrange("p n d -> p (n d)"), ps[:, 0, :]).then_inc(vtok_ready, 1)

            def ktok_copy(g):
                act.wait_ge(ktok_psum, g + 1)
                nc.scalar.copy(ka[:, 4 * g:4 * g + 4, :, 0, :], heads(ps[:, 0, :])).then_inc(ktok_ready, 1)

            load_x(0)
            for g in range(GROUPS):
                for i in range(3):
                    act.wait_ge(conv_psum, 3 * g + i + 1)
                    dst = (rows(ks, g), rows(qs, g), v_rows(g))[i]
                    nc.scalar.activation(dst, ps[:, (1, 2, 1)[i], :], ACT.Silu).then_inc(silu_done, 1)
                    if i == 0 and g + 1 < GROUPS:
                        load_x(g + 1)
                    if i == 1 and g >= 1:
                        vtok_copy(g - 1)
                if g >= 1:
                    ktok_copy(g - 1)
                act.wait_ge(gates_biased, g + 1)
                nc.scalar.preload_act_table_set("natural_log_exp_and_others")
                nc.scalar.activation(gates[:, 4 * g:4 * g + 4, :], gates[:, 4 * g:4 * g + 4, :], ACT.Exp, scale=-1.0)
                nc.scalar.activation(mixw[:, 4 * g:4 * g + 4, :], mixw[:, 4 * g:4 * g + 4, :], ACT.Exp).then_inc(gates_exp, 1)
                norms(g, 0)
                norms(g, 1)
            vtok_copy(GROUPS - 1)
            ktok_copy(GROUPS - 1)
            for g in range(GROUPS):
                act.wait_ge(fir_psum, g + 1)
                nc.scalar.copy(long_[:, g // 2, GT * (g % 2):GT * (g % 2) + GT], ps[:, g, :]).then_inc(fir_begun, 1)
            for b in range(B):
                act.wait_ge(uw_psum, b + 1)
                for k in range(4):
                    last = nc.scalar.copy(inv_flat[:, b].rearrange("p i e -> p (i e)")[:, 512 * k:512 * k + 512], ps[:, 4 + k, :])
                last.then_inc(uw_ready, 1)
                act.wait_ge(b_psum, b + 1)
                for c in range(4):
                    last = nc.scalar.copy(bc[:, b, c].rearrange("p n e -> p (n e)"), ps[:, 4 + c, 0:256])
                last.then_inc(b_ready, 1)
            for j in range(32):
                act.wait_ge(state_psum, j + 1)
                nc.scalar.copy(state[:, j + 1], ps[:, j % 2, 0:B * C].rearrange("p (b e) -> p b e", b=B)).then_inc(state_ready, 1)

            def squares(i):
                act.wait_ge(blended, i + 1)
                if i >= 2:
                    act.wait_ge(oss_ready, i - 1)
                nc.scalar.activation(osq[:, i % 2, :], blend[:, FINAL[i], :], ACT.Square).then_inc(osq_ready, 1)

            squares(0)
            squares(1)
            for i in range(GROUPS):
                act.wait_ge(oT_psum, i + 1)
                if i >= 2:
                    act.wait_ge(y_psum, i - 1)
                nc.scalar.copy(oT[:, i % 2, :], ps[:, 2 + i % 2, :]).then_inc(oT_ready, 1)
                if i + 2 < GROUPS:
                    squares(i + 2)

        @block.tensor
        def _(pe):
            def transposes(g):
                if g >= 3:
                    pe.wait_ge(ktok_ready, g - 2)
                for n in range(4):
                    last = nc.tensor.transpose(ps[:, 0, P * n:P * n + P], X[:, 4 * g + n, :], ident[:])
                last.then_inc(xT_psum, 1)

            def conv(g, i):
                if g == 0:
                    pe.wait_ge(wc_ready, 2 * i + 2)
                if i == 0 and g >= 1:
                    pe.wait_ge(silu_done, 3 * g)
                if i == 1 and g >= 1:
                    pe.wait_ge(ln_done, 2 * g)
                if i == 2:
                    pe.wait_ge(silu_done, 3 * g + 1)
                bank = ps[:, (1, 2, 1)[i], :]
                for t in range(CONV):
                    cols = slice(GT * (g % 2) + t, GT * (g % 2) + t + GT)
                    xh, xl = x_hi[:, g // 2, cols], x_lo[:, g // 2, cols]
                    nc.tensor.matmul(bank, wc_lo[:, i, t, :], xh, start=(t == 0), stop=False)
                    nc.tensor.matmul(bank, wc_hi[:, i, t, :], xl, start=False, stop=False)
                    last = nc.tensor.matmul(bank, wc_hi[:, i, t, :], xh, start=False, stop=(t == CONV - 1))
                last.then_inc(conv_psum, 1)

            def gate_products(g):
                pe.wait_ge(xf_ready, g + 1)
                if g >= 1:
                    pe.wait_ge(ln_done, 2 * g - 1)
                for n in range(4):
                    last = nc.tensor.matmul(ps[:, 3, 20 * n:20 * n + 20], xf[:, P * n:P * n + P], wgates[:], start=True, stop=True)
                last.then_inc(gates_psum, 1)

            def sums(g, i):
                pe.wait_ge(sq_ready, 2 * g + i + 1)
                if i == 0:
                    pe.wait_ge(gates_biased, g + 1)
                else:
                    pe.wait_ge(silu_done, 3 * g + 2)
                nc.tensor.matmul(ps[:, (3, 2)[i], :], head_ones[:], sq[:, i, :], start=True, stop=True).then_inc(ss_psum, 1)

            def v_to_tokens(g):
                pe.wait_ge(silu_done, 3 * g + 3)
                for loaded in (xf_ready, xhi_ready, xlo_ready):
                    pe.wait_ge(loaded, min(g + 3, GROUPS))
                if g == GROUPS - 1:
                    pe.wait_ge(ktok_ready, g)
                for n in range(4):
                    t = 4 * g + n
                    off = FIRL - 1 + P * (t % 8)
                    last = nc.tensor.transpose(ps[:, 0, P * n:P * n + P], vpad[:, t // 8, off:off + P], ident[:])
                last.then_inc(vtok_psum, 1)

            def k_to_tokens(g):
                pe.wait_ge(normed, 2 * g + 1)
                pe.wait_ge(vtok_ready, g + 1)
                for n in range(4):
                    t = 4 * g + n
                    last = nc.tensor.transpose(ps[:, 0, P * n:P * n + P], ks[:, P * t:P * t + P], ident[:])
                last.then_inc(ktok_psum, 1)

            def chunk(n, c):
                t0 = P * n + C * c
                return slice(t0, t0 + C)

            def triangles(g):
                pe.wait_ge(normed, 2 * g + 2)
                if g >= 1:
                    pe.wait_ge(tri_masked, g)
                    pe.wait_ge(att_ready, g)
                for other, col in ((ks, 0), (qs, 128)):
                    for n in range(4):
                        for h in range(4):
                            f = slice(32 * h, 32 * h + 32)
                            for c in range(4):
                                o = col + 32 * n
                                last = nc.tensor.matmul(ps[32 * c:32 * c + 32, 4 + h, o:o + 32], ks[f, chunk(4 * g + n, c)],
                                                        other[f, chunk(4 * g + n, c)], start=True, stop=True)
                last.then_inc(tri_psum, 1)

            pe.wait_ge(gates_in, 16 * 6)
            transposes(0)
            pe.wait_ge(padded, 1)
            pe.wait_ge(masks_ready, 1)
            for g in range(GROUPS):
                pe.wait_ge(xhi_ready, g + 1)
                pe.wait_ge(xlo_ready, g + 1)
                conv(g, 0)
                gate_products(g)
                if g + 1 < GROUPS:
                    transposes(g + 1)
                conv(g, 1)
                if g >= 1:
                    v_to_tokens(g - 1)
                sums(g, 0)
                if g >= 1:
                    triangles(g - 1)
                conv(g, 2)
                if g >= 1:
                    k_to_tokens(g - 1)
                sums(g, 1)
            v_to_tokens(GROUPS - 1)
            triangles(GROUPS - 1)
            k_to_tokens(GROUPS - 1)
            pe.wait_ge(diag_ready, 1)
            pe.wait_ge(ktok_ready, GROUPS)
            pe.wait_ge(ln_done, 2 * GROUPS)
            for g in range(GROUPS):
                off = GT * (g % 2)
                for t in range(FIR_PE):
                    last = nc.tensor.matmul(ps[:, g, :], fir_diag[:, t, :], vpad[:, g // 2, off + t:off + t + GT], start=(t == 0), stop=(t == FIR_PE - 1))
                last.then_inc(fir_psum, 1)

            def per_chunk(cols, lhs, rhs, place):
                for n in range(8):
                    for c in range(4):
                        for h in range(4):
                            r = slice(32 * c, 32 * c + 32)
                            bank, o = place(n, c)
                            last = nc.tensor.matmul(ps[32 * h:32 * h + 32, bank, o:o + cols], lhs(r, n, h), rhs(r, n, h), start=True, stop=True)
                return last

            pe.wait_ge(att_ready, GROUPS)
            pe.wait_ge(ktok_ready, GROUPS)
            pe.wait_ge(ln_done, 2 * GROUPS)
            for b in range(B):
                pe.wait_ge(inv_in[b], 16)
                pe.wait_ge(vb_ready, 2 * (b + 1))
                pe.wait_ge(kb_ready, 2 * (b + 1))
                if b:
                    pe.wait_ge(b_ready, b)
                for n in range(8):
                    for h in range(4):
                        for c in range(4):
                            r = slice(32 * c, 32 * c + 32)
                            last = nc.tensor.matmul(ps[r, 4 + n // 2, (4 * (n % 2) + h) * 64:(4 * (n % 2) + h) * 64 + 64],
                                                    tT[r, b, 8 * h + n, :], vk[r, 8 * b + n, h].rearrange("p a e -> p (a e)"),
                                                    start=True, stop=True)
                last.then_inc(uw_psum, 1)
                pe.wait_ge(uw_ready, b + 1)
                if b == 0:
                    pe.wait_ge(fir_begun, GROUPS)
                else:
                    pe.wait_ge(g_ready, b)
                    pe.wait_ge(m_ready, b)
                per_chunk(64, lambda r, n, h: uw(b, r, n, h)[:, 32:64], lambda r, n, h: ka[r, 8 * b + n, h].rearrange("p a e -> p (a e)"),
                          lambda n, c: (c, 64 * n)).then_inc(mg_psum, 1)
                per_chunk(32, lambda r, n, h: ka[r, 8 * b + n, h, 0, :], lambda r, n, h: uw(b, r, n, h)[:, 0:32],
                          lambda n, c: (4 + c, 32 * n)).then_inc(b_psum, 1)
            pe.wait_ge(b_ready, B)

            def o_region(b, n, c, h):
                t = 8 * b + n
                return ps[32 * c:32 * c + 32, 4 + h, C * t:C * t + C]

            for b in range(B):
                for n in range(8):
                    for h in range(4):
                        for c in range(4):
                            r = slice(32 * c, 32 * c + 32)
                            last = nc.tensor.matmul(o_region(b, n, c, h), ka[r, 8 * b + n, h, 1, :], uw(b, r, n, h)[:, 0:32],
                                                    start=(b == 0 and n == 0), stop=False, skip_group_check=True)
            last.then_inc(o_begun, 1)
            pe.wait_ge(o_begun, 1)

            def input_term(j):
                nc.tensor.matmul(ps[:, j % 2, 0:B * C].rearrange("p (b e) -> p b e", b=B), ident[:], bc[:, :, j % 4, j // 4, :], start=True, stop=False,
                                 skip_group_check=True)

            pe.wait_ge(m_ready, B)
            pe.wait_ge(g_ready, B)
            input_term(0)
            for j in range(32):
                n, c = j // 4, j % 4
                if j >= 1:
                    pe.wait_ge(state_ready, j)
                for b in range(B):
                    for h in range(4):
                        f = slice(32 * h, 32 * h + 32)
                        last = nc.tensor.matmul(ps[f, j % 2, C * b:C * b + C], mt[f, b, c, n, :], state[f, j, b, :], start=False, stop=True,
                                                skip_group_check=True)
                last.then_inc(state_psum, 1)
                for b in range(B):
                    for h in range(4):
                        f = slice(32 * h, 32 * h + 32)
                        last = nc.tensor.matmul(o_region(b, n, c, h), gT[f, chunk(8 * b + n, c)], state[f, j, b, :], start=False, stop=True,
                                                skip_group_check=True)
                if j == 31:
                    last.then_inc(o_psum, 1)
                if j + 1 < 32:
                    input_term(j + 1)

            for k in range(8):
                i, g = k % 2, FINAL[k // 2]
                b = g // 2
                pe.wait_ge((short_done, long_done)[i], b + 1)
                if k >= 2:
                    pe.wait_ge(local_used, k - 1)
                for n in range(4):
                    off = GT * (g % 2) + P * n
                    last = nc.tensor.transpose(ps[:, 2 + i, P * n:P * n + P], (short, long_)[i][:, b, off:off + P], ident[:])
                last.then_inc(local_psum, 1)
            pe.wait_ge(wo_scaled, 1)
            pe.wait_ge(local_used, 8)

            def project(i):
                g = FINAL[i]
                pe.wait_ge(oT_ready, i + 1)
                if i >= 2:
                    pe.wait_ge(stats_ready, i - 1)
                else:
                    pe.wait_ge(state_ready, 31 + i)
                for n in range(4):
                    last = nc.tensor.matmul(ps[:, i % 2, P * n:P * n + P], oT[:, i % 2, P * n:P * n + P], wo1[:], start=True, stop=True)
                last.then_inc(y_psum, 1)

            for i in range(GROUPS):
                g = FINAL[i]
                pe.wait_ge(o_scaled, i + 1)
                if i >= 2:
                    pe.wait_ge(oT_ready, i - 1)
                for n in range(4):
                    last = nc.tensor.transpose(ps[:, 2 + i % 2, P * n:P * n + P], blend[:, g, P * n:P * n + P], ident[:])
                last.then_inc(oT_psum, 1)
                if i >= 1:
                    project(i - 1)
            project(GROUPS - 1)
    sub.close()
    sub = ExitStack()

    def sb5(name, shape, dt=F32):
        return sub.enter_context(nc.sbuf_tensor(name, shape, dt))

    k0, k1, k2 = sb5("k0", [P, 2, FH], U8), sb5("k1", [P, FB, FH], U8), sb5("k2", [P, FB, D], U8)
    sw0, sw1, sw2 = sb5("sw0", [P, FH], F32R), sb5("sw1", [P, FB, FH], F32R), sb5("sw2", [P, FB, D], F32R)
    s_in, s_out = sb5("s_in", [P, 3]), sb5("s_out", [P, 3])
    xt_hi, xt_lo = sb5("xt_hi5", [P, GT], F32R), sb5("xt_lo5", [P, GT], F32R)
    hf = sb5("hf5", [P, FB, GT])
    h_hi, h_lo = sb5("h_hi5", [P, 2, FB, GT], F32R), sb5("h_lo5", [P, 2, FB, GT], F32R)
    mv4, st64, rs4 = sb5("mv4", [P, GROUPS, 4, 2]), sb5("st64", [P, GROUPS, 4, 6]), sb5("rs4", [P, GROUPS, 4])

    with nc.Block() as block:
        k_in, scales_in = [sem(f"signs_in{i}") for i in range(3)], sem("signs_scales_in")
        first_signs, signs_ready, scales_ready = sem("first_signs"), sem("signs_ready"), sem("signs_scales_ready")
        xT_psum, xT_hi, xT_lo = sem("x3T_psum"), sem("x3T_hi"), sem("x3T_lo")
        hid_psum, relu_done = sem("hid5_psum"), sem("relu_done")
        hi_ready, lo_ready = sem("h5_hi_ready"), sem("h5_lo_ready")
        y_psum = sem("y5_psum")
        stats_ready, rstd_ready, out_ready, stored = sem("ln4_stats"), sem("ln4_rstd"), sem("out_ready"), sem("stored")
        dve_step, pool_step = sem("dve_step5"), sem("pool_step5")

        @block.sync
        def _(sp):
            sp.dma_start(k0[:], dr["L1_ffn_k0"].rearrange("(a p) n -> p a n", p=P)).then_inc(k_in[0], 16)
            sp.dma_start(k1[:], dr["L1_ffn_k1"].rearrange("(a p) n -> p a n", p=P)).then_inc(k_in[1], 16)
            sp.dma_start(k2[:], dr["L1_ffn_k2"].rearrange("(a p) n -> p a n", p=P)).then_inc(k_in[2], 16)
            for i in range(3):
                sp.dma_start(s_in[:, i:i + 1], dr[f"L1_ffn_s{i}"].rearrange("(o n) -> o n", o=1).broadcast_to([P, 1])).then_inc(scales_in, 16)
            out_tiles = out_dram.rearrange("(n p) d -> p n d", p=P)
            for g in range(GROUPS):
                sp.wait_ge(out_ready, g + 1)
                sp.dma_start(out_tiles[:, 4 * g:4 * g + 4, :], X[:, 4 * g:4 * g + 4, :]).then_inc(stored, 16)
            sp.wait_ge(stored, 16 * GROUPS)

        @block.scalar
        def _(act):
            def transposed(g):
                act.wait_ge(xT_psum, g + 1)
                nc.scalar.copy(xt_hi[:], ps[:, 1, :]).then_inc(xT_hi, 1)

            transposed(0)
            act.wait_ge(scales_ready, 1)
            for g in range(GROUPS):
                for layer in range(2):
                    for o in range(FB):
                        act.wait_ge(hid_psum, 8 * g + 4 * layer + o + 1)
                        if g >= 1 or layer == 1:
                            act.wait_ge(lo_ready, 8 * g + 4 * (layer - 1) + o + 1)
                        nc.scalar.activation(hf[:, o, :], ps[:, 4 * layer + o, :], ACT.Relu, scale=s_out[:, layer:layer + 1]).then_inc(relu_done, 1)
                if g + 1 < GROUPS:
                    transposed(g + 1)

        @block.gpsimd
        def _(pool):
            link = Chain(pool, pool_step)
            pool.wait_ge(k_in[1], 16)
            nc.gpsimd.tensor_scalar(sw1[:], k1[:], 2.0, -1.0, ALU.mult, ALU.add).then_inc(signs_ready, 1)
            pool.wait_ge(k_in[2], 16)
            nc.gpsimd.tensor_scalar(sw2[:], k2[:], 2.0, -1.0, ALU.mult, ALU.add).then_inc(signs_ready, 1)

            def rstd(g):
                pool.wait_ge(stats_ready, g + 1)
                link(nc.gpsimd.tensor_scalar(rs4[:, g, :], mv4[:, g, :, 1], LN_EPS, None, ALU.add))
                nc.gpsimd.tensor_tensor(rs4[:, g, :], rs4[:, g, :], neg_half[:, 0:4], ALU.pow).then_inc(rstd_ready, 1)

            for g in range(GROUPS):
                for layer in range(2):
                    for o in range(FB):
                        pool.wait_ge(hi_ready, 8 * g + 4 * layer + o + 1)
                        nc.gpsimd.tensor_tensor(h_lo[:, layer, o, :], hf[:, o, :], h_hi[:, layer, o, :].bitcast(F32), ALU.subtract).then_inc(lo_ready, 1)
                    if layer == 0 and g >= 1:
                        rstd(g - 1)
            rstd(GROUPS - 1)

        @block.vector
        def _(dve):
            link = Chain(dve, dve_step)

            def transposed(g):
                dve.wait_ge(xT_hi, g + 1)
                nc.vector.tensor_tensor(xt_lo[:], ps[:, 1, :], xt_hi[:].bitcast(F32), ALU.subtract).then_inc(xT_lo, 1)

            def normalise(g):
                dve.wait_ge(rstd_ready, g + 1)
                for n in range(4):
                    tile = X[:, 4 * g + n, :]
                    last = nc.vector.tensor_scalar(tile, tile, mv4[:, g, n, 0:1], rs4[:, g, n:n + 1], ALU.subtract, ALU.mult)
                last.then_inc(out_ready, 1)

            dve.wait_ge(k_in[0], 16)
            nc.vector.tensor_tensor(sw0[:], k0[:, 0, :], k0[:, 1, :], ALU.subtract).then_inc(first_signs, 1)
            dve.wait_ge(scales_in, 48)
            nc.vector.tensor_scalar(s_out[:, 0:1], s_in[:, 0:1], 4.0, None, ALU.mult)
            nc.vector.tensor_scalar(s_out[:, 1:2], s_in[:, 1:2], 2.0, None, ALU.mult).then_inc(scales_ready, 1)
            transposed(0)
            for g in range(GROUPS):
                for layer in range(2):
                    for o in range(FB):
                        dve.wait_ge(relu_done, 8 * g + 4 * layer + o + 1)
                        nc.vector.tensor_copy(h_hi[:, layer, o, :], hf[:, o, :]).then_inc(hi_ready, 1)
                    if layer == 0 and g >= 1:
                        normalise(g - 1)
                if g + 1 < GROUPS:
                    transposed(g + 1)
                dve.wait_ge(y_psum, g + 1)
                x4 = X[:, 4 * g:4 * g + 4, :].rearrange("p n d -> p (n d)")
                link(nc.vector.scalar_tensor_tensor(x4, ps[:, 0, :], s_in[:, 2:3], x4, ALU.mult, ALU.add))
                for n in range(4):
                    last = nc.vector.bn_stats(st64[:, g, n, :], X[:, 4 * g + n, :])
                link(last)
                for n in range(4):
                    last = nc.vector.bn_aggr(mv4[:, g, n, :], st64[:, g, n, :])
                last.then_inc(stats_ready, 1)
            normalise(GROUPS - 1)

        @block.tensor
        def _(pe):
            def transposes(g):
                if g >= 1:
                    pe.wait_ge(relu_done, 8 * g - 4)
                for n in range(4):
                    last = nc.tensor.transpose(ps[:, 1, P * n:P * n + P], X[:, 4 * g + n, :], ident[:])
                last.then_inc(xT_psum, 1)

            transposes(0)
            for g in range(GROUPS):
                pe.wait_ge(xT_hi, g + 1)
                pe.wait_ge(xT_lo, g + 1)
                pe.wait_ge(first_signs, 1)
                if g >= 1:
                    pe.wait_ge(stats_ready, g)
                for o in range(FB):
                    w = sw0[:, P * o:P * o + P]
                    nc.tensor.matmul(ps[:, o, :], w, xt_lo[:], start=True, stop=False)
                    nc.tensor.matmul(ps[:, o, :], w, xt_hi[:], start=False, stop=True).then_inc(hid_psum, 1)
                pe.wait_ge(signs_ready, 1)
                for k in range(FB):
                    pe.wait_ge(lo_ready, 8 * g + k + 1)
                    for o in range(FB):
                        if k == 0 and g >= 1:
                            pe.wait_ge(relu_done, 8 * g - 4 + o + 1)
                        w = sw1[:, k, P * o:P * o + P]
                        nc.tensor.matmul(ps[:, 4 + o, :], w, h_lo[:, 0, k, :], start=(k == 0), stop=False)
                        last = nc.tensor.matmul(ps[:, 4 + o, :], w, h_hi[:, 0, k, :], start=False, stop=(k == FB - 1))
                        if k == FB - 1:
                            last.then_inc(hid_psum, 1)
                if g + 1 < GROUPS:
                    transposes(g + 1)
                pe.wait_ge(lo_ready, 8 * g + 8)
                pe.wait_ge(signs_ready, 2)
                for n in range(4):
                    tok = slice(P * n, P * n + P)
                    for k in range(FB):
                        nc.tensor.matmul(ps[:, 0, tok], h_lo[:, 1, k, tok], sw2[:, k, :], start=(k == 0), stop=False)
                        last = nc.tensor.matmul(ps[:, 0, tok], h_hi[:, 1, k, tok], sw2[:, k, :], start=False, stop=(k == FB - 1))
                last.then_inc(y_psum, 1)
    sub.close()


def kernel(**inputs):
    import numpy as _np
    import concourse.bacc as _bacc
    from concourse import mybir as _mybir
    from concourse.bass_utils import run_bass_kernel_spmd as _run

    arrays = {}
    for name, a in inputs.items():
        a = _np.asarray(a)
        if name in ("L0_attn_x",):
            a = a.reshape(-1, a.shape[-1])
        elif name.startswith("L0_ffn") and name.endswith("_w"):
            a = a.T
        elif name.startswith("L0_ffn") and name.endswith("_s") and a.size > 128:
            a = a.reshape(-1, 128).T
        elif a.ndim == 0:
            a = a.reshape(1)
        arrays[name] = _np.ascontiguousarray(a)
    nc = _bacc.Bacc("TRN2", target_bir_lowering=False, num_devices=1)
    dr = {n: nc.dram_tensor(n, a.shape, _mybir.dt.from_np(a.dtype), kind="ExternalInput").ap() for n, a in arrays.items()}
    out = nc.dram_tensor("out", (B * S, D), _mybir.dt.float32, kind="ExternalOutput").ap()
    build(nc, dr, out)
    r = _run(nc, [arrays], core_ids=[0])
    return r.results[0]["out"].reshape(B, S, D)
```

```python
import concourse.bass as bass
from concourse import mybir
from contextlib import ExitStack

F32, F32R, BF16, U8 = mybir.dt.float32, mybir.dt.float32r, mybir.dt.bfloat16, mybir.dt.uint8
ALU = mybir.AluOpType
ACT = mybir.ActivationFunctionType
AX = mybir.AxisListType

P = 128
D = 128
B, S = 2, 1024
NT = B * S // P
GT = 512
GROUPS = B * S // GT
H0 = 8
NH = B * H0
DK0 = D // H0
SCORE_SCALE = float(DK0) ** -0.5
FH = 512
FB = FH // P
LN_EPS = 1e-5
C = 32
CONV, FIRS, FIRL = 4, 3, 31


class Chain:

    def __init__(self, engine, semaphore, base=0):
        self.engine, self.semaphore, self.base, self.n = engine, semaphore, base, 0

    def __call__(self, instruction):
        self.n += 1
        instruction.then_inc(self.semaphore, 1)
        self.engine.wait_ge(self.semaphore, self.base + self.n)


def split3(engine, link, parts, src, rest, done):
    link(engine.tensor_copy(parts[:, 0], src[:]))
    link(engine.tensor_tensor(rest[:, 0], src[:], parts[:, 0], ALU.subtract))
    link(engine.tensor_copy(parts[:, 1], rest[:, 0]))
    link(engine.tensor_tensor(rest[:, 1], rest[:, 0], parts[:, 1], ALU.subtract))
    engine.tensor_copy(parts[:, 2], rest[:, 1]).then_inc(done, 1)


def build(nc, dr, out_dram):
    x_dram = dr["L0_attn_x"]
    q_scratch = nc.dram_tensor("q_scratch", (3, B, P, S), BF16, kind="Internal").ap()
    k_scratch = nc.dram_tensor("k_scratch", (3, B, P, S), BF16, kind="Internal").ap()

    with ExitStack() as ctx:
        program(nc, dr, out_dram, x_dram, q_scratch, k_scratch, ctx)


def program(nc, dr, out_dram, x_dram, q_scratch, k_scratch, ctx):
    def sb(name, shape, dt=F32):
        return ctx.enter_context(nc.sbuf_tensor(name, shape, dt))

    early = ExitStack()
    early_sems = []

    def sem(name):
        early_sems.append(early.enter_context(nc.semaphore(name)))
        return early_sems[-1]

    ps = ctx.enter_context(nc.psum_tensor("ps", [P, 8, 512], F32))
    X = sb("X", [P, NT, D])
    ident, ident_bf = sb("ident", [P, P]), sb("ident_bf", [P, P], BF16)
    neg_half = sb("neg_half", [P, 16])
    st6, mv, rs = sb("st6", [P, GROUPS, 4, 6]), sb("mv", [P, GROUPS, 4, 2]), sb("rs", [P, GROUPS, 4])
    xn = sb("xn", [P, 2, 4, P])
    eps_l2, eps_rms = sb("eps_l2", [P, 1]), sb("eps_rms", [P, 1])
    wqkv, wgates = sb("wqkv", [P, 3, P]), sb("wgates", [P, 20])
    prep = sb("prep", [P, 4 * P * CONV])
    tap_rows = prep[:, 0:3 * P * CONV].rearrange("p (i c) -> p i c", i=3)
    wc_full = prep[:, 3 * P * CONV:].rearrange("p (k c) -> p k c", k=CONV)
    bc = prep[:].rearrange("p (b c n e) -> p b c n e", b=B, c=4, n=8)
    wc_hi, wc_lo = sb("wc_hi", [P, 3, CONV, P], F32R), sb("wc_lo", [P, 3, CONV, P], F32R)
    gate_bias, temp = sb("gate_bias", [P, 16]), sb("temp", [P, 4])
    head_ones, eye32 = sb("head_ones", [P, P]), sb("eye32", [P, C])
    low_mask, up_mask = sb("low_mask", [P, C]), sb("up_mask", [P, C])
    w4_in, wc_full_ready, wc_ready = sem("w4_in"), sem("wc_full_ready"), sem("wc_ready")
    W4_LOADS = 12
    CONVS = "kqv"

    ffn_weights = ExitStack()

    def sbw(name, shape, dt=F32):
        return ffn_weights.enter_context(nc.sbuf_tensor(name, shape, dt))

    W1, W2, WH1, WH2, W3 = 0, FH, 2 * FH, 2 * FH + FB * FH, 2 * FH + 2 * FB * FH
    WCOLS = W3 + FB * D
    w_raw = sbw("w_raw", [P, WCOLS])
    w_hi, w_lo = sbw("w_hi", [P, WCOLS], F32R), sbw("w_lo", [P, WCOLS], F32R)
    ffn_scale = sbw("ffn_scale", [P, 4, FB])
    w3s = sbw("w3s", [P, 1])
    w_in, w_split = sem("ffn_w_in"), sem("ffn_w_split")
    W_LOADS = 10

    sub = ExitStack()

    def sb(name, shape, dt=F32):
        return sub.enter_context(nc.sbuf_tensor(name, shape, dt))

    wq, wk, wv = sb("wq", [P, P]), sb("wk", [P, P]), sb("wv", [P, H0 * D])
    bq, bk, gam, bet = sb("bq", [P, 1]), sb("bk", [P, 1]), sb("gam", [P, 1]), sb("bet", [P, 1])
    bv_rows, wv_sum, bv_sum = sb("bv_rows", [P, H0 * D]), sb("wv_sum", [P, P]), sb("bv_sum", [P, P])
    xnT = sb("xnT", [P, 2, GT])
    qf, kf = sb("qf", [P, GT]), sb("kf", [P, GT])
    q_rest, k_rest = sb("q_rest", [P, 2, GT]), sb("k_rest", [P, 2, GT])
    qsplit, ksplit = sb("qsplit", [P, 2, 3, GT], BF16), sb("ksplit", [P, 2, 3, GT], BF16)
    vp = sb("vp", [P, NH, 8, 32])
    fold_sel = sb("fold_sel", [P, 32])
    qst, kst = sb("qst", [P, 2, S], BF16), sb("kst", [P, 2, S], BF16)
    qm, km = sb("qm", [P, 2, S], BF16), sb("km", [P, 2, S], BF16)
    mx, nmax = sb("mx", [P, 2, 8]), sb("nmax", [P, 2, 8])
    shift3, shift_sb = sb("shift3", [P, 2, 24], BF16), sb("shift_sb", [P, 2, P], BF16)
    prob = sb("prob", [P, 16, 512])
    vst = sb("vst", [P, 2, 8, 32])
    ot = q_rest
    ot_by_m = ot[:].rearrange("p c t -> p (c t)").rearrange("p (r m) -> p m r", m=8)
    zeros8 = sb("zeros8", [P, 8])
    rsum, att = sb("rsum", [P, 8]), sb("att", [P, P])
    q_scr_h = q_scratch.rearrange("a b (h k) t -> a (b h) k t", k=DK0)
    k_scr_h = k_scratch.rearrange("a b (h k) t -> a (b h) k t", k=DK0)
    mx_in = [sem(f"mx_in{p}") for p in range(2)]
    splits_stored = [sem(f"splits_stored{g}") for g in range(GROUPS)]

    def load_max(sp, h, p):
        qh = q_scr_h[:, bass.ds(h, 1)]
        kh = k_scr_h[:, bass.ds(h, 1)]
        for r in (0, 64):
            sp.dma_start(qm[r:r + 32, p, :], qh[0:1].rearrange("a h k t -> (a h k) t").rearrange("(o k) t -> o k t", o=1).broadcast_to([2, 16, S])).then_inc(mx_in[p], 16)
            sp.dma_start(qm[r + 32:r + 48, p, :], qh[1:2].rearrange("a h k t -> (a h k) t")).then_inc(mx_in[p], 16)
            sp.dma_start(km[r:r + 32, p, :], kh[0:2].rearrange("a h k t -> a (h k) t")).then_inc(mx_in[p], 16)
            sp.dma_start(km[r + 32:r + 48, p, :], kh[0:1].rearrange("a h k t -> (a h k) t")).then_inc(mx_in[p], 16)

    with nc.Block() as block:
        x_in = [sem(f"x_in{g}") for g in range(GROUPS)]
        weights_in = sem("weights_in")
        ident_ready = sem("ident_ready")
        stats_ready = sem("stats_ready")
        rstd_ready = sem("rstd_ready")
        xn_ready = sem("xn_ready")
        xnT_psum = sem("xnT_psum")
        xnT_ready = sem("xnT_ready")
        wv_summed = sem("wv_summed")
        q_psum, k_psum, v_psum = sem("q_psum"), sem("k_psum"), sem("v_psum")
        q_ready, k_ready, v_ready = sem("q_ready"), sem("k_ready"), sem("v_ready")
        q_rounded, q_left, k_split = sem("q_rounded"), sem("q_left"), sem("k_split")
        dve_step, pool_step = sem("dve_step1"), sem("pool_step1")

        @block.sync
        def _(sp):
            xg = x_dram.rearrange("(n p) d -> p n d", p=P)
            for g in range(GROUPS):
                sp.dma_start(X[:, 4 * g:4 * g + 4, :], xg[:, 4 * g:4 * g + 4, :]).then_inc(x_in[g], 16)
            for g in range(GROUPS):
                b, cols = g // 2, slice(GT * (g % 2), GT * (g % 2) + GT)
                if g == GROUPS - 1:
                    sp.wait_ge(splits_stored[0], 2 * 16)
                    sp.wait_ge(splits_stored[1], 2 * 16)
                    load_max(sp, 0, 0)
                sp.wait_ge(q_rounded, 3 * g + 3)
                sp.dma_start(q_scratch[:, b, :, cols].rearrange("a p t -> p a t"), qsplit[:, g % 2]).then_inc(splits_stored[g], 16)
                sp.wait_ge(k_split, g + 1)
                sp.dma_start(k_scratch[:, b, :, cols].rearrange("a p t -> p a t"), ksplit[:, g % 2]).then_inc(splits_stored[g], 16)

        @block.scalar
        def _(act):
            for dst, src in ((wq, "Wq"), (wk, "Wk"), (wv, "Wv")):
                act.dma_start(dst[:], dr["L0_attn_" + src]).then_inc(weights_in, 16)
            for dst, src in ((bq, "bq"), (bk, "bk"), (gam, "gamma"), (bet, "beta")):
                act.dma_start(dst[:], dr["L0_attn_" + src].rearrange("(p o) -> p o", o=1)).then_inc(weights_in, 16)
            act.dma_start(bv_rows[:], dr["L0_attn_bv"].rearrange("(o n) -> o n", o=1).broadcast_to([P, H0 * D])).then_inc(weights_in, 16)
            act.wait_ge(weights_in, 8 * 16)

            def load_xnT(g):
                act.wait_ge(xnT_psum, g + 1)
                if g >= 2:
                    act.wait_ge(v_psum, g - 1)
                nc.scalar.activation(xnT[:, g % 2, :], ps[:, 0, :], ACT.Identity, scale=gam[:, 0:1], bias=bet[:, 0:1]).then_inc(xnT_ready, 1)

            load_xnT(0)
            for g in range(GROUPS):
                act.wait_ge(q_psum, g + 1)
                if g >= 1:
                    act.wait_ge(q_left, 2 * g)
                nc.scalar.activation(qf[:], ps[:, 1, :], ACT.Identity, bias=bq[:, 0:1]).then_inc(q_ready, 1)
                act.wait_ge(k_psum, g + 1)
                if g >= 1:
                    act.wait_ge(k_split, g)
                nc.scalar.activation(kf[:], ps[:, 2, :], ACT.Identity, bias=bk[:, 0:1]).then_inc(k_ready, 1)
                act.wait_ge(q_ready, g + 1)
                if g >= 2:
                    act.wait_ge(splits_stored[g - 2], 2 * 16)
                for i in range(3):
                    if i:
                        act.wait_ge(q_left, 2 * g + i)
                    nc.scalar.copy(qsplit[:, g % 2, i], qf[:] if i == 0 else q_rest[:, i - 1]).then_inc(q_rounded, 1)
                    if i == 0 and g + 1 < GROUPS:
                        load_xnT(g + 1)

        @block.gpsimd
        def _(pool):
            link = Chain(pool, pool_step)
            link(nc.gpsimd.memset(ident[:], 0.0))
            nc.gpsimd.affine_select(out=ident[:], in_=ident[:], compare_op=ALU.not_equal, fill=1.0, base=0,
                                    pattern=[[-1, P]], channel_multiplier=1).then_inc(ident_ready, 1)
            pool.wait_ge(ident_ready, 1)
            nc.gpsimd.tensor_copy(ident_bf[:], ident[:]).then_inc(ident_ready, 1)
            link(nc.gpsimd.memset(fold_sel[:], 0.0))
            for j in range(4):
                link(nc.gpsimd.affine_select(out=fold_sel[:], in_=fold_sel[:], compare_op=ALU.not_equal, fill=1.0,
                                             base=-32 * j, pattern=[[-1, 32]], channel_multiplier=1))
            link(nc.gpsimd.memset(neg_half[:], -0.5))
            link(nc.gpsimd.memset(zeros8[:], 0.0))
            link(nc.gpsimd.memset(eps_l2[:], 1e-6))
            link(nc.gpsimd.memset(eps_rms[:], LN_EPS))
            link(nc.gpsimd.memset(kst[96:99, 0], 1.0))
            link(nc.gpsimd.memset(kst[96:99, 1], 1.0))
            link(nc.gpsimd.memset(vp[:, :, :, 17:32], 0.0))
            link(nc.gpsimd.memset(vp[:, :, :, 16:17], 1.0))

            def rstd(g):
                pool.wait_ge(stats_ready, g + 1)
                link(nc.gpsimd.tensor_scalar(rs[:, g, :], mv[:, g, :, 1], LN_EPS, None, ALU.add))
                nc.gpsimd.tensor_tensor(rs[:, g, :], rs[:, g, :], neg_half[:, 0:4], ALU.pow).then_inc(rstd_ready, 1)

            rstd(0)
            for g in range(GROUPS):
                if g + 1 < GROUPS:
                    rstd(g + 1)
                for i in range(2):
                    pool.wait_ge(q_rounded, 3 * g + i + 1)
                    src = qf[:] if i == 0 else q_rest[:, 0]
                    nc.gpsimd.tensor_tensor(q_rest[:, i], src, qsplit[:, g % 2, i], ALU.subtract).then_inc(q_left, 1)

        @block.vector
        def _(dve):
            link = Chain(dve, dve_step)

            def stats(g):
                dve.wait_ge(x_in[g], 16)
                for n in range(4):
                    last = nc.vector.bn_stats(st6[:, g, n, :], X[:, 4 * g + n, :])
                link(last)
                for n in range(4):
                    last = nc.vector.bn_aggr(mv[:, g, n, :], st6[:, g, n, :])
                last.then_inc(stats_ready, 1)

            def normalise(g):
                dve.wait_ge(rstd_ready, g + 1)
                if g >= 2:
                    dve.wait_ge(xnT_psum, g - 1)
                for n in range(4):
                    last = nc.vector.tensor_scalar(xn[:, g % 2, n, :], X[:, 4 * g + n, :], mv[:, g, n, 0:1],
                                                   rs[:, g, n:n + 1], ALU.subtract, ALU.mult)
                last.then_inc(xn_ready, 1)

            stats(0)
            normalise(0)
            dve.wait_ge(weights_in, 8 * 16)
            nc.vector.tensor_reduce(wv_sum[:], wv[:].rearrange("p (n e) -> p n e", e=H0), AX.X, ALU.add).then_inc(wv_summed, 1)
            nc.vector.tensor_reduce(bv_sum[:], bv_rows[:].rearrange("p (n e) -> p n e", e=H0), AX.X, ALU.add).then_inc(wv_summed, 1)
            dve.wait_ge(wv_summed, 2)
            for g in range(GROUPS):
                if g + 1 < GROUPS:
                    stats(g + 1)
                    normalise(g + 1)
                b, half = g // 2, g % 2
                dve.wait_ge(v_psum, g + 1)
                heads = vp[:, 8 * b:8 * b + 8, 4 * half:4 * half + 4, 0:16].rearrange("p h t e -> p t h e")
                for t in range(4):
                    last = nc.vector.tensor_tensor(heads[:, t], ps[:, 3, 128 * t:128 * t + 128].rearrange("p (h e) -> p h e", e=16),
                                                   bv_sum[:].rearrange("p (h e) -> p h e", e=16), ALU.add)
                last.then_inc(v_ready, 1)
                dve.wait_ge(k_ready, g + 1)
                if g >= 2:
                    dve.wait_ge(splits_stored[g - 2], 2 * 16)
                split3(nc.vector, link, ksplit[:, g % 2], kf, k_rest, k_split)

        @block.tensor
        def _(pe):
            pe.wait_ge(ident_ready, 2)

            def transposes(g):
                pe.wait_ge(xn_ready, g + 1)
                if g >= 1:
                    pe.wait_ge(xnT_ready, g)
                for n in range(4):
                    last = nc.tensor.transpose(ps[:, 0, P * n:P * n + P], xn[:, g % 2, n, :], ident[:])
                last.then_inc(xnT_psum, 1)

            transposes(0)
            for g in range(GROUPS):
                pe.wait_ge(xnT_ready, g + 1)
                if g >= 1:
                    pe.wait_ge(q_ready, g)
                nc.tensor.matmul(ps[:, 1, :], wq[:], xnT[:, g % 2, :], start=True, stop=True).then_inc(q_psum, 1)
                if g >= 1:
                    pe.wait_ge(k_ready, g)
                nc.tensor.matmul(ps[:, 2, :], wk[:], xnT[:, g % 2, :], start=True, stop=True).then_inc(k_psum, 1)
                if g + 1 < GROUPS:
                    transposes(g + 1)
                pe.wait_ge(wv_summed, 2)
                if g >= 1:
                    pe.wait_ge(v_ready, g)
                for n in range(4):
                    last = nc.tensor.matmul(ps[:, 3, P * n:P * n + P], xnT[:, g % 2, P * n:P * n + P], wv_sum[:], start=True, stop=True)
                last.then_inc(v_psum, 1)

    with nc.Block() as block:
        stack_in = [sem(f"stack_in{p}") for p in range(2)]
        shift_in = sem("shift_in")
        max_psum, max_done = sem("max_psum"), sem("max_done")
        shift_split, shift_psum, shift_rows = sem("shift_split"), sem("shift_psum"), sem("shift_rows")
        score_psum, exp_done = sem("score_psum"), sem("exp_done")
        v_staged, pv_psum = sem("v_staged"), sem("pv_psum")
        ot_half0, ot_half1 = sem("ot_half0"), sem("ot_half1")
        out_psum, out_normed, out_added = sem("out_psum"), sem("out_normed"), sem("out_added")
        dve_step, divide_step, pool_step = sem("dve_step2"), sem("divide_step"), sem("pool_step2")
        maxp = ps[:, 0:4, :].rearrange("p (k c) t -> p k (c t)", k=2)
        expp = ps[:, 4:6, :]
        pvp = ps[:, 6:8, :]
        misc = ps[:, 7, :]

        def windows(eng, window):
            for w in range(4):
                window(w, w % 2)
            with eng.Fori(4, NH - 2, 2) as w0:
                for p in range(2):
                    window(w0 + p, p)
            for w in range(NH - 2, NH + 3):
                window(w, w % 2)

        def inside(w, lo, hi):
            return lo <= w < hi if isinstance(w, int) else True

        @block.sync
        def _(sp):
            def load_stack(h, p):
                qh = q_scr_h[:, bass.ds(h, 1)]
                kh = k_scr_h[:, bass.ds(h, 1)]
                sp.dma_start(qst[0:48, p, :], qh[0:1].rearrange("a h k t -> (a h) k t").broadcast_to([3, 16, S])).then_inc(stack_in[p], 16)
                sp.dma_start(qst[48:80, p, :], qh[1:2].rearrange("a h k t -> (a h) k t").broadcast_to([2, 16, S])).then_inc(stack_in[p], 16)
                sp.dma_start(qst[80:96, p, :], qh[2:3].rearrange("a h k t -> (a h k) t")).then_inc(stack_in[p], 16)
                sp.dma_start(kst[0:48, p, :], kh[0:3].rearrange("a h k t -> a (h k) t")).then_inc(stack_in[p], 16)
                sp.dma_start(kst[48:80, p, :], kh[0:2].rearrange("a h k t -> a (h k) t")).then_inc(stack_in[p], 16)
                sp.dma_start(kst[80:96, p, :], kh[0:1].rearrange("a h k t -> (a h k) t")).then_inc(stack_in[p], 16)

            def window(w, p):
                if isinstance(w, int) and w == 2:
                    sp.wait_ge(splits_stored[2], 2 * 16)
                    sp.wait_ge(splits_stored[3], 2 * 16)
                if inside(w, 0, NH - 1):
                    if inside(w, 1, NH):
                        sp.wait_ge(max_psum, 8 * w)
                    load_max(sp, w + 1, 1 - p)
                if inside(w, 1, NH + 1):
                    sp.wait_ge(shift_rows, w)
                    for j in range(3):
                        sp.dma_start(qst[96 + j:97 + j, 1 - p, :], shift_sb[8 * j:8 * j + 8, 1 - p, :]).then_inc(shift_in, 16)
                if inside(w, 0, NH):
                    if inside(w, 2, NH):
                        sp.wait_ge(score_psum, 16 * (w - 1))
                    load_stack(w, p)
                if isinstance(w, int) and w == 0:
                    for o, name in ((W1, "w1"), (W2, "w2")):
                        sp.dma_start(w_raw[:, o:o + FH], dr[f"L0_ffn_{name}_w"]).then_inc(w_in, 16)
                    for o, name, n in ((WH1, "h1", FH), (WH2, "h2", FH), (W3, "w3", D)):
                        sp.dma_start(w_raw[:, o:o + FB * n].rearrange("p (k n) -> p k n", k=FB),
                                     dr[f"L0_ffn_{name}_w"].rearrange("(k p) n -> p k n", p=P)).then_inc(w_in, 16)
                    for i, name in enumerate(("w1", "w2", "h1", "h2")):
                        sp.dma_start(ffn_scale[:, i, :], dr[f"L0_ffn_{name}_s"]).then_inc(w_in, 16)
                    sp.dma_start(w3s[:], dr["L0_ffn_w3_s"].rearrange("(p o) -> p o", o=1)).then_inc(w_in, 16)
                    for i, n in enumerate(CONVS):
                        sp.dma_start(wqkv[:, i, :], dr[f"L1_attn_W{n}"]).then_inc(w4_in, 16)
                        sp.dma_start(tap_rows[:, i, :], dr[f"L1_attn_conv_{n}"].rearrange("(o c) k -> o (c k)", o=1).broadcast_to([P, P * CONV])).then_inc(w4_in, 16)
                    sp.dma_start(wgates[:, 0:4], dr["L1_attn_Wb"]).then_inc(w4_in, 16)
                    sp.dma_start(wgates[:, 4:8], dr["L1_attn_Wg"]).then_inc(w4_in, 16)
                    sp.dma_start(wgates[:, 8:20], dr["L1_attn_Wl"]).then_inc(w4_in, 16)
                    for dst, name, n in ((gate_bias[:, 0:4], "bg", 4), (gate_bias[:, 4:16], "bl", 12), (temp[:], "log_temp", 4)):
                        sp.dma_start(dst, dr["L1_attn_" + name].rearrange("(o n) -> o n", o=1).broadcast_to([P, n])).then_inc(w4_in, 16)

            windows(sp, window)

        @block.scalar
        def _(act):
            def exps(h, units):
                for u in units:
                    act.wait_ge(score_psum, 16 * h + u + 1)
                    if inside(h, 1, NH + 9):
                        act.wait_ge(pv_psum, 4 * h - 3 + u // 4)
                    nc.scalar.activation(prob[:, u, :], expp[:, u % 2, :], ACT.Exp, scale=SCORE_SCALE).then_inc(exp_done, 1)

            def keep_products(h, half, done):
                act.wait_ge(pv_psum, 4 * h + 2 * half + 2)
                if inside(h, 1, NH + 9):
                    act.wait_ge(out_psum, h)
                nc.scalar.copy(ot[:, half, :], pvp[:, half, :]).then_inc(done, 1)

            def window(w, p):
                for k in range(8):
                    if k == 7 and inside(w, 2, NH + 2):
                        keep_products(w - 2, 1, ot_half1)
                    if k == 2 and inside(w, 1, NH + 1):
                        act.wait_ge(shift_psum, w)
                        if inside(w, 3, NH + 1):
                            act.wait_ge(shift_in, 48 * (w - 2))
                        nc.scalar.copy(shift_sb[0:24, 1 - p, :], misc[0:24, 0:P]).then_inc(shift_rows, 1)
                    if k < 5 and inside(w, 2, NH + 2):
                        exps(w - 2, (6 + 2 * k, 7 + 2 * k))
                    if k >= 5 and inside(w, 1, NH + 1):
                        exps(w - 1, (2 * k - 10, 2 * k - 9))
                    if k == 3 and inside(w, 2, NH + 2):
                        keep_products(w - 2, 0, ot_half0)

            windows(act, window)

        @block.vector
        def _(dve):
            def row_max(w, p, k):
                dve.wait_ge(max_psum, 8 * w + k + 1)
                if k == 0 and inside(w, 2, NH):
                    dve.wait_ge(shift_split, w - 1)
                nc.vector.tensor_reduce(mx[:, p, k:k + 1], maxp[:, k % 2, :], AX.X, ALU.max).then_inc(max_done, 1)

            def divide(w):
                dve.wait_ge(out_psum, w - 2)
                folded = misc[:, 0:256].rearrange("p (m e) -> p m e", e=32)
                nc.vector.reciprocal(rsum[:], folded[:, :, 16]).then_inc(divide_step, 1)
                dve.wait_ge(divide_step, w - 2)
                if inside(w, 4, NH + 3):
                    dve.wait_ge(out_added, w - 3)
                nc.vector.tensor_tensor(att[:].rearrange("p (m e) -> p m e", e=16), folded[:, :, 0:16],
                                        rsum[:].rearrange("p (m o) -> p m o", o=1).broadcast_to([P, 8, 16]), ALU.mult).then_inc(out_normed, 1)

            def split_shift(w, p):
                dve.wait_ge(max_done, 8 * (w + 1))
                if inside(w, 2, NH):
                    dve.wait_ge(shift_psum, w - 1)
                link = Chain(dve, dve_step, 5 * w)
                link(nc.vector.tensor_tensor(nmax[:, 0, :], zeros8[:], mx[:, p, :], ALU.subtract))
                link(nc.vector.tensor_tensor(shift3[:, p, 0:8], nmax[:, 0, :], zeros8[:], ALU.add))
                link(nc.vector.tensor_tensor(nmax[:, 1, :], nmax[:, 0, :], shift3[:, p, 0:8], ALU.subtract))
                link(nc.vector.tensor_tensor(shift3[:, p, 8:16], nmax[:, 1, :], zeros8[:], ALU.add))
                link(nc.vector.tensor_tensor(nmax[:, 0, :], nmax[:, 1, :], shift3[:, p, 8:16], ALU.subtract))
                nc.vector.tensor_tensor(shift3[:, p, 16:24], nmax[:, 0, :], zeros8[:], ALU.add).then_inc(shift_split, 1)

            def window(w, p):
                for k in range(8):
                    if inside(w, 0, NH):
                        row_max(w, p, k)
                    if k == 0 and inside(w, 3, NH + 3):
                        divide(w)
                if inside(w, 0, NH):
                    split_shift(w, p)

            windows(dve, window)

        @block.gpsimd
        def _(pool):
            def window(w, p):
                if inside(w, 3, NH + 3):
                    pool.wait_ge(out_normed, w - 2)
                    add_residual(w - 3)
                if inside(w, 0, NH):
                    if inside(w, 2, NH):
                        pool.wait_ge(pv_psum, 4 * (w - 1))
                    nc.gpsimd.tensor_copy(vst[:, p], vp[:, bass.ds(w, 1)].rearrange("p h t e -> p (h t) e")).then_inc(v_staged, 1)
                if isinstance(w, int) and 1 <= w < 4:
                    pool.wait_ge(w_in, 16 * W_LOADS)
                    for i in range(4 * w - 4, min(4 * w, WCOLS // 512)):
                        split_weights(i)
                if isinstance(w, int) and NH - 2 <= w < NH + 1:
                    convolve_weights(w - NH + 2)
                if isinstance(w, int) and w == NH + 1:
                    make_masks()

            def split_weights(i):
                cols = slice(512 * i, 512 * i + 512)
                nc.gpsimd.tensor_copy(w_hi[:, cols], w_raw[:, cols]).then_inc(w_split, 1)
                pool.wait_ge(w_split, 2 * i + 1)
                nc.gpsimd.tensor_tensor(w_lo[:, cols], w_raw[:, cols], w_hi[:, cols].bitcast(F32), ALU.subtract).then_inc(w_split, 1)

            def convolve_weights(i):
                pool.wait_ge(w4_in, 16 * W4_LOADS)
                if i:
                    pool.wait_ge(wc_ready, 2 * i)
                taps = tap_rows[:, i, :].rearrange("p (c k) -> p k c", k=CONV)
                for k in range(CONV):
                    last = nc.gpsimd.tensor_tensor(wc_full[:, k, :], wqkv[:, i, :], taps[:, k, :], ALU.mult)
                last.then_inc(wc_full_ready, 1)
                pool.wait_ge(wc_full_ready, i + 1)
                nc.gpsimd.tensor_copy(wc_hi[:, i], wc_full).then_inc(wc_ready, 1)
                pool.wait_ge(wc_ready, 2 * i + 1)
                nc.gpsimd.tensor_tensor(wc_lo[:, i], wc_full, wc_hi[:, i].bitcast(F32), ALU.subtract).then_inc(wc_ready, 1)

            def make_masks():
                link = Chain(pool, pool_step)
                link(nc.gpsimd.memset(head_ones[:], 0.0))
                link(nc.gpsimd.memset(low_mask[:], 1.0))
                link(nc.gpsimd.memset(up_mask[:], 1.0))
                for h in range(4):
                    q = slice(32 * h, 32 * h + 32)
                    link(nc.gpsimd.memset(head_ones[q, q], 1.0))
                    link(nc.gpsimd.tensor_copy(eye32[q, :], ident[q, q]))
                    link(nc.gpsimd.affine_select(out=low_mask[q, :], in_=low_mask[q, :], compare_op=ALU.is_gt, fill=0.0, base=0,
                                                 pattern=[[-1, C]], channel_multiplier=1))
                    link(nc.gpsimd.affine_select(out=up_mask[q, :], in_=up_mask[q, :], compare_op=ALU.is_ge, fill=0.0, base=0,
                                                 pattern=[[1, C]], channel_multiplier=-1))

            def add_residual(h):
                tile = X[:, bass.ds(h, 1), :].rearrange("p a d -> p (a d)")
                nc.gpsimd.tensor_tensor(tile, tile, att[:], ALU.add).then_inc(out_added, 1)

            windows(pool, window)

        @block.tensor
        def _(pe):
            def row_scores(w, p, k):
                if k == 0:
                    pe.wait_ge(mx_in[p], 8 * 16 * (w // 2 + 1) if isinstance(w, int) else 64 * w + (128 - 64 * p))
                if inside(w, 1, NH) or k >= 2:
                    pe.wait_ge(max_done, 8 * w + k - 1)
                nc.tensor.matmul(maxp[:, k % 2, 0:512], qm[0:48, p, P * k:P * k + P], km[0:48, p, 0:512], start=True, stop=True)
                nc.tensor.matmul(maxp[:, k % 2, 512:1024], qm[64:112, p, P * k:P * k + P], km[64:112, p, 512:1024],
                                 start=True, stop=True).then_inc(max_psum, 1)

            def scores(h, p, units):
                for u in units:
                    if u == 0:
                        pe.wait_ge(stack_in[p], 96 * (h // 2 + 1) if isinstance(h, int) else 48 * h + (96 - 48 * p))
                        pe.wait_ge(shift_in, 48 * (h + 1))
                    if inside(h, 1, NH + 9) or u >= 2:
                        pe.wait_ge(exp_done, 16 * h + u - 1)
                    s, t = u // 8, u % 8
                    nc.tensor.matmul(expp[:, u % 2, :], kst[0:99, p, P * t:P * t + P], qst[0:99, p, 512 * s:512 * s + 512],
                                     start=True, stop=True).then_inc(score_psum, 1)

            def pv(w, h, p, g, part):
                if part == 0:
                    pe.wait_ge(exp_done, 16 * h + 4 * g + 4)
                if g == 0 and part == 0:
                    pe.wait_ge(v_staged, h + 1)
                    if inside(h, 1, NH + 9):
                        pe.wait_ge(ot_half0, h)
                if g == 2 and part == 0:
                    if inside(w, 1, NH + 1):
                        pe.wait_ge(shift_rows, w)
                    else:
                        pe.wait_ge(out_normed, w - 2)
                cols = slice(256 * part, 256 * part + 256)
                for j in range(4):
                    u = 4 * g + j
                    last = nc.tensor.matmul(pvp[32 * j:32 * j + 32, g // 2, cols], vst[:, p, u % 8, :], prob[:, u, cols],
                                            start=(g % 2 == 0 and part == 0), stop=(g % 2 == 1), skip_group_check=True)
                if part == 1:
                    last.then_inc(pv_psum, 1)

            def fold(w):
                pe.wait_ge(ot_half0, w - 2)
                pe.wait_ge(ot_half1, w - 2)
                for m in range(8):
                    last = nc.tensor.matmul(misc[:, 32 * m:32 * m + 32], ot_by_m[:, m, :], fold_sel[:], start=True, stop=True)
                last.then_inc(out_psum, 1)

            def shift_to_rows(w, p):
                pe.wait_ge(shift_split, w)
                if inside(w, 3, NH + 1):
                    pe.wait_ge(out_normed, w - 2)
                nc.tensor.matmul(misc[0:24, 0:P], shift3[:, 1 - p, :], ident_bf[:], start=True, stop=True).then_inc(shift_psum, 1)

            def window(w, p):
                if isinstance(w, int) and w == 2:
                    pe.wait_ge(shift_rows, w - 1)
                    for _ in range(32):
                        nc.tensor.matmul(misc[:, 0:P], ident_bf[:], ident_bf[:], start=True, stop=True)
                for k in range(8):
                    if k < 5 and inside(w, 2, NH + 2):
                        scores(w - 2, p, (6 + 2 * k, 7 + 2 * k))
                    if k >= 5 and inside(w, 1, NH + 1):
                        scores(w - 1, 1 - p, (2 * k - 10, 2 * k - 9))
                    if inside(w, 0, NH):
                        row_scores(w, p, k)
                    if k == 1 and inside(w, 1, NH + 1):
                        shift_to_rows(w, p)
                    if k == 7:
                        if inside(w, 1, NH + 1):
                            pv(w, w - 1, 1 - p, 0, 0)
                    elif inside(w, 2, NH + 2):
                        pv(w, w - 2, p, (k + 1) // 2, (k + 1) % 2)
                    if k == 0 and inside(w, 3, NH + 3):
                        fold(w)

            windows(pe, window)
    sub.close()
    sub = ExitStack()

    def sb3(name, shape, dt=F32):
        return sub.enter_context(nc.sbuf_tensor(name, shape, dt))

    xt_hi, xt_lo = sb3("xt_hi", [P, GT], F32R), sb3("xt_lo", [P, GT], F32R)
    hf = sb3("hf", [P, FB, GT])
    h_hi, h_lo = sb3("h_hi", [P, 2, FB, GT], F32R), sb3("h_lo", [P, 2, FB, GT], F32R)
    y_feat = sb3("y_feat", [P, GT])
    mv2, st62, rs2 = sb3("mv2", [P, GROUPS, 4, 2]), sb3("st62", [P, GROUPS, 4, 6]), sb3("rs2", [P, GROUPS, 4])

    with nc.Block() as block:
        stats_ready, rstd_ready, x1_ready = sem("ln1_stats"), sem("ln1_rstd"), sem("x1_ready")
        stats2_ready, rstd2_ready, x2_ready = sem("ln2_stats"), sem("ln2_rstd"), sem("x2_ready")
        xT_psum, xT_hi, xT_lo = sem("x1T_psum"), sem("x1T_hi"), sem("x1T_lo")
        gate_psum, up_psum = sem("gate_psum"), sem("up_psum")
        silu_done, h_ready = sem("silu_done"), sem("h_ready")
        hid_psum, gelu_done = sem("hid_psum"), sem("gelu_done")
        hi_ready, lo_ready = sem("h_hi_ready"), sem("h_lo_ready")
        y_psum, y_scaled, yT_psum, y_added = sem("y_psum"), sem("y_scaled"), sem("yT_psum"), sem("y_added")
        dve_step, pool_step = sem("dve_step3"), sem("pool_step3")

        @block.scalar
        def _(act):

            def transposed(g):
                act.wait_ge(xT_psum, g + 1)
                nc.scalar.copy(xt_hi[:], ps[:, 1, :]).then_inc(xT_hi, 1)

            def silus(g):
                for o in range(FB):
                    act.wait_ge(gate_psum, 4 * g + o + 1)
                    if g >= 1:
                        act.wait_ge(lo_ready, 12 * (g - 1) + 8 + o + 1)
                    nc.scalar.activation(hf[:, o, :], ps[:, o, :], ACT.Silu, scale=ffn_scale[:, 0, o:o + 1]).then_inc(silu_done, 1)

            transposed(0)
            silus(0)
            for g in range(GROUPS):
                for layer in (1, 2):
                    for o in range(FB):
                        act.wait_ge(hid_psum, 8 * g + 4 * (layer - 1) + o + 1)
                        act.wait_ge(lo_ready, 12 * g + 4 * (layer - 1) + o + 1)
                        nc.scalar.activation(hf[:, o, :], ps[:, 4 * (layer - 1) + o, :], ACT.Gelu,
                                             scale=ffn_scale[:, 1 + layer, o:o + 1]).then_inc(gelu_done, 1)
                    if layer == 1 and g + 1 < GROUPS:
                        transposed(g + 1)
                if g + 1 < GROUPS:
                    silus(g + 1)
                act.wait_ge(y_psum, g + 1)
                if g >= 1:
                    act.wait_ge(yT_psum, g)
                nc.scalar.activation(y_feat[:], ps[:, 7, :], ACT.Copy, scale=w3s[:, 0:1]).then_inc(y_scaled, 1)

        @block.gpsimd
        def _(pool):
            link = Chain(pool, pool_step)

            def rstd(g, stats, rstd_sem, mvt, rst):
                pool.wait_ge(stats, g + 1)
                link(nc.gpsimd.tensor_scalar(rst[:, g, :], mvt[:, g, :, 1], LN_EPS, None, ALU.add))
                nc.gpsimd.tensor_tensor(rst[:, g, :], rst[:, g, :], neg_half[:, 0:4], ALU.pow).then_inc(rstd_sem, 1)

            for g in range(GROUPS):
                rstd(g, stats_ready, rstd_ready, mv, rs)
            for g in range(GROUPS):
                for layer in range(3):
                    for o in range(FB):
                        i = 4 * layer + o
                        pool.wait_ge(hi_ready, 12 * g + i + 1)
                        nc.gpsimd.tensor_tensor(h_lo[:, layer % 2, o, :], hf[:, o, :], h_hi[:, layer % 2, o, :].bitcast(F32),
                                                ALU.subtract).then_inc(lo_ready, 1)
                    if layer == 1 and g >= 1:
                        rstd(g - 1, stats2_ready, rstd2_ready, mv2, rs2)
            rstd(GROUPS - 1, stats2_ready, rstd2_ready, mv2, rs2)

        @block.vector
        def _(dve):
            link = Chain(dve, dve_step)

            def stats(g, ready, st, mvt):
                for n in range(4):
                    last = nc.vector.bn_stats(st[:, g, n, :], X[:, 4 * g + n, :])
                link(last)
                for n in range(4):
                    last = nc.vector.bn_aggr(mvt[:, g, n, :], st[:, g, n, :])
                last.then_inc(ready, 1)

            def normalise(g, rstd, ready, mvt, rst):
                dve.wait_ge(rstd, g + 1)
                for n in range(4):
                    tile = X[:, 4 * g + n, :]
                    last = nc.vector.tensor_scalar(tile, tile, mvt[:, g, n, 0:1], rst[:, g, n:n + 1], ALU.subtract, ALU.mult)
                last.then_inc(ready, 1)

            def transposed(g):
                dve.wait_ge(xT_hi, g + 1)
                nc.vector.tensor_tensor(xt_lo[:], ps[:, 1, :], xt_hi[:].bitcast(F32), ALU.subtract).then_inc(xT_lo, 1)

            def hi(g, layer, o):
                nc.vector.tensor_copy(h_hi[:, layer % 2, o, :], hf[:, o, :]).then_inc(hi_ready, 1)

            def gated(g):
                for o in range(FB):
                    dve.wait_ge(silu_done, 4 * g + o + 1)
                    dve.wait_ge(up_psum, 4 * g + o + 1)
                    nc.vector.scalar_tensor_tensor(hf[:, o, :], ps[:, 4 + o, :], ffn_scale[:, 1, o:o + 1], hf[:, o, :],
                                                   ALU.mult, ALU.mult).then_inc(h_ready, 1)
                    dve.wait_ge(h_ready, 4 * g + o + 1)
                    hi(g, 0, o)

            stats(0, stats_ready, st6, mv)
            normalise(0, rstd_ready, x1_ready, mv, rs)
            transposed(0)
            for g in range(1, GROUPS):
                stats(g, stats_ready, st6, mv)
            gated(0)
            for g in range(GROUPS):
                if g + 1 < GROUPS:
                    normalise(g + 1, rstd_ready, x1_ready, mv, rs)
                for layer in (1, 2):
                    for o in range(FB):
                        dve.wait_ge(gelu_done, 8 * g + 4 * (layer - 1) + o + 1)
                        hi(g, layer, o)
                    if layer == 1 and g + 1 < GROUPS:
                        transposed(g + 1)
                    if layer == 1 and g >= 1:
                        normalise(g - 1, rstd2_ready, x2_ready, mv2, rs2)
                dve.wait_ge(yT_psum, g + 1)
                x4 = X[:, 4 * g:4 * g + 4, :].rearrange("p n d -> p (n d)")
                nc.vector.tensor_tensor(x4, x4, ps[:, 6, :], ALU.add).then_inc(y_added, 1)
                if g + 1 < GROUPS:
                    gated(g + 1)
                dve.wait_ge(y_added, g + 1)
                stats(g, stats2_ready, st62, mv2)
            normalise(GROUPS - 1, rstd2_ready, x2_ready, mv2, rs2)
            dve.wait_ge(x2_ready, GROUPS)

        @block.tensor
        def _(pe):
            def product(out, w, x, start, stop):
                (wh, wl), (xh, xl) = w, x
                nc.tensor.matmul(out, wl, xh, start=start, stop=False)
                nc.tensor.matmul(out, wh, xl, start=False, stop=False)
                return nc.tensor.matmul(out, wh, xh, start=False, stop=stop)

            def weights(o, n):
                return w_hi[:, o:o + n], w_lo[:, o:o + n]

            def transposes(g):
                pe.wait_ge(x1_ready, g + 1)
                if g >= 1:
                    pe.wait_ge(gelu_done, 8 * g - 6)
                for n in range(4):
                    last = nc.tensor.transpose(ps[:, 1, P * n:P * n + P], X[:, 4 * g + n, :], ident[:])
                last.then_inc(xT_psum, 1)

            xT = xt_hi[:], xt_lo[:]

            def gate(g):
                pe.wait_ge(xT_hi, g + 1)
                pe.wait_ge(xT_lo, g + 1)
                for o in range(FB):
                    if g >= 1:
                        pe.wait_ge(gelu_done, 8 * g - 8 + o + 1)
                    product(ps[:, o, :], weights(W1 + P * o, P), xT, True, True).then_inc(gate_psum, 1)

            def up(g, blocks):
                for o in blocks:
                    if g >= 1 and o >= 2:
                        pe.wait_ge(y_added, g)
                    product(ps[:, 4 + o, :], weights(W2 + P * o, P), xT, True, True).then_inc(up_psum, 1)

            def hidden(g, layer, w0):
                src = (layer - 1) % 2
                for k in range(FB):
                    pe.wait_ge(hi_ready, 12 * g + 4 * (layer - 1) + k + 1)
                    pe.wait_ge(lo_ready, 12 * g + 4 * (layer - 1) + k + 1)
                    for o in range(FB):
                        if k == 0:
                            pe.wait_ge(silu_done if layer == 1 else h_ready, 4 * g + o + 1)
                        last = product(ps[:, 4 * (layer - 1) + o, :], weights(w0 + FH * k + P * o, P),
                                       (h_hi[:, src, k, :], h_lo[:, src, k, :]), k == 0, k == FB - 1)
                        if k == FB - 1:
                            last.then_inc(hid_psum, 1)
                    if layer == 2 and k == 0 and g + 1 < GROUPS:
                        transposes(g + 1)

            transposes(0)
            gate(0)
            up(0, range(FB))
            for g in range(GROUPS):
                hidden(g, 1, WH1)
                hidden(g, 2, WH2)
                if g + 1 < GROUPS:
                    gate(g + 1)
                for k in range(FB):
                    pe.wait_ge(lo_ready, 12 * g + 8 + k + 1)
                    pe.wait_ge(gelu_done, 8 * g + 8)
                    last = product(ps[:, 7, :], weights(W3 + D * k, D), (h_hi[:, 0, k, :], h_lo[:, 0, k, :]), k == 0, k == FB - 1)
                last.then_inc(y_psum, 1)
                if g + 1 < GROUPS:
                    up(g + 1, (0, 1))
                pe.wait_ge(y_scaled, g + 1)
                for n in range(4):
                    last = nc.tensor.transpose(ps[:, 6, P * n:P * n + P], y_feat[:, P * n:P * n + P], ident[:])
                last.then_inc(yT_psum, 1)
                if g + 1 < GROUPS:
                    up(g + 1, (2, 3))
    sub.close()
    ffn_weights.close()

    with nc.Block() as block:
        @block.gpsimd
        def _(pool):
            for s in early_sems[0::4]:
                pool.sem_clear(s)

        @block.sync
        def _(sp):
            for s in early_sems[1::4]:
                sp.sem_clear(s)

        @block.scalar
        def _(act):
            for s in early_sems[2::4]:
                act.sem_clear(s)

        @block.vector
        def _(dve):
            for s in early_sems[3::4]:
                dve.sem_clear(s)
    early.close()

    def sem(name):
        return ctx.enter_context(nc.semaphore(name))
    sub = ExitStack()

    def sb4(name, shape, dt=F32):
        return sub.enter_context(nc.sbuf_tensor(name, shape, dt))

    def sem4(name, n=1):
        made = [ctx.enter_context(nc.semaphore(f"{name}{i}")) for i in range(n)]
        return made if n > 1 else made[0]

    def sb_kept(name, shape, dt=F32):
        return ctx.enter_context(nc.sbuf_tensor(name, shape, dt))

    k0, k1, k2 = sb_kept("k0", [P, 2, FH], U8), sb_kept("k1", [P, FB, FH], U8), sb_kept("k2", [P, FB, D], U8)
    sw0 = sb_kept("sw0", [P, FH], F32R)
    s_in, s_out = sb_kept("s_in", [P, 3]), sb_kept("s_out", [P, 3])

    XCOLS = S + CONV - 1
    FIR_PE = 8
    wo1 = sb4("wo1", [P, P])
    fir_s, fir_l = sb4("fir_s", [P, FIRS]), sb4("fir_l", [P, FIRL])
    fir_diag = sb4("fir_diag", [P, FIR_PE, P])
    rmsw = sb4("rmsw", [P, 1])
    gates, mixw = sb4("gates", [P, NT, 8]), sb4("mixw", [P, NT, 12])
    gmax, gsum = sb4("gmax", [P, NT, 4]), sb4("gsum", [P, NT, 4])
    keep_local = sb4("keep_local", [P, NT, 4])
    xf = sb4("xf", [P, GT])
    x_hi, x_lo = sb4("x_hi4", [P, B, XCOLS], F32R), sb4("x_lo4", [P, B, XCOLS], F32R)
    mt = sb4("mt", [P, B, 4, 8, C])
    ks, qs = sb4("ks", [P, B * S]), sb4("qs", [P, B * S])
    vpad = sb4("vpad", [P, B, S + FIRL - 1])
    sq = sb4("sq", [P, 2, GT])
    rn = xn[:].rearrange("p a n d -> p a (n d)")
    vtok = sb4("vtok", [P, NT, P])
    ka = sb4("ka", [P, NT, 4, 2, C])
    vk = sb4("vk", [P, NT, 4, 2, C])
    low = sb4("low", [P, 4, NT, C])
    inv_flat = sb4("inv_flat", [P, B, 3, C * C])
    lp, tp, prod = (inv_flat[:, :, i].rearrange("p b (i e) -> p b i e", i=C) for i in range(3))
    tT = sb4("tT", [P, B, C, C])
    state = sb4("state", [P, 33, B, C])
    short, long_ = sb4("short", [P, B, S]), sb4("long_", [P, B, S])
    tapped = sq[:].rearrange("p i t -> p (i t)")
    gT = qs
    blend = low[:].rearrange("p h (a n) e -> p (h a) (n e)", a=1)
    oss, ors = sb4("oss", [P, GROUPS, 16]), sb4("ors", [P, GROUPS, 16])
    osq, oT = (vk[:, 8 * i:8 * i + 4].rearrange("p n h a e -> p (n h a e)").rearrange("p (i t) -> p i t", i=2) for i in range(2))
    mv3, st63, rs3 = mv, st6, rs
    low_dram = nc.dram_tensor("low_dram", (B, 4, 8, 4, C, C), F32, kind="Internal").ap()
    inv_dram = nc.dram_tensor("inv_dram", (B, 4, 8, 4, C, C), F32, kind="Internal").ap()

    def uw(b, r, n, h):
        o = (4 * n + h) * 64
        return inv_flat[r, b].rearrange("p i e -> p (i e)")[:, o:o + 64]

    def rows(ap, g):
        return ap[:, GT * g:GT * g + GT]

    def v_rows(g):
        return vpad[:, g // 2, FIRL - 1 + GT * (g % 2):FIRL - 1 + GT * (g % 2) + GT]

    def heads(ap):
        return ap.rearrange("p (n h e) -> p n h e", h=4, e=C)

    def per_head(ap):
        return ap.rearrange("p n (h o) -> p n h o", o=1).broadcast_to([P, ap.shape[1], 4, C])

    FINAL = (0, 2, 1, 3)

    with nc.Block() as block:
        rest_in, signs_in = sem4("rest_in"), sem4("signs_in")
        padded, temp_exp = sem4("padded"), sem4("temp_exp")
        diag_ready, wo_scaled = sem4("diag_ready"), sem4("wo_scaled")
        xT_psum, xf_ready, xhi_ready, xlo_ready = sem4("x2T_psum"), sem4("xf_ready"), sem4("xhi_ready"), sem4("xlo_ready")
        conv_psum, silu_done = sem4("conv_psum"), sem4("silu_done4")
        gates_psum, gates_biased, gates_exp, beta_ready, mix_done = (sem4("gates_psum"), sem4("gates_biased"), sem4("gates_exp"),
                                                                     sem4("beta_ready"), sem4("mix_done"))
        sq_ready, ss_psum, ln_done, rn_ready, normed = (sem4("sq_ready"), sem4("ss_psum"), sem4("ln_done"), sem4("rn_ready"),
                                                        sem4("qk_normed"))
        vtok_psum, vtok_ready, ktok_psum, ktok_ready, vb_ready, kb_ready = (
            sem4("vtok_psum"), sem4("vtok_ready"), sem4("ktok_psum"), sem4("ktok_ready"), sem4("vb_ready"), sem4("kb_ready"))
        tri_psum, att_psum, tri_masked, att_ready, low_ready = (sem4("tri_psum"), sem4("att_psum"), sem4("tri_masked"),
                                                                sem4("att_ready"), sem4("low_ready", 2))
        low_stored, low_in, inv_ready, inv_stored, inv_in = (sem4("low_stored", 2), sem4("low_in", 2), sem4("inv_ready", 2),
                                                             sem4("inv_stored", 2), sem4("inv_in", 2))
        fir_psum, fir_begun, long_done, short_done = sem4("fir_psum"), sem4("fir_begun"), sem4("long_done"), sem4("short_done")
        uw_psum, uw_ready, mg_psum, m_ready, g_ready, b_psum, b_ready = (
            sem4("uw_psum"), sem4("uw_ready"), sem4("mg_psum"), sem4("m_ready"), sem4("g_ready"), sem4("b_psum"), sem4("b_ready"))
        state_psum, state_ready, o_begun, o_psum = sem4("state_psum"), sem4("state_ready"), sem4("o_begun"), sem4("o_psum")
        local_psum, local_used, local_ready = sem4("local_psum"), sem4("local_used"), sem4("local_ready")
        blended, osq_ready, oss_ready, ors_ready, o_scaled = (sem4("blended"), sem4("osq_ready"), sem4("oss_ready"), sem4("ors_ready"),
                                                              sem4("o_scaled"))
        oT_psum, oT_ready, y_psum, stats_ready, rstd_ready, x3_ready = (
            sem4("oT_psum"), sem4("oT_ready"), sem4("y4_psum"), sem4("ln3_stats"), sem4("ln3_rstd"), sem4("x3_ready"))
        dve_step, pool_step = sem4("dve_step4"), sem4("pool_step4")

        @block.sync
        def _(sp):
            sp.dma_start(fir_s[:], dr["L1_attn_fir_short"].rearrange("h c k -> (h c) k")).then_inc(rest_in, 16)
            sp.dma_start(fir_l[:], dr["L1_attn_fir_long"].rearrange("h c k -> (h c) k")).then_inc(rest_in, 16)
            sp.dma_start(wo1[:], dr["L1_attn_Wo"]).then_inc(rest_in, 16)
            for h in range(4):
                sp.dma_start(rmsw[32 * h:32 * h + 32, :], dr["L1_attn_rms_w"].rearrange("(p o) -> p o", o=1)).then_inc(rest_in, 16)
            sp.dma_start(k0[:], dr["L1_ffn_k0"].rearrange("(a p) n -> p a n", p=P)).then_inc(signs_in, 16)
            sp.dma_start(k1[:], dr["L1_ffn_k1"].rearrange("(a p) n -> p a n", p=P)).then_inc(signs_in, 16)
            sp.dma_start(k2[:], dr["L1_ffn_k2"].rearrange("(a p) n -> p a n", p=P)).then_inc(signs_in, 16)
            for i in range(3):
                sp.dma_start(s_in[:, i:i + 1], dr[f"L1_ffn_s{i}"].rearrange("(o n) -> o n", o=1).broadcast_to([P, 1])).then_inc(signs_in, 16)
            for b in range(B):
                sp.wait_ge(low_ready[b], 2)
                for h in range(4):
                    sp.dma_start(low_dram[b, h].rearrange("n c t e -> (c t) n e"), low[:, h, 8 * b:8 * b + 8, :]).then_inc(low_stored[b], 16)
                sp.wait_ge(low_stored[b], 64)
                sp.dma_start(lp[:, b], low_dram[b].rearrange("h n c t e -> (h n c) t e")).then_inc(low_in[b], 16)
            for b in range(B):
                sp.wait_ge(inv_ready[b], 1)
                sp.dma_start(inv_dram[b].rearrange("h n c e i -> (h n c) e i"), tp[:, b]).then_inc(inv_stored[b], 16)
                sp.wait_ge(inv_stored[b], 16)
                sp.dma_start(tT[:, b], inv_dram[b].rearrange("h n c e i -> (c e) (h n) i")).then_inc(inv_in[b], 16)

        def invert(engine, eng, link, b):
            eng.wait_ge(low_in[b], 16)
            for j in range(C - 1):
                n, m = j + 1, C - 1 - j
                part = prod[:, b, 0:n, 0:m]
                link(engine.tensor_tensor(part, lp[:, b, j + 1:C, j:j + 1].rearrange("p i o -> p o i").broadcast_to([P, n, m]),
                                          tp[:, b, 0:n, j:j + 1].broadcast_to([P, n, m]), ALU.mult))
                ins = engine.tensor_tensor(tp[:, b, 0:n, j + 1:C], tp[:, b, 0:n, j + 1:C], part, ALU.subtract)
                if j < C - 2:
                    link(ins)
                else:
                    ins.then_inc(inv_ready[b], 1)

        def start_inverse(engine, link, b):
            link(engine.memset(tp[:, b], 0.0))
            link(engine.memset(tp[:, b].rearrange("p e i -> p (e i)")[:, 0:C * C:C + 1], 1.0))

        def times_beta(engine, eng, g):
            for i, ready, done in ((0, vtok_ready, vb_ready), (1, ktok_ready, kb_ready)):
                eng.wait_ge(ready, g + 1)
                for n in range(4):
                    t = 4 * g + n
                    src = vtok[:, t, :].rearrange("p (h e) -> p h e", h=4) if i == 0 else ka[:, t, :, 0, :]
                    last = engine.tensor_tensor(vk[:, t, :, i, :], src,
                                                gates[:, t, 0:4].rearrange("p (h o) -> p h o", o=1).broadcast_to([P, 4, C]), ALU.mult)
                last.then_inc(done, 1)

        def triangles_times_beta(engine, eng, g):
            eng.wait_ge(tri_masked, g + 1)
            t = 4 * g
            for h in range(4):
                tri = low[:, h, t:t + 4, :]
                last = engine.tensor_tensor(tri, tri, gates[:, t:t + 4, h:h + 1].broadcast_to([P, 4, C]), ALU.mult)
            last.then_inc(low_ready[g // 2], 1)

        @block.vector
        def _(dve):
            link = Chain(dve, dve_step)

            def split_x(g):
                dve.wait_ge(xhi_ready, g + 1)
                cols = slice(CONV - 1 + GT * (g % 2), CONV - 1 + GT * (g % 2) + GT)
                nc.vector.tensor_tensor(x_lo[:, g // 2, cols], ps[:, 0, :], x_hi[:, g // 2, cols].bitcast(F32), ALU.subtract).then_inc(xlo_ready, 1)

            def square(g, i):
                dve.wait_ge(silu_done, 3 * g + i + 1)
                if g >= 1:
                    dve.wait_ge(ss_psum, 2 * g - 1 + i)
                t = rows((ks, qs)[i], g)
                nc.vector.tensor_tensor(sq[:, i, :], t, t, ALU.mult).then_inc(sq_ready, 1)

            def normalise(g, i):
                dve.wait_ge(rn_ready, 2 * g + i + 1)
                t = rows((ks, qs)[i], g)
                nc.vector.tensor_tensor(t, t, rn[:, i, :], ALU.mult).then_inc(normed, 1)

            def gate_logits(g):
                dve.wait_ge(gates_psum, g + 1)
                n4 = slice(4 * g, 4 * g + 4)
                gp = ps[:, 3, 0:80].rearrange("p (n e) -> p n e", n=4)
                bias = gate_bias[:].rearrange("p (o e) -> p o e", o=1)
                nc.vector.tensor_copy(gates[:, n4, 0:4], gp[:, :, 0:4])
                nc.vector.tensor_tensor(gates[:, n4, 4:8], gp[:, :, 4:8], bias[:, :, 0:4].broadcast_to([P, 4, 4]), ALU.add)
                link(nc.vector.tensor_tensor(mixw[:, n4, :], gp[:, :, 8:20], bias[:, :, 4:16].broadcast_to([P, 4, 12]), ALU.add))
                for j in range(3):
                    last = nc.vector.tensor_tensor(mixw[:, n4, j:12:3], mixw[:, n4, j:12:3],
                                                   temp[:].rearrange("p (o h) -> p o h", o=1).broadcast_to([P, 4, 4]), ALU.mult)
                link(last)
                logits = mixw[:, n4, :].rearrange("p n (h j) -> p (n h) j", j=3)
                gm = gmax[:, n4, :].rearrange("p n h -> p (n h)")
                link(nc.vector.tensor_reduce(gm, logits, AX.X, ALU.max))
                nc.vector.tensor_tensor(logits, logits, gm.rearrange("p (a o) -> p a o", o=1).broadcast_to([P, 16, 3]),
                                        ALU.subtract).then_inc(gates_biased, 1)

            def gate_sigmoids(g):
                dve.wait_ge(gates_exp, g + 1)
                n4 = slice(4 * g, 4 * g + 4)
                link(nc.vector.tensor_scalar(gates[:, n4, :], gates[:, n4, :], 1.0, None, ALU.add))
                nc.vector.reciprocal(gates[:, n4, :], gates[:, n4, :]).then_inc(beta_ready, 1)

            def masks(g):
                dve.wait_ge(tri_psum, g + 1)
                n4 = slice(4 * g, 4 * g + 4)

                def mask4(m):
                    return m[:].rearrange("p (a o e) -> p a o e", a=1, o=1).broadcast_to([P, 4, 4, C])

                nc.vector.tensor_tensor(low[:, :, n4, :], ps[:, 4:8, 0:128].rearrange("p h (n e) -> p h n e", e=C), mask4(low_mask),
                                        ALU.mult).then_inc(tri_masked, 1)
                nc.vector.tensor_tensor(ka[:, n4, :, 1, :].rearrange("p n h e -> p h n e"),
                                        ps[:, 4:8, 128:256].rearrange("p h (n e) -> p h n e", e=C), mask4(up_mask),
                                        ALU.mult).then_inc(att_ready, 1)

            def fir(b, lo, hi, done=False):
                dve.wait_ge(fir_begun, 2 * b + 2)
                for t in range(lo, hi):
                    ins = nc.vector.scalar_tensor_tensor(long_[:, b], vpad[:, b, t:t + S], fir_l[:, t:t + 1], long_[:, b], ALU.mult, ALU.add)
                    if done and t == hi - 1:
                        ins.then_inc(long_done, 1)
                    else:
                        link(ins)

            dve.wait_ge(temp_exp, 1)
            split_x(0)
            start_inverse(nc.vector, link, 1)
            for g in range(GROUPS):
                gate_logits(g)
                if g + 1 < GROUPS:
                    split_x(g + 1)
                square(g, 0)
                square(g, 1)
                if g >= 1:
                    masks(g - 1)
                if g >= 3:
                    triangles_times_beta(nc.vector, dve, g - 1)
                    times_beta(nc.vector, dve, g - 1)
                gate_sigmoids(g)
                normalise(g, 0)
                normalise(g, 1)
            masks(3)
            triangles_times_beta(nc.vector, dve, 3)
            times_beta(nc.vector, dve, 3)
            dve.wait_ge(gates_exp, GROUPS)
            logits = mixw[:].rearrange("p n (h j) -> p (n h) j", j=3)
            gs = gsum[:].rearrange("p n h -> p (n h)")
            nc.vector.tensor_scalar(keep_local[:], gates[:, :, 4:8], -1.0, 1.0, ALU.mult, ALU.add)
            link(nc.vector.tensor_reduce(gs, logits, AX.X, ALU.add))
            link(nc.vector.reciprocal(gs, gs))
            link(nc.vector.tensor_tensor(gs, gs, keep_local[:].rearrange("p n h -> p (n h)"), ALU.mult))
            nc.vector.tensor_tensor(logits, logits, gs.rearrange("p (a o) -> p a o", o=1).broadcast_to([P, 4 * NT, 3]),
                                    ALU.mult).then_inc(mix_done, 1)
            invert(nc.vector, dve, link, 1)

            def transitions(b):
                view = "p (n a e) -> p n a e"
                dve.wait_ge(mg_psum, b + 1)
                for c in range(4):
                    src = ps[:, c, :].rearrange(view, n=8, a=2)
                    last = nc.vector.tensor_tensor(mt[:, b, c], eye32[:].rearrange("p (o e) -> p o e", o=1).broadcast_to([P, 8, C]),
                                                   src[:, :, 0, :], ALU.subtract)
                last.then_inc(m_ready, 1)
                for c in range(4):
                    src = ps[:, c, :].rearrange(view, n=8, a=2)
                    q = qs[:, S * b:S * b + S].rearrange("p (n c t) -> p c n t", n=8, c=4)[:, c]
                    last = nc.vector.tensor_tensor(q, q, src[:, :, 1, :], ALU.subtract)
                last.then_inc(g_ready, 1)

            fir(0, FIR_PE, FIR_PE + 4)
            transitions(0)
            fir(0, FIR_PE + 4, FIR_PE + 9)
            transitions(1)
            fir(0, FIR_PE + 9, FIRL, done=True)
            fir(1, FIR_PE, FIRL, done=True)

            def local(g, i):
                n4 = slice(4 * g, 4 * g + 4)
                k = 2 * FINAL.index(g) + i
                dve.wait_ge(local_psum, k + 1)
                if i == 1:
                    tmp = tapped[:, GT:2 * GT]
                else:
                    tmp = tapped[:, 0:GT]
                if k >= 2:
                    dve.wait_ge(local_ready, k // 2)
                nc.vector.tensor_tensor(heads(tmp), heads(ps[:, 2 + i, :]), per_head(mixw[:, n4, 1 + i:12:3]), ALU.mult).then_inc(local_used, 1)

            def blend_global(i):
                g = FINAL[i]
                dve.wait_ge(o_psum, 1)
                nc.vector.tensor_tensor(heads(blend[:, g, :]), ps[:, 4:8, P * g:P * g + P].rearrange("p h (n e) -> p n h e", e=C), per_head(gates[:, 4 * g:4 * g + 4, 4:8]), ALU.mult).then_inc(dve_step, 1)
                link.n += 1
                dve.wait_ge(dve_step, link.n)
                dve.wait_ge(local_ready, i + 1)
                nc.vector.tensor_tensor(blend[:, g, :], blend[:, g, :], vtok[:, 4 * g:4 * g + 4, :].rearrange("p n d -> p (n d)"), ALU.add).then_inc(blended, 1)

            def sum_squares(i):
                g = FINAL[i]
                dve.wait_ge(osq_ready, i + 1)
                nc.vector.tensor_reduce(oss[:, g, :], osq[:, i % 2, :].rearrange("p (a e) -> p a e", e=C), AX.X, ALU.add).then_inc(oss_ready, 1)

            def scale_o(i):
                g = FINAL[i]
                dve.wait_ge(ors_ready, i + 1)
                b3 = blend[:, g, :].rearrange("p (a e) -> p a e", e=C)
                nc.vector.tensor_tensor(b3, b3, ors[:, g, :].rearrange("p (a o) -> p a o", o=1).broadcast_to([P, 16, C]), ALU.mult).then_inc(o_scaled, 1)

            def residual(i):
                g = FINAL[i]
                dve.wait_ge(y_psum, i + 1)
                x4 = X[:, 4 * g:4 * g + 4, :].rearrange("p n d -> p (n d)")
                link(nc.vector.tensor_tensor(x4, x4, ps[:, i % 2, :], ALU.add))
                for n in range(4):
                    last = nc.vector.bn_stats(st63[:, g, n, :], X[:, 4 * g + n, :])
                link(last)
                for n in range(4):
                    last = nc.vector.bn_aggr(mv3[:, g, n, :], st63[:, g, n, :])
                last.then_inc(stats_ready, 1)

            def last_norm(i):
                g = FINAL[i]
                dve.wait_ge(rstd_ready, i + 1)
                for n in range(4):
                    tile = X[:, 4 * g + n, :]
                    last = nc.vector.tensor_scalar(tile, tile, mv3[:, g, n, 0:1], rs3[:, g, n:n + 1], ALU.subtract, ALU.mult)
                last.then_inc(x3_ready, 1)

            dve.wait_ge(signs_in, 16 * 6)
            nc.vector.tensor_tensor(sw0[:], k0[:, 0, :], k0[:, 1, :], ALU.subtract)
            dve.wait_ge(short_done, B)
            for g in FINAL:
                local(g, 0)
                local(g, 1)
            blend_global(0)
            blend_global(1)
            sum_squares(0)
            for i in range(GROUPS):
                if i + 2 < GROUPS:
                    blend_global(i + 2)
                if i + 1 < GROUPS:
                    sum_squares(i + 1)
                scale_o(i)
                if i >= 1:
                    residual(i - 1)
                if i >= 2:
                    last_norm(i - 2)
            residual(GROUPS - 1)
            last_norm(GROUPS - 2)
            last_norm(GROUPS - 1)

        @block.gpsimd
        def _(pool):
            link = Chain(pool, pool_step)
            link(nc.gpsimd.memset(xf[:, 0:2 * (CONV - 1)], 0.0))
            for b in range(B):
                link(nc.gpsimd.tensor_copy(x_hi[:, b, 0:CONV - 1], xf[:, 0:CONV - 1]))
                link(nc.gpsimd.tensor_copy(x_lo[:, b, 0:CONV - 1], xf[:, 0:CONV - 1]))
            nc.gpsimd.memset(vpad[:, :, 0:FIRL - 1], 0.0).then_inc(padded, 1)

            link(nc.gpsimd.memset(state[:, 0], 0.0))
            start_inverse(nc.gpsimd, link, 0)
            for g in range(2):
                pool.wait_ge(beta_ready, g + 1)
                times_beta(nc.gpsimd, pool, g)
                triangles_times_beta(nc.gpsimd, pool, g)
            pool.wait_ge(rest_in, 16 * 7)
            nc.gpsimd.tensor_scalar(wo1[:], wo1[:], rmsw[:, 0:1], None, ALU.mult).then_inc(wo_scaled, 1)
            for t in range(FIR_PE):
                last = nc.gpsimd.tensor_scalar(fir_diag[:, t, :], ident[:], fir_l[:, t:t + 1], None, ALU.mult)
            last.then_inc(diag_ready, 1)
            invert(nc.gpsimd, pool, link, 0)
            for b in range(B):
                pool.wait_ge(silu_done, 6 * b + 6)
                for t in range(FIRS):
                    pool.wait_ge(ss_psum, 2 * GROUPS)
                    src = vpad[:, b, FIRL - FIRS + t:FIRL - FIRS + t + S]
                    tap = fir_s[:, t:t + 1].broadcast_to([P, S])
                    if t == 0:
                        link(nc.gpsimd.tensor_tensor(short[:, b], src, tap, ALU.mult))
                        continue
                    link(nc.gpsimd.tensor_tensor(tapped, src, tap, ALU.mult))
                    ins = nc.gpsimd.tensor_tensor(short[:, b], short[:, b], tapped, ALU.add)
                    if t < FIRS - 1:
                        link(ins)
                    else:
                        ins.then_inc(short_done, 1)
                        pool.wait_ge(short_done, b + 1)
            pool.wait_ge(signs_in, 16 * 6)
            nc.gpsimd.tensor_scalar(s_out[:, 0:1], s_in[:, 0:1], 4.0, None, ALU.mult)
            nc.gpsimd.tensor_scalar(s_out[:, 1:2], s_in[:, 1:2], 2.0, None, ALU.mult)
            pool.wait_ge(mix_done, 1)
            for g in FINAL:
                last = nc.gpsimd.tensor_tensor(vtok[:, 4 * g:4 * g + 4, :].rearrange("p n (h e) -> p n h e", h=4),
                                               vtok[:, 4 * g:4 * g + 4, :].rearrange("p n (h e) -> p n h e", h=4),
                                               per_head(mixw[:, 4 * g:4 * g + 4, 0:12:3]), ALU.mult)
            link(last)
            for i, g in enumerate(FINAL):
                v4 = vtok[:, 4 * g:4 * g + 4, :].rearrange("p n d -> p (n d)")
                pool.wait_ge(local_used, 2 * i + 1)
                link(nc.gpsimd.tensor_tensor(v4, v4, tapped[:, 0:GT], ALU.add))
                pool.wait_ge(local_used, 2 * i + 2)
                nc.gpsimd.tensor_tensor(v4, v4, tapped[:, GT:2 * GT], ALU.add).then_inc(local_ready, 1)

            def rstd(i):
                g = FINAL[i]
                pool.wait_ge(stats_ready, i + 1)
                link(nc.gpsimd.tensor_scalar(rs3[:, g, :], mv3[:, g, :, 1], LN_EPS, None, ALU.add))
                nc.gpsimd.tensor_tensor(rs3[:, g, :], rs3[:, g, :], neg_half[:, 0:4], ALU.pow).then_inc(rstd_ready, 1)

            for i in range(GROUPS):
                rstd(i)

        @block.scalar
        def _(act):
            nc.scalar.activation(temp[:], temp[:], ACT.Exp, scale=-1.0).then_inc(temp_exp, 1)
            act.wait_ge(padded, 1)

            def load_x(g):
                act.wait_ge(xT_psum, g + 1)
                if g >= 1:
                    act.wait_ge(gates_psum, g)
                nc.scalar.copy(xf[:], ps[:, 0, :]).then_inc(xf_ready, 1)
                cols = slice(CONV - 1 + GT * (g % 2), CONV - 1 + GT * (g % 2) + GT)
                nc.scalar.copy(x_hi[:, g // 2, cols], ps[:, 0, :]).then_inc(xhi_ready, 1)

            def norms(g, i):
                act.wait_ge(ss_psum, 2 * g + i + 1)
                if g >= 1:
                    act.wait_ge(normed, 2 * g - 1 + i)
                nc.scalar.activation(rn[:, i, :], ps[:, (3, 2)[i], :], ACT.Ln, bias=eps_l2[:, 0:1]).then_inc(ln_done, 1)
                act.wait_ge(ln_done, 2 * g + i + 1)
                nc.scalar.activation(rn[:, i, :], rn[:, i, :], ACT.Exp, scale=-0.5).then_inc(rn_ready, 1)

            def vtok_copy(g):
                act.wait_ge(vtok_psum, g + 1)
                nc.scalar.copy(vtok[:, 4 * g:4 * g + 4, :].rearrange("p n d -> p (n d)"), ps[:, 0, :]).then_inc(vtok_ready, 1)

            def ktok_copy(g):
                act.wait_ge(ktok_psum, g + 1)
                nc.scalar.copy(ka[:, 4 * g:4 * g + 4, :, 0, :], heads(ps[:, 0, :])).then_inc(ktok_ready, 1)

            load_x(0)
            for g in range(GROUPS):
                for i in range(3):
                    act.wait_ge(conv_psum, 3 * g + i + 1)
                    dst = (rows(ks, g), rows(qs, g), v_rows(g))[i]
                    nc.scalar.activation(dst, ps[:, (1, 2, 1)[i], :], ACT.Silu).then_inc(silu_done, 1)
                    if i == 0 and g + 1 < GROUPS:
                        load_x(g + 1)
                    if i == 1 and g >= 1:
                        vtok_copy(g - 1)
                if g >= 1:
                    ktok_copy(g - 1)
                act.wait_ge(gates_biased, g + 1)
                nc.scalar.preload_act_table_set("natural_log_exp_and_others")
                nc.scalar.activation(gates[:, 4 * g:4 * g + 4, :], gates[:, 4 * g:4 * g + 4, :], ACT.Exp, scale=-1.0)
                nc.scalar.activation(mixw[:, 4 * g:4 * g + 4, :], mixw[:, 4 * g:4 * g + 4, :], ACT.Exp).then_inc(gates_exp, 1)
                norms(g, 0)
                norms(g, 1)
            vtok_copy(GROUPS - 1)
            ktok_copy(GROUPS - 1)
            for g in range(GROUPS):
                act.wait_ge(fir_psum, g + 1)
                nc.scalar.copy(long_[:, g // 2, GT * (g % 2):GT * (g % 2) + GT], ps[:, g, :]).then_inc(fir_begun, 1)
            for b in range(B):
                act.wait_ge(uw_psum, b + 1)
                for k in range(4):
                    last = nc.scalar.copy(inv_flat[:, b].rearrange("p i e -> p (i e)")[:, 512 * k:512 * k + 512], ps[:, 4 + k, :])
                last.then_inc(uw_ready, 1)
                act.wait_ge(b_psum, b + 1)
                for c in range(4):
                    last = nc.scalar.copy(bc[:, b, c].rearrange("p n e -> p (n e)"), ps[:, 4 + c, 0:256])
                last.then_inc(b_ready, 1)
            for j in range(32):
                act.wait_ge(state_psum, j + 1)
                nc.scalar.copy(state[:, j + 1], ps[:, j % 2, 0:B * C].rearrange("p (b e) -> p b e", b=B)).then_inc(state_ready, 1)

            def squares(i):
                act.wait_ge(blended, i + 1)
                if i >= 2:
                    act.wait_ge(oss_ready, i - 1)
                nc.scalar.activation(osq[:, i % 2, :], blend[:, FINAL[i], :], ACT.Square).then_inc(osq_ready, 1)

            def norms_of_o(i):
                g = FINAL[i]
                act.wait_ge(oss_ready, i + 1)
                nc.scalar.activation(ors[:, g, :], oss[:, g, :], ACT.Ln, scale=1.0 / C, bias=eps_rms[:, 0:1]).then_inc(ln_done, 1)
                act.wait_ge(ln_done, 2 * GROUPS + i + 1)
                nc.scalar.activation(ors[:, g, :], ors[:, g, :], ACT.Exp, scale=-0.5).then_inc(ors_ready, 1)

            squares(0)
            squares(1)
            norms_of_o(0)
            for i in range(GROUPS):
                if i + 1 < GROUPS:
                    norms_of_o(i + 1)
                act.wait_ge(oT_psum, i + 1)
                if i >= 2:
                    act.wait_ge(y_psum, i - 1)
                nc.scalar.copy(oT[:, i % 2, :], ps[:, 2 + i % 2, :]).then_inc(oT_ready, 1)
                if i + 2 < GROUPS:
                    squares(i + 2)

        @block.tensor
        def _(pe):
            def transposes(g):
                if g >= 3:
                    pe.wait_ge(ktok_ready, g - 2)
                for n in range(4):
                    last = nc.tensor.transpose(ps[:, 0, P * n:P * n + P], X[:, 4 * g + n, :], ident[:])
                last.then_inc(xT_psum, 1)

            def conv(g, i):
                if i == 0 and g >= 1:
                    pe.wait_ge(silu_done, 3 * g)
                if i == 1 and g >= 1:
                    pe.wait_ge(ln_done, 2 * g)
                if i == 2:
                    pe.wait_ge(silu_done, 3 * g + 1)
                bank = ps[:, (1, 2, 1)[i], :]
                for t in range(CONV):
                    cols = slice(GT * (g % 2) + t, GT * (g % 2) + t + GT)
                    xh, xl = x_hi[:, g // 2, cols], x_lo[:, g // 2, cols]
                    nc.tensor.matmul(bank, wc_lo[:, i, t, :], xh, start=(t == 0), stop=False)
                    nc.tensor.matmul(bank, wc_hi[:, i, t, :], xl, start=False, stop=False)
                    last = nc.tensor.matmul(bank, wc_hi[:, i, t, :], xh, start=False, stop=(t == CONV - 1))
                last.then_inc(conv_psum, 1)

            def gate_products(g):
                pe.wait_ge(xf_ready, g + 1)
                if g >= 1:
                    pe.wait_ge(ln_done, 2 * g - 1)
                for n in range(4):
                    last = nc.tensor.matmul(ps[:, 3, 20 * n:20 * n + 20], xf[:, P * n:P * n + P], wgates[:], start=True, stop=True)
                last.then_inc(gates_psum, 1)

            def sums(g, i):
                pe.wait_ge(sq_ready, 2 * g + i + 1)
                if i == 0:
                    pe.wait_ge(gates_biased, g + 1)
                else:
                    pe.wait_ge(silu_done, 3 * g + 2)
                nc.tensor.matmul(ps[:, (3, 2)[i], :], head_ones[:], sq[:, i, :], start=True, stop=True).then_inc(ss_psum, 1)

            def v_to_tokens(g):
                pe.wait_ge(silu_done, 3 * g + 3)
                for loaded in (xf_ready, xhi_ready, xlo_ready):
                    pe.wait_ge(loaded, min(g + 3, GROUPS))
                if g == GROUPS - 1:
                    pe.wait_ge(ktok_ready, g)
                for n in range(4):
                    t = 4 * g + n
                    off = FIRL - 1 + P * (t % 8)
                    last = nc.tensor.transpose(ps[:, 0, P * n:P * n + P], vpad[:, t // 8, off:off + P], ident[:])
                last.then_inc(vtok_psum, 1)

            def k_to_tokens(g):
                pe.wait_ge(normed, 2 * g + 1)
                pe.wait_ge(vtok_ready, g + 1)
                for n in range(4):
                    t = 4 * g + n
                    last = nc.tensor.transpose(ps[:, 0, P * n:P * n + P], ks[:, P * t:P * t + P], ident[:])
                last.then_inc(ktok_psum, 1)

            def chunk(n, c):
                t0 = P * n + C * c
                return slice(t0, t0 + C)

            def triangles(g):
                pe.wait_ge(normed, 2 * g + 2)
                if g >= 1:
                    pe.wait_ge(tri_masked, g)
                    pe.wait_ge(att_ready, g)
                for other, col in ((ks, 0), (qs, 128)):
                    for n in range(4):
                        for i in range(16):
                                h, c = i % 4, (i + i // 4) % 4
                                f = slice(32 * h, 32 * h + 32)
                                o = col + 32 * n
                                last = nc.tensor.matmul(ps[32 * c:32 * c + 32, 4 + h, o:o + 32], ks[f, chunk(4 * g + n, c)],
                                                        other[f, chunk(4 * g + n, c)], start=True, stop=True)
                last.then_inc(tri_psum, 1)

            transposes(0)
            pe.wait_ge(padded, 1)
            for g in range(GROUPS):
                pe.wait_ge(xhi_ready, g + 1)
                pe.wait_ge(xlo_ready, g + 1)
                conv(g, 0)
                gate_products(g)
                if g + 1 < GROUPS:
                    transposes(g + 1)
                conv(g, 1)
                if g >= 1:
                    v_to_tokens(g - 1)
                sums(g, 0)
                if g >= 1:
                    triangles(g - 1)
                conv(g, 2)
                if g >= 1:
                    k_to_tokens(g - 1)
                sums(g, 1)
            v_to_tokens(GROUPS - 1)
            triangles(GROUPS - 1)
            k_to_tokens(GROUPS - 1)
            pe.wait_ge(diag_ready, 1)
            pe.wait_ge(ktok_ready, GROUPS)
            pe.wait_ge(ln_done, 2 * GROUPS)
            for g in range(GROUPS):
                off = GT * (g % 2)
                for t in range(FIR_PE):
                    last = nc.tensor.matmul(ps[:, g, :], fir_diag[:, t, :], vpad[:, g // 2, off + t:off + t + GT], start=(t == 0), stop=(t == FIR_PE - 1))
                last.then_inc(fir_psum, 1)

            def per_chunk(cols, lhs, rhs, place):
                for n in range(8):
                    for i in range(16):
                            c, h = i % 4, (i + i // 4) % 4
                            r = slice(32 * c, 32 * c + 32)
                            bank, o = place(n, c)
                            last = nc.tensor.matmul(ps[32 * h:32 * h + 32, bank, o:o + cols], lhs(r, n, h), rhs(r, n, h), start=True, stop=True)
                return last

            pe.wait_ge(att_ready, GROUPS)
            pe.wait_ge(ktok_ready, GROUPS)
            pe.wait_ge(ln_done, 2 * GROUPS)
            for b in range(B):
                pe.wait_ge(inv_in[b], 16)
                pe.wait_ge(vb_ready, 2 * (b + 1))
                pe.wait_ge(kb_ready, 2 * (b + 1))
                if b:
                    pe.wait_ge(b_ready, b)
                for n in range(8):
                    for h in range(4):
                        for c in range(4):
                            r = slice(32 * c, 32 * c + 32)
                            last = nc.tensor.matmul(ps[r, 4 + n // 2, (4 * (n % 2) + h) * 64:(4 * (n % 2) + h) * 64 + 64],
                                                    tT[r, b, 8 * h + n, :], vk[r, 8 * b + n, h].rearrange("p a e -> p (a e)"),
                                                    start=True, stop=True)
                last.then_inc(uw_psum, 1)
                pe.wait_ge(uw_ready, b + 1)
                if b == 0:
                    pe.wait_ge(fir_begun, GROUPS)
                else:
                    pe.wait_ge(g_ready, b)
                    pe.wait_ge(m_ready, b)
                per_chunk(64, lambda r, n, h: uw(b, r, n, h)[:, 32:64], lambda r, n, h: ka[r, 8 * b + n, h].rearrange("p a e -> p (a e)"),
                          lambda n, c: (c, 64 * n)).then_inc(mg_psum, 1)
                per_chunk(32, lambda r, n, h: ka[r, 8 * b + n, h, 0, :], lambda r, n, h: uw(b, r, n, h)[:, 0:32],
                          lambda n, c: (4 + c, 32 * n)).then_inc(b_psum, 1)
            pe.wait_ge(b_ready, B)

            def o_region(b, n, c, h):
                t = 8 * b + n
                return ps[32 * c:32 * c + 32, 4 + h, C * t:C * t + C]

            for b in range(B):
                for n in range(8):
                    for h in range(4):
                        for c in range(4):
                            r = slice(32 * c, 32 * c + 32)
                            last = nc.tensor.matmul(o_region(b, n, c, h), ka[r, 8 * b + n, h, 1, :], uw(b, r, n, h)[:, 0:32],
                                                    start=(b == 0 and n == 0), stop=False, skip_group_check=True)
            last.then_inc(o_begun, 1)
            pe.wait_ge(o_begun, 1)

            def outputs(n, i):
                for b in range(B):
                    for h in range(4):
                        f, c = slice(32 * h, 32 * h + 32), (h + i) % 4
                        last = nc.tensor.matmul(o_region(b, n, c, h), gT[f, chunk(8 * b + n, c)], state[f, 4 * n + c, b, :], start=False,
                                                stop=True, skip_group_check=True)
                return last

            def input_term(j):
                nc.tensor.matmul(ps[:, j % 2, 0:B * C].rearrange("p (b e) -> p b e", b=B), ident[:], bc[:, :, j % 4, j // 4, :], start=True, stop=False,
                                 skip_group_check=True)

            def filters_to_tokens(k):
                i, g = k % 2, FINAL[k // 2]
                b = g // 2
                pe.wait_ge((short_done, long_done)[i], b + 1)
                if k >= 2:
                    pe.wait_ge(local_used, k - 1)
                for n in range(4):
                    off = GT * (g % 2) + P * n
                    last = nc.tensor.transpose(ps[:, 2 + i, P * n:P * n + P], (short, long_)[i][:, b, off:off + P], ident[:])
                last.then_inc(local_psum, 1)

            pe.wait_ge(m_ready, B)
            pe.wait_ge(g_ready, B)
            input_term(0)
            for j in range(32):
                n, c = j // 4, j % 4
                if j >= 1:
                    pe.wait_ge(state_ready, j)
                for b in range(B):
                    for h in range(4):
                        f = slice(32 * h, 32 * h + 32)
                        last = nc.tensor.matmul(ps[f, j % 2, C * b:C * b + C], mt[f, b, c, n, :], state[f, j, b, :], start=False, stop=True,
                                                skip_group_check=True)
                last.then_inc(state_psum, 1)
                if n >= 1:
                    outputs(n - 1, c)
                if j + 1 < 32:
                    input_term(j + 1)
                if j >= 24:
                    filters_to_tokens(j - 24)

            for i in range(4):
                last = outputs(7, i)
            last.then_inc(o_psum, 1)

            pe.wait_ge(wo_scaled, 1)
            pe.wait_ge(local_used, 8)

            def project(i):
                g = FINAL[i]
                pe.wait_ge(oT_ready, i + 1)
                if i >= 2:
                    pe.wait_ge(stats_ready, i - 1)
                else:
                    pe.wait_ge(state_ready, 31 + i)
                for n in range(4):
                    last = nc.tensor.matmul(ps[:, i % 2, P * n:P * n + P], oT[:, i % 2, P * n:P * n + P], wo1[:], start=True, stop=True)
                last.then_inc(y_psum, 1)

            for i in range(GROUPS):
                g = FINAL[i]
                pe.wait_ge(o_scaled, i + 1)
                if i >= 2:
                    pe.wait_ge(oT_ready, i - 1)
                for n in range(4):
                    last = nc.tensor.transpose(ps[:, 2 + i % 2, P * n:P * n + P], blend[:, g, P * n:P * n + P], ident[:])
                last.then_inc(oT_psum, 1)
                if i >= 1:
                    project(i - 1)
            project(GROUPS - 1)
    sub.close()
    sub = ExitStack()

    def sb5(name, shape, dt=F32):
        return sub.enter_context(nc.sbuf_tensor(name, shape, dt))

    sw1, sw2 = sb5("sw1", [P, FB, FH], F32R), sb5("sw2", [P, FB, D], F32R)
    xt_hi, xt_lo = sb5("xt_hi5", [P, GT], F32R), sb5("xt_lo5", [P, GT], F32R)
    hf = sb5("hf5", [P, FB, GT])
    y_feat = sb5("y_feat5", [P, GT])
    h_hi, h_lo = sb5("h_hi5", [P, 2, FB, GT], F32R), sb5("h_lo5", [P, 2, FB, GT], F32R)
    mv4, st64, rs4 = sb5("mv4", [P, GROUPS, 4, 2]), sb5("st64", [P, GROUPS, 4, 6]), sb5("rs4", [P, GROUPS, 4])

    with nc.Block() as block:
        signs_ready = sem("signs_ready")
        xT_psum, xT_hi, xT_lo = sem("x3T_psum"), sem("x3T_hi"), sem("x3T_lo")
        hid_psum, relu_done = [sem(f"hid5_psum{i}") for i in range(2)], sem("relu_done")
        hi_ready, lo_ready = sem("h5_hi_ready"), sem("h5_lo_ready")
        y_psum, y_scaled, yT_psum, y_added = sem("y5_psum"), sem("y5_scaled"), sem("y5T_psum"), sem("y5_added")
        stats_ready, rstd_ready, out_ready, stored = sem("ln4_stats"), sem("ln4_rstd"), sem("out_ready"), sem("stored")
        dve_step, pool_step = sem("dve_step5"), sem("pool_step5")

        @block.sync
        def _(sp):
            out_tiles = out_dram.rearrange("(n p) d -> p n d", p=P)
            for g in range(GROUPS):
                sp.wait_ge(out_ready, g + 1)
                sp.dma_start(out_tiles[:, 4 * g:4 * g + 4, :], X[:, 4 * g:4 * g + 4, :]).then_inc(stored, 16)
            sp.wait_ge(stored, 16 * GROUPS)

        @block.scalar
        def _(act):
            def transposed(g):
                act.wait_ge(xT_psum, g + 1)
                nc.scalar.copy(xt_hi[:], ps[:, 1, :]).then_inc(xT_hi, 1)

            def relus(g, layer):
                for o in range(FB):
                    act.wait_ge(hid_psum[layer], 4 * g + o + 1)
                    i = 8 * g + 4 * layer + o
                    if i >= FB:
                        act.wait_ge(lo_ready, i - FB + 1)
                    nc.scalar.activation(hf[:, o, :], ps[:, 4 * layer + o, :], ACT.Relu, scale=s_out[:, layer:layer + 1]).then_inc(relu_done, 1)

            transposed(0)
            relus(0, 0)
            for g in range(GROUPS):
                if g + 1 < GROUPS:
                    transposed(g + 1)
                relus(g, 1)
                if g + 1 < GROUPS:
                    relus(g + 1, 0)
                act.wait_ge(y_psum, g + 1)
                if g >= 1:
                    act.wait_ge(yT_psum, g)
                nc.scalar.activation(y_feat[:], ps[:, 7, :], ACT.Copy, scale=s_in[:, 2:3]).then_inc(y_scaled, 1)

        @block.gpsimd
        def _(pool):
            link = Chain(pool, pool_step)

            def rstd(g):
                pool.wait_ge(stats_ready, g + 1)
                link(nc.gpsimd.tensor_scalar(rs4[:, g, :], mv4[:, g, :, 1], LN_EPS, None, ALU.add))
                nc.gpsimd.tensor_tensor(rs4[:, g, :], rs4[:, g, :], neg_half[:, 0:4], ALU.pow).then_inc(rstd_ready, 1)

            nc.gpsimd.tensor_scalar(sw1[:], k1[:], 2.0, -1.0, ALU.mult, ALU.add).then_inc(signs_ready, 1)
            nc.gpsimd.tensor_scalar(sw2[:], k2[:], 2.0, -1.0, ALU.mult, ALU.add).then_inc(signs_ready, 1)
            for g in range(GROUPS):
                for layer in range(2):
                    for o in range(FB):
                        pool.wait_ge(hi_ready, 8 * g + 4 * layer + o + 1)
                        nc.gpsimd.tensor_tensor(h_lo[:, layer, o, :], hf[:, o, :], h_hi[:, layer, o, :].bitcast(F32), ALU.subtract).then_inc(lo_ready, 1)
                    if layer == 0 and g >= 1:
                        rstd(g - 1)
            rstd(GROUPS - 1)

        @block.vector
        def _(dve):
            link = Chain(dve, dve_step)

            def transposed(g):
                dve.wait_ge(xT_hi, g + 1)
                nc.vector.tensor_tensor(xt_lo[:], ps[:, 1, :], xt_hi[:].bitcast(F32), ALU.subtract).then_inc(xT_lo, 1)

            def normalise(g):
                dve.wait_ge(rstd_ready, g + 1)
                for n in range(4):
                    tile = X[:, 4 * g + n, :]
                    last = nc.vector.tensor_scalar(tile, tile, mv4[:, g, n, 0:1], rs4[:, g, n:n + 1], ALU.subtract, ALU.mult)
                last.then_inc(out_ready, 1)

            def his(g, layer):
                for o in range(FB):
                    i = 8 * g + 4 * layer + o
                    dve.wait_ge(relu_done, i + 1)
                    if g >= 1 and layer == 1:
                        dve.wait_ge(y_psum, g)
                    nc.vector.tensor_copy(h_hi[:, layer, o, :], hf[:, o, :]).then_inc(hi_ready, 1)

            transposed(0)
            his(0, 0)
            for g in range(GROUPS):
                if g + 1 < GROUPS:
                    transposed(g + 1)
                if g >= 1:
                    normalise(g - 1)
                his(g, 1)
                if g + 1 < GROUPS:
                    his(g + 1, 0)
                dve.wait_ge(yT_psum, g + 1)
                x4 = X[:, 4 * g:4 * g + 4, :].rearrange("p n d -> p (n d)")
                nc.vector.tensor_tensor(x4, x4, ps[:, 6, :], ALU.add).then_inc(y_added, 1)
                dve.wait_ge(y_added, g + 1)
                for n in range(4):
                    last = nc.vector.bn_stats(st64[:, g, n, :], X[:, 4 * g + n, :])
                link(last)
                for n in range(4):
                    last = nc.vector.bn_aggr(mv4[:, g, n, :], st64[:, g, n, :])
                last.then_inc(stats_ready, 1)
            normalise(GROUPS - 1)

        @block.tensor
        def _(pe):
            def transposes(g):
                if g >= 1:
                    pe.wait_ge(relu_done, 8 * g - 6)
                for n in range(4):
                    last = nc.tensor.transpose(ps[:, 1, P * n:P * n + P], X[:, 4 * g + n, :], ident[:])
                last.then_inc(xT_psum, 1)

            def first(g):
                pe.wait_ge(xT_hi, g + 1)
                pe.wait_ge(xT_lo, g + 1)
                for o in range(FB):
                    if g >= 1:
                        pe.wait_ge(relu_done, 8 * g - 8 + o + 1)
                    w = sw0[:, P * o:P * o + P]
                    nc.tensor.matmul(ps[:, o, :], w, xt_lo[:], start=True, stop=False)
                    nc.tensor.matmul(ps[:, o, :], w, xt_hi[:], start=False, stop=True).then_inc(hid_psum[0], 1)

            transposes(0)
            first(0)
            pe.wait_ge(signs_ready, 1)
            for g in range(GROUPS):
                for k in range(FB):
                    pe.wait_ge(lo_ready, 8 * g + k + 1)
                    for o in range(FB):
                        if k == 0 and g >= 1:
                            pe.wait_ge(relu_done, 8 * g - 4 + o + 1)
                            if o >= 2:
                                pe.wait_ge(y_added, g)
                        w = sw1[:, k, P * o:P * o + P]
                        nc.tensor.matmul(ps[:, 4 + o, :], w, h_lo[:, 0, k, :], start=(k == 0), stop=False)
                        last = nc.tensor.matmul(ps[:, 4 + o, :], w, h_hi[:, 0, k, :], start=False, stop=(k == FB - 1))
                        if k == FB - 1:
                            last.then_inc(hid_psum[1], 1)
                    if k == 0 and g + 1 < GROUPS:
                        transposes(g + 1)
                if g + 1 < GROUPS:
                    first(g + 1)
                pe.wait_ge(signs_ready, 2)
                pe.wait_ge(relu_done, 8 * g + 8)
                for k in range(FB):
                    pe.wait_ge(lo_ready, 8 * g + 4 + k + 1)
                    nc.tensor.matmul(ps[:, 7, :], sw2[:, k, :], h_lo[:, 1, k, :], start=(k == 0), stop=False)
                    last = nc.tensor.matmul(ps[:, 7, :], sw2[:, k, :], h_hi[:, 1, k, :], start=False, stop=(k == FB - 1))
                last.then_inc(y_psum, 1)
                pe.wait_ge(y_scaled, g + 1)
                for n in range(4):
                    last = nc.tensor.transpose(ps[:, 6, P * n:P * n + P], y_feat[:, P * n:P * n + P], ident[:])
                last.then_inc(yT_psum, 1)
    sub.close()


def kernel(**inputs):
    import numpy as _np
    import concourse.bacc as _bacc
    from concourse import mybir as _mybir
    from concourse.bass_utils import run_bass_kernel_spmd as _run

    arrays = {}
    for name, a in inputs.items():
        a = _np.asarray(a)
        if name in ("L0_attn_x",):
            a = a.reshape(-1, a.shape[-1])
        elif name.startswith("L0_ffn") and name.endswith("_w"):
            a = a.T
        elif name.startswith("L0_ffn") and name.endswith("_s") and a.size > 128:
            a = a.reshape(-1, 128).T
        elif a.ndim == 0:
            a = a.reshape(1)
        arrays[name] = _np.ascontiguousarray(a)
    nc = _bacc.Bacc("TRN2", target_bir_lowering=False, num_devices=1)
    dr = {n: nc.dram_tensor(n, a.shape, _mybir.dt.from_np(a.dtype), kind="ExternalInput").ap() for n, a in arrays.items()}
    out = nc.dram_tensor("out", (B * S, D), _mybir.dt.float32, kind="ExternalOutput").ap()
    build(nc, dr, out)
    r = _run(nc, [arrays], core_ids=[0])
    return r.results[0]["out"].reshape(B, S, D)
```
